# Optimizing a Trainium2 kernel written in Bass

```python
import numpy as np
import jax
import jax.numpy as jnp

def _softmax(x, axis=-1):
    return jax.nn.softmax(x, axis=axis)

def _gelu(x):
    return jax.nn.gelu(x, approximate=True)

def _silu(x):
    return jax.nn.silu(x)

def _sigmoid(x):
    return jax.nn.sigmoid(x)

def _layernorm(x, axis=-1, eps=1e-05):
    m = jnp.mean(x, axis=axis, keepdims=True)
    v = jnp.var(x, axis=axis, keepdims=True)
    return (x - m) / jnp.sqrt(v + eps)

def _scatter_add(tgt, idx, src, axis=0):
    return tgt.at[idx].add(src)

def _segment_sum(src, seg, n):
    return jax.ops.segment_sum(src, seg, n)
kernel_name = 'mk_macaron_d2_jaxref_r8_14e3b7'

def setup_inputs(seed: int=0):
    np.random.seed(seed)
    _w = jnp.asarray

    def _L0_attn_setup():
        import jax, jax.numpy as jnp
        import numpy as np
        N_HEADS = 16
        BUCKETS = 32
        MAX_REL = 64
        ATT_SPAN = BUCKETS
        LN_EPS = 1e-07

        def make_log_bucket_position(relative_pos, bucket_size, max_position):
            sign = jnp.sign(relative_pos)
            mid = bucket_size // 2
            abs_pos = jnp.where((relative_pos < mid) & (relative_pos > -mid), mid - 1, jnp.abs(relative_pos))
            log_pos = jnp.ceil(jnp.log(abs_pos / mid) / jnp.log((max_position - 1) / mid) * (mid - 1)) + mid
            bucket_pos = jnp.where(abs_pos <= mid, abs_pos, log_pos * sign)
            return bucket_pos.astype(jnp.int32)

        def build_relative_position(q_size, k_size, bucket_size, max_position):
            rel = jnp.arange(q_size)[:, None] - jnp.arange(k_size)[None, :]
            rel = make_log_bucket_position(rel, bucket_size, max_position)
            return rel.astype(jnp.int32)
        key = jax.random.key(seed)
        ks = jax.random.split(key, 16)
        B, S, H = (4, 128, 128)
        std = 0.02
        inp = {'hidden_states': jax.random.normal(ks[0], (B, S, H), jnp.float32), 'attention_mask': jnp.ones((B, S), jnp.float32), 'rel_embeddings': jax.random.normal(ks[1], (2 * ATT_SPAN, H), jnp.float32) * std, 'Wq': jax.random.normal(ks[2], (H, H), jnp.float32) * std, 'bq': jnp.zeros((H,), jnp.float32), 'Wk': jax.random.normal(ks[3], (H, H), jnp.float32) * std, 'bk': jnp.zeros((H,), jnp.float32), 'Wv': jax.random.normal(ks[4], (H, H), jnp.float32) * std, 'bv': jnp.zeros((H,), jnp.float32), 'Wo': jax.random.normal(ks[5], (H, H), jnp.float32) * std, 'bo': jnp.zeros((H,), jnp.float32), 'ln_scale': jnp.ones((H,), jnp.float32), 'ln_bias': jnp.zeros((H,), jnp.float32)}
        return inp
    _L0_attn_in = _L0_attn_setup()

    def _L0_ffn_setup():
        import jax, jax.numpy as jnp
        import numpy as np
        B, S, D = (4, 256, 128)
        E, F = (8, 512)
        key = jax.random.key(seed)
        ks = jax.random.split(key, 5)
        x = jax.random.normal(ks[0], (B, S, D), dtype=jnp.float32)
        switch_w = jax.random.normal(ks[1], (D, E), dtype=jnp.float32) * D ** (-0.5)
        switch_b = jnp.zeros((E,), dtype=jnp.float32)
        w1 = jax.random.normal(ks[2], (E, D, F), dtype=jnp.float32) * D ** (-0.5)
        b1 = jnp.zeros((E, F), dtype=jnp.float32)
        w2 = jax.random.normal(ks[3], (E, F, D), dtype=jnp.float32) * F ** (-0.5)
        b2 = jnp.zeros((E, D), dtype=jnp.float32)
        return {'x': x, 'switch_w': switch_w, 'switch_b': switch_b, 'w1': w1, 'b1': b1, 'w2': w2, 'b2': b2}
    _L0_ffn_in = _L0_ffn_setup()

    def _L1_attn_setup():
        import jax, jax.numpy as jnp
        import numpy as np
        B, T, C = (8, 256, 128)

        def _rotate(z, cos_a, sin_a):
            b, t, c = z.shape
            z = z.reshape(b, t, c // 2, 2)
            z0, z1 = (z[..., 0], z[..., 1])
            r0 = cos_a * z0 + sin_a * z1
            r1 = -sin_a * z0 + cos_a * z1
            return jnp.stack([r0, r1], axis=-1).reshape(b, t, c)
        key = jax.random.key(seed)
        ks = jax.random.split(key, 9)
        s = 1.0 / np.sqrt(C)
        return {'x': jax.random.normal(ks[0], (B, T, C), dtype=jnp.float32), 'Wk': jax.random.uniform(ks[1], (C, C), jnp.float32, -s, s), 'bk': jax.random.uniform(ks[2], (C,), jnp.float32, -s, s), 'Wq': jax.random.uniform(ks[3], (C, C), jnp.float32, -s, s), 'bq': jax.random.uniform(ks[4], (C,), jnp.float32, -s, s), 'Wv': jax.random.uniform(ks[5], (C, C), jnp.float32, -s, s), 'bv': jax.random.uniform(ks[6], (C,), jnp.float32, -s, s), 'Wp': jax.random.uniform(ks[7], (C, C), jnp.float32, -s, s), 'bp': jax.random.uniform(ks[8], (C,), jnp.float32, -s, s)}
    _L1_attn_in = _L1_attn_setup()

    def _L1_ffn_setup():
        import jax, jax.numpy as jnp
        import numpy as np
        D_MODEL = 128
        NUM_TILES = 64
        TPC = 8
        NUM_CLUSTERS = NUM_TILES // TPC
        GRID = 16
        COMP_H = 32
        NUM_KNOTS = 8
        EPS_LN = 1e-05

        def _calibrate(scores, knots, temperature):
            K = knots.shape[0]
            normalized = jax.nn.sigmoid(scores / (temperature[0] + 1e-06))
            idx_float = normalized * (K - 1)
            idx_low = jnp.clip(idx_float.astype(jnp.int32), 0, K - 2)
            idx_high = idx_low + 1
            t = idx_float - idx_low.astype(scores.dtype)
            val_low = knots[idx_low]
            val_high = knots[idx_high]
            return val_low + t * (val_high - val_low)

        def _forward(x, signatures_raw, knot_values, temperature, compress_w1, compress_b1, compress_w2, compress_b2, spline_w1, spline_b1, spline_w2, spline_b2, directions, norm_gamma, norm_beta, output_scale):
            B, T, D = x.shape
            xf = x.reshape(-1, D)
            q = jnp.where(signatures_raw > 0.3, 1.0, jnp.where(signatures_raw < -0.3, -1.0, 0.0)).astype(signatures_raw.dtype)
            sigs = signatures_raw + jax.lax.stop_gradient(q - signatures_raw)
            cluster_sigs = jnp.sign(sigs.reshape(NUM_CLUSTERS, TPC, D).mean(axis=1))
            cluster_scores = xf @ cluster_sigs.T
            cluster_gates = _calibrate(cluster_scores, knot_values, temperature)
            cluster_idx = jnp.argmax(cluster_gates, axis=-1)
            tile_scores = xf @ sigs.T
            tile_gates = _calibrate(tile_scores, knot_values, temperature)
            gates_by_cluster = tile_gates.reshape(-1, NUM_CLUSTERS, TPC)
            sel_gates = jnp.take_along_axis(gates_by_cluster, cluster_idx[:, None, None], axis=1)[:, 0, :]
            local_idx = jnp.argmax(sel_gates, axis=-1)
            tile_idx = cluster_idx * TPC + local_idx
            h = jax.nn.gelu(xf @ compress_w1 + compress_b1, approximate=False)
            comp = jnp.tanh(h @ compress_w2 + compress_b2)
            w1 = spline_w1[tile_idx]
            b1 = spline_b1[tile_idx]
            hh = jax.nn.relu(jnp.einsum('ni,nig->ng', comp, w1) + b1)
            w2 = spline_w2[tile_idx]
            b2 = spline_b2[tile_idx]
            mag = jnp.einsum('ng,ngo->no', hh, w2) + b2
            ffn_out = mag * directions[tile_idx] * output_scale[0]
            y = xf + ffn_out
            mu = y.mean(axis=-1, keepdims=True)
            var = ((y - mu) ** 2).mean(axis=-1, keepdims=True)
            y = (y - mu) / jnp.sqrt(var + EPS_LN) * norm_gamma + norm_beta
            return y.reshape(B, T, D)
        key = jax.random.key(seed)
        ks = jax.random.split(key, 12)
        B, T = (4, 512)
        x = jax.random.normal(ks[0], (B, T, D_MODEL), dtype=jnp.float32)
        signatures_raw = jax.random.normal(ks[1], (NUM_TILES, D_MODEL), dtype=jnp.float32) * 0.5
        knot_values = jax.nn.sigmoid(jnp.linspace(-3.0, 3.0, NUM_KNOTS).astype(jnp.float32))
        temperature = jnp.ones((1,), dtype=jnp.float32)
        compress_w1 = jax.random.normal(ks[2], (D_MODEL, COMP_H), dtype=jnp.float32) * (1.0 / np.sqrt(D_MODEL))
        compress_b1 = jnp.zeros((COMP_H,), dtype=jnp.float32)
        compress_w2 = jax.random.normal(ks[3], (COMP_H, 2), dtype=jnp.float32) * (1.0 / np.sqrt(COMP_H))
        compress_b2 = jnp.zeros((2,), dtype=jnp.float32)
        spline_w1 = jax.random.normal(ks[4], (NUM_TILES, 2, GRID), dtype=jnp.float32) * (1.0 / np.sqrt(2.0))
        spline_b1 = jnp.zeros((NUM_TILES, GRID), dtype=jnp.float32)
        spline_w2 = jax.random.normal(ks[5], (NUM_TILES, GRID, 1), dtype=jnp.float32) * (1.0 / np.sqrt(GRID))
        spline_b2 = jnp.zeros((NUM_TILES, 1), dtype=jnp.float32)
        directions = jax.random.normal(ks[6], (NUM_TILES, D_MODEL), dtype=jnp.float32) * 0.02
        norm_gamma = jnp.ones((D_MODEL,), dtype=jnp.float32)
        norm_beta = jnp.zeros((D_MODEL,), dtype=jnp.float32)
        output_scale = jnp.ones((1,), dtype=jnp.float32) * 0.1
        return dict(x=x, signatures_raw=signatures_raw, knot_values=knot_values, temperature=temperature, compress_w1=compress_w1, compress_b1=compress_b1, compress_w2=compress_w2, compress_b2=compress_b2, spline_w1=spline_w1, spline_b1=spline_b1, spline_w2=spline_w2, spline_b2=spline_b2, directions=directions, norm_gamma=norm_gamma, norm_beta=norm_beta, output_scale=output_scale)
    _L1_ffn_in = _L1_ffn_setup()
    _d = {'L0_attn_hidden_states': _L0_attn_in['hidden_states'], 'L0_attn_attention_mask': _L0_attn_in['attention_mask'], 'L0_attn_rel_embeddings': _L0_attn_in['rel_embeddings'], 'L0_attn_Wq': _L0_attn_in['Wq'], 'L0_attn_bq': _L0_attn_in['bq'], 'L0_attn_Wk': _L0_attn_in['Wk'], 'L0_attn_bk': _L0_attn_in['bk'], 'L0_attn_Wv': _L0_attn_in['Wv'], 'L0_attn_bv': _L0_attn_in['bv'], 'L0_attn_Wo': _L0_attn_in['Wo'], 'L0_attn_bo': _L0_attn_in['bo'], 'L0_attn_ln_scale': _L0_attn_in['ln_scale'], 'L0_attn_ln_bias': _L0_attn_in['ln_bias'], 'L0_ffn_switch_w': _L0_ffn_in['switch_w'], 'L0_ffn_switch_b': _L0_ffn_in['switch_b'], 'L0_ffn_w1': _L0_ffn_in['w1'], 'L0_ffn_b1': _L0_ffn_in['b1'], 'L0_ffn_w2': _L0_ffn_in['w2'], 'L0_ffn_b2': _L0_ffn_in['b2'], 'L1_attn_Wk': _L1_attn_in['Wk'], 'L1_attn_bk': _L1_attn_in['bk'], 'L1_attn_Wq': _L1_attn_in['Wq'], 'L1_attn_bq': _L1_attn_in['bq'], 'L1_attn_Wv': _L1_attn_in['Wv'], 'L1_attn_bv': _L1_attn_in['bv'], 'L1_attn_Wp': _L1_attn_in['Wp'], 'L1_attn_bp': _L1_attn_in['bp'], 'L1_ffn_signatures_raw': _L1_ffn_in['signatures_raw'], 'L1_ffn_knot_values': _L1_ffn_in['knot_values'], 'L1_ffn_temperature': _L1_ffn_in['temperature'], 'L1_ffn_compress_w1': _L1_ffn_in['compress_w1'], 'L1_ffn_compress_b1': _L1_ffn_in['compress_b1'], 'L1_ffn_compress_w2': _L1_ffn_in['compress_w2'], 'L1_ffn_compress_b2': _L1_ffn_in['compress_b2'], 'L1_ffn_spline_w1': _L1_ffn_in['spline_w1'], 'L1_ffn_spline_b1': _L1_ffn_in['spline_b1'], 'L1_ffn_spline_w2': _L1_ffn_in['spline_w2'], 'L1_ffn_spline_b2': _L1_ffn_in['spline_b2'], 'L1_ffn_directions': _L1_ffn_in['directions'], 'L1_ffn_norm_gamma': _L1_ffn_in['norm_gamma'], 'L1_ffn_norm_beta': _L1_ffn_in['norm_beta'], 'L1_ffn_output_scale': _L1_ffn_in['output_scale']}
    _x0 = _d['L0_attn_hidden_states']
    _d['L0_attn_hidden_states'] = jax.random.normal(jax.random.fold_in(jax.random.key(seed), 1), (4, 512, 128), dtype=_x0.dtype)
    del _x0
    return _d

def reference(L0_attn_hidden_states, L0_attn_attention_mask, L0_attn_rel_embeddings, L0_attn_Wq, L0_attn_bq, L0_attn_Wk, L0_attn_bk, L0_attn_Wv, L0_attn_bv, L0_attn_Wo, L0_attn_bo, L0_attn_ln_scale, L0_attn_ln_bias, L0_ffn_switch_w, L0_ffn_switch_b, L0_ffn_w1, L0_ffn_b1, L0_ffn_w2, L0_ffn_b2, L1_attn_Wk, L1_attn_bk, L1_attn_Wq, L1_attn_bq, L1_attn_Wv, L1_attn_bv, L1_attn_Wp, L1_attn_bp, L1_ffn_signatures_raw, L1_ffn_knot_values, L1_ffn_temperature, L1_ffn_compress_w1, L1_ffn_compress_b1, L1_ffn_compress_w2, L1_ffn_compress_b2, L1_ffn_spline_w1, L1_ffn_spline_b1, L1_ffn_spline_w2, L1_ffn_spline_b2, L1_ffn_directions, L1_ffn_norm_gamma, L1_ffn_norm_beta, L1_ffn_output_scale):

    def _L0_attn_ref(hidden_states, attention_mask, rel_embeddings, Wq, bq, Wk, bk, Wv, bv, Wo, bo, ln_scale, ln_bias):
        import jax, jax.numpy as jnp
        import numpy as np
        N_HEADS = 16
        BUCKETS = 32
        MAX_REL = 64
        ATT_SPAN = BUCKETS
        LN_EPS = 1e-07

        def make_log_bucket_position(relative_pos, bucket_size, max_position):
            sign = jnp.sign(relative_pos)
            mid = bucket_size // 2
            abs_pos = jnp.where((relative_pos < mid) & (relative_pos > -mid), mid - 1, jnp.abs(relative_pos))
            log_pos = jnp.ceil(jnp.log(abs_pos / mid) / jnp.log((max_position - 1) / mid) * (mid - 1)) + mid
            bucket_pos = jnp.where(abs_pos <= mid, abs_pos, log_pos * sign)
            return bucket_pos.astype(jnp.int32)

        def build_relative_position(q_size, k_size, bucket_size, max_position):
            rel = jnp.arange(q_size)[:, None] - jnp.arange(k_size)[None, :]
            rel = make_log_bucket_position(rel, bucket_size, max_position)
            return rel.astype(jnp.int32)
        B, S, H = hidden_states.shape
        nH = N_HEADS
        d = H // nH

        def split_heads(x):
            return jnp.transpose(x.reshape(B, S, nH, d), (0, 2, 1, 3))
        q = split_heads(hidden_states @ Wq + bq)
        k = split_heads(hidden_states @ Wk + bk)
        v = split_heads(hidden_states @ Wv + bv)
        scale_factor = 3
        scale = jnp.sqrt(jnp.asarray(d * scale_factor, hidden_states.dtype))
        scores = jnp.einsum('bhqd,bhkd->bhqk', q, k) / scale
        rel = build_relative_position(S, S, BUCKETS, MAX_REL)
        pos_k = (rel_embeddings @ Wk + bk).reshape(2 * ATT_SPAN, nH, d)
        pos_k = jnp.transpose(pos_k, (1, 0, 2))
        c2p_att = jnp.einsum('bhqd,hpd->bhqp', q, pos_k)
        c2p_pos = jnp.clip(rel + ATT_SPAN, 0, 2 * ATT_SPAN - 1)
        c2p = jnp.take_along_axis(c2p_att, jnp.broadcast_to(c2p_pos[None, None], (B, nH, S, S)), axis=-1)
        p2c_pos = jnp.clip(-rel + ATT_SPAN, 0, 2 * ATT_SPAN - 1)
        p2c_att = jnp.einsum('bhkd,hpd->bhkp', k, pos_k)
        p2c = jnp.take_along_axis(p2c_att, jnp.broadcast_to(p2c_pos[None, None], (B, nH, S, S)), axis=-1)
        p2c = jnp.swapaxes(p2c, -1, -2)
        scores = scores + (c2p + p2c) / scale
        probs = jax.nn.softmax(scores, axis=-1)
        ctx = jnp.einsum('bhqk,bhkd->bhqd', probs, v)
        ctx = jnp.transpose(ctx, (0, 2, 1, 3)).reshape(B, S, H)
        out = ctx @ Wo + bo + hidden_states
        mu = jnp.mean(out, axis=-1, keepdims=True)
        var = jnp.mean(jnp.square(out - mu), axis=-1, keepdims=True)
        out = (out - mu) * jax.lax.rsqrt(var + LN_EPS) * ln_scale + ln_bias
        return out

    def _L0_ffn_ref(x, switch_w, switch_b, w1, b1, w2, b2):
        import jax, jax.numpy as jnp
        import numpy as np
        B, S, D = (4, 256, 128)
        E, F = (8, 512)
        b, s, d = x.shape
        t = x.reshape(-1, d)
        logits = t @ switch_w + switch_b
        route_prob = jax.nn.softmax(logits, axis=-1)
        route_prob_max = jnp.max(route_prob, axis=-1)
        routes = jnp.argmax(route_prob, axis=-1)
        out = jnp.zeros_like(t)
        n_experts = w1.shape[0]
        for e in range(n_experts):
            h = jax.nn.gelu(t @ w1[e] + b1[e])
            y = h @ w2[e] + b2[e]
            mask = (routes == e)[:, None]
            out = jnp.where(mask, y, out)
        out = out * route_prob_max[:, None]
        return out.reshape(b, s, d)

    def _L1_attn_ref(x, Wk, bk, Wq, bq, Wv, bv, Wp, bp):
        import jax, jax.numpy as jnp
        import numpy as np
        B, T, C = (8, 256, 128)

        def _rotate(z, cos_a, sin_a):
            b, t, c = z.shape
            z = z.reshape(b, t, c // 2, 2)
            z0, z1 = (z[..., 0], z[..., 1])
            r0 = cos_a * z0 + sin_a * z1
            r1 = -sin_a * z0 + cos_a * z1
            return jnp.stack([r0, r1], axis=-1).reshape(b, t, c)
        b, t, c = x.shape
        half = c // 2
        k = x @ Wk + bk
        q = x @ Wq + bq
        v = x @ Wv + bv
        angle = jnp.outer(jnp.arange(t, dtype=jnp.float32), jnp.arange(half, dtype=jnp.float32))[::-1]
        cos_a = jnp.cos(angle)
        sin_a = jnp.sin(angle)
        k = _rotate(k, cos_a, sin_a)
        q = _rotate(q, cos_a, sin_a)
        wei = jnp.einsum('bic,bjc->bij', k, q) * c ** (-0.5)
        mask = jnp.tril(jnp.ones((t, t), dtype=bool))
        wei = jnp.where(mask, wei, -jnp.inf)
        wei = jax.nn.softplus(wei)
        out = wei @ v
        out = out @ Wp + bp
        return out

    def _L1_ffn_ref(x, signatures_raw, knot_values, temperature, compress_w1, compress_b1, compress_w2, compress_b2, spline_w1, spline_b1, spline_w2, spline_b2, directions, norm_gamma, norm_beta, output_scale):
        import jax, jax.numpy as jnp
        import numpy as np
        D_MODEL = 128
        NUM_TILES = 64
        TPC = 8
        NUM_CLUSTERS = NUM_TILES // TPC
        GRID = 16
        COMP_H = 32
        NUM_KNOTS = 8
        EPS_LN = 1e-05

        def _calibrate(scores, knots, temperature):
            K = knots.shape[0]
            normalized = jax.nn.sigmoid(scores / (temperature[0] + 1e-06))
            idx_float = normalized * (K - 1)
            idx_low = jnp.clip(idx_float.astype(jnp.int32), 0, K - 2)
            idx_high = idx_low + 1
            t = idx_float - idx_low.astype(scores.dtype)
            val_low = knots[idx_low]
            val_high = knots[idx_high]
            return val_low + t * (val_high - val_low)

        def _forward(x, signatures_raw, knot_values, temperature, compress_w1, compress_b1, compress_w2, compress_b2, spline_w1, spline_b1, spline_w2, spline_b2, directions, norm_gamma, norm_beta, output_scale):
            B, T, D = x.shape
            xf = x.reshape(-1, D)
            q = jnp.where(signatures_raw > 0.3, 1.0, jnp.where(signatures_raw < -0.3, -1.0, 0.0)).astype(signatures_raw.dtype)
            sigs = signatures_raw + jax.lax.stop_gradient(q - signatures_raw)
            cluster_sigs = jnp.sign(sigs.reshape(NUM_CLUSTERS, TPC, D).mean(axis=1))
            cluster_scores = xf @ cluster_sigs.T
            cluster_gates = _calibrate(cluster_scores, knot_values, temperature)
            cluster_idx = jnp.argmax(cluster_gates, axis=-1)
            tile_scores = xf @ sigs.T
            tile_gates = _calibrate(tile_scores, knot_values, temperature)
            gates_by_cluster = tile_gates.reshape(-1, NUM_CLUSTERS, TPC)
            sel_gates = jnp.take_along_axis(gates_by_cluster, cluster_idx[:, None, None], axis=1)[:, 0, :]
            local_idx = jnp.argmax(sel_gates, axis=-1)
            tile_idx = cluster_idx * TPC + local_idx
            h = jax.nn.gelu(xf @ compress_w1 + compress_b1, approximate=False)
            comp = jnp.tanh(h @ compress_w2 + compress_b2)
            w1 = spline_w1[tile_idx]
            b1 = spline_b1[tile_idx]
            hh = jax.nn.relu(jnp.einsum('ni,nig->ng', comp, w1) + b1)
            w2 = spline_w2[tile_idx]
            b2 = spline_b2[tile_idx]
            mag = jnp.einsum('ng,ngo->no', hh, w2) + b2
            ffn_out = mag * directions[tile_idx] * output_scale[0]
            y = xf + ffn_out
            mu = y.mean(axis=-1, keepdims=True)
            var = ((y - mu) ** 2).mean(axis=-1, keepdims=True)
            y = (y - mu) / jnp.sqrt(var + EPS_LN) * norm_gamma + norm_beta
            return y.reshape(B, T, D)
        return _forward(x, signatures_raw, knot_values, temperature, compress_w1, compress_b1, compress_w2, compress_b2, spline_w1, spline_b1, spline_w2, spline_b2, directions, norm_gamma, norm_beta, output_scale)
    x = L0_attn_hidden_states
    x = x + 0.5 * _L0_ffn_ref(_layernorm(x, axis=-1), L0_ffn_switch_w, L0_ffn_switch_b, L0_ffn_w1, L0_ffn_b1, L0_ffn_w2, L0_ffn_b2)
    x = x + _L0_attn_ref(_layernorm(x, axis=-1), L0_attn_attention_mask, L0_attn_rel_embeddings, L0_attn_Wq, L0_attn_bq, L0_attn_Wk, L0_attn_bk, L0_attn_Wv, L0_attn_bv, L0_attn_Wo, L0_attn_bo, L0_attn_ln_scale, L0_attn_ln_bias)
    x = x + 0.5 * _L0_ffn_ref(_layernorm(x, axis=-1), L0_ffn_switch_w, L0_ffn_switch_b, L0_ffn_w1, L0_ffn_b1, L0_ffn_w2, L0_ffn_b2)
    x = x + 0.5 * _L1_ffn_ref(_layernorm(x, axis=-1), L1_ffn_signatures_raw, L1_ffn_knot_values, L1_ffn_temperature, L1_ffn_compress_w1, L1_ffn_compress_b1, L1_ffn_compress_w2, L1_ffn_compress_b2, L1_ffn_spline_w1, L1_ffn_spline_b1, L1_ffn_spline_w2, L1_ffn_spline_b2, L1_ffn_directions, L1_ffn_norm_gamma, L1_ffn_norm_beta, L1_ffn_output_scale)
    x = x + _L1_attn_ref(_layernorm(x, axis=-1), L1_attn_Wk, L1_attn_bk, L1_attn_Wq, L1_attn_bq, L1_attn_Wv, L1_attn_bv, L1_attn_Wp, L1_attn_bp)
    x = x + 0.5 * _L1_ffn_ref(_layernorm(x, axis=-1), L1_ffn_signatures_raw, L1_ffn_knot_values, L1_ffn_temperature, L1_ffn_compress_w1, L1_ffn_compress_b1, L1_ffn_compress_w2, L1_ffn_compress_b2, L1_ffn_spline_w1, L1_ffn_spline_b1, L1_ffn_spline_w2, L1_ffn_spline_b2, L1_ffn_directions, L1_ffn_norm_gamma, L1_ffn_norm_beta, L1_ffn_output_scale)
    return x

_drawn_inputs = setup_inputs


def setup_inputs(seed=0):
    import zlib

    import numpy as np

    out = dict(_drawn_inputs(seed))
    spreads = {'L0_attn_bq': (0.0, 0.8),
     'L0_attn_bk': (0.0, 0.8),
     'L0_attn_bv': (0.0, 0.1),
     'L0_attn_bo': (0.0, 0.1),
     'L0_attn_ln_scale': (1.0, 0.2),
     'L0_attn_ln_bias': (0.0, 0.1),
     'L0_ffn_switch_b': (0.0, 0.1),
     'L0_ffn_b1': (0.0, 0.1),
     'L0_ffn_b2': (0.0, 0.1),
     'L1_ffn_compress_b1': (0.0, 2.0),
     'L1_ffn_compress_b2': (0.0, 2.0),
     'L1_ffn_spline_b1': (0.0, 2.0),
     'L1_ffn_spline_b2': (0.0, 2.0),
     'L1_ffn_norm_gamma': (1.0, 0.2),
     'L1_ffn_norm_beta': (0.0, 0.1)}
    factors = {'L0_attn_rel_embeddings': 8.0,
     'L0_attn_Wq': 8.0,
     'L0_attn_Wk': 8.0,
     'L0_attn_Wv': 6.493,
     'L1_attn_bk': 6.539,
     'L1_attn_bq': 6.493,
     'L1_attn_bp': 8.0,
     'L1_ffn_signatures_raw': 8.0,
     'L1_ffn_knot_values': 8.0,
     'L1_ffn_compress_w1': 8.0,
     'L1_ffn_compress_w2': 8.0,
     'L1_ffn_spline_w1': 8.0,
     'L1_ffn_spline_w2': 8.0,
     'L1_ffn_directions': 8.0}
    for name, (base, spread) in spreads.items():
        noise = np.random.default_rng([zlib.crc32(name.encode()), seed]).standard_normal(out[name].shape)
        drawn = base * np.exp(spread * noise) if base else spread * noise
        out[name] = jnp.asarray(drawn.astype(out[name].dtype))
    for name, factor in factors.items():
        out[name] = (out[name] * factor).astype(out[name].dtype)
    return out
```

```python
from contextlib import ExitStack

import numpy as np

import concourse.bass as bass
from concourse import mybir

F32 = mybir.dt.float32
BF16 = mybir.dt.bfloat16
I32 = mybir.dt.int32
ALU = mybir.AluOpType
ACT = mybir.ActivationFunctionType
AX = mybir.AxisListType

P = 128
B, S, D = 4, 512, 128
TILES = B * S // P
EXPERTS, FF = 8, 512
FC = FF // P
UNROLL = 4
SLOTS = -(-(TILES + EXPERTS - 1) // UNROLL) * UNROLL
ROUNDS = SLOTS // UNROLL
ROUND_ORDER = [("turn", 0), ("turn", 1), ("up", 0), ("turn", 2), ("up", 1), ("turn_h", 0), ("turn", 3), ("up", 2),
               ("down", 0), ("turn_h", 1), ("up", 3), ("down", 1), ("turn_h", 2), ("down", 2), ("turn_h", 3),
               ("down", 3)]

SIGS, CLUSTERS = 64, 8
PER = SIGS // CLUSTERS
KNOTS, GRID, COMP = 8, 16, 32
SCORES = CLUSTERS + SIGS
W1_AT, B1_AT, W2_AT, B2_AT, DIR_AT = 0, 2 * GRID, 3 * GRID, 4 * GRID, 4 * GRID + 1
PARAMS = DIR_AT + D
SPLINE_LOADS = 15
CAUSAL_LOADS = 10

HEADS, DH = 16, 8
BUCKETS, MAX_REL = 32, 64
NB = S // 64
WIN = 192
GROUP = 4
GROUPS = HEADS // GROUP
T4 = S // P
QUOTA = S + 2 * 64
ROWS = 12


def bucket(d):
    mid = BUCKETS // 2
    size = mid - 1 if -mid < d < mid else abs(d)
    if size <= mid:
        return size
    f = np.float32
    far = np.ceil(np.log(f(size) / f(mid)) / np.log(f((MAX_REL - 1) / mid)) * f(mid - 1)) + f(mid)
    return int(far) * (1 if d > 0 else -1)


def clipped(v):
    return min(max(v, 0), 2 * BUCKETS - 1)


def bucket_runs():
    pair = {d: (clipped(bucket(d) + BUCKETS), clipped(BUCKETS - bucket(-d))) for d in range(1 - S, S)}
    right = max(d for d in pair if all(pair[k] == pair[1 - S] for k in range(1 - S, d + 1)))
    left = min(d for d in pair if all(pair[k] == pair[S - 1] for k in range(d, S)))
    assert left <= 64 and right >= -64
    runs = []
    for d in range(right + 1, left):
        if runs and runs[-1][2:] == pair[d]:
            runs[-1] = (runs[-1][0], d, *pair[d])
        else:
            runs.append((d, d, *pair[d]))
    return runs, left, right, pair[S - 1], pair[1 - S]


RUNS, LEFT, RIGHT, LEFT_ROWS, RIGHT_ROWS = bucket_runs()
USED = sorted({r for run in RUNS for r in run[2:]} | set(LEFT_ROWS) | set(RIGHT_ROWS))
CUT = next(n for n in range(1, len(USED)) if USED[n] != USED[n - 1] + 1)
STRETCHES = [(USED[0], 0, CUT), (USED[CUT], CUT, len(USED) - CUT)]
NP_ = len(USED)
ROW_OF = {p: n for n, p in enumerate(USED)}
PER_CHUNK = P // NP_
CHUNKS = [(h, min(PER_CHUNK, HEADS - h)) for h in range(0, HEADS, PER_CHUNK)]

PREP_LOADS = 10
HUGE = 3.0e38
TURN_LAG, COPY_LAG, WEIGH_AT, HEADS_AT, TURN_AT = 2, 3, 3, 5, 7


def host_tables():
    p = np.arange(P)
    i = np.arange(NB)
    mine = (p % NB)[:, None]
    angle = np.outer(np.arange(S, dtype=np.float32), np.arange(D // 2, dtype=np.float32))[::-1].astype(np.float64)
    return {
        "own_head": (p[:, None] // DH == np.arange(HEADS)).astype(np.float32),
        "far_mask": np.stack([mine < i - 1, mine > i + 1], 1).astype(np.float32),
        "block_hot": (mine == i).astype(np.float32),
        "cos": np.cos(angle).astype(np.float32),
        "sin": np.sin(angle).astype(np.float32),
    }


def attention_dram(nc):
    def dram(n, shape, dt=F32):
        return nc.dram_tensor(n, shape, dt).ap()

    return {
        "q": dram("stacked_q", (B, P, ROWS, S), BF16),
        "k": dram("stacked_k", (B, P, ROWS, S), BF16),
        "tab_q": dram("position_q", (B, HEADS * NP_, S)),
        "tab_k": dram("position_k", (B, HEADS * NP_, QUOTA)),
        "v": dram("values", (B, GROUPS, P, T4 * P)),
        "near": dram("near_terms", (B, P, 64, WIN)),
    }


def clear_semaphores(nc, sems):
    numbers = sorted(s.num for s in sems)
    starts = [n for n in numbers if n - 1 not in numbers]
    ends = [n + 1 for n in numbers if n + 1 not in numbers]
    with nc.Block() as block:

        @block.sync
        def _(sp):
            for first, end in zip(starts, ends):
                sp.sem_clear(range(first, end))


def constants_phase(nc, ctx, x, x_dram, xs_dram):
    def sb(n, shape, dt=F32):
        return ctx.enter_context(nc.sbuf_tensor(f"c_{n}", shape, dt))

    c = {
        "ident": sb("ident", [P, P]),
        "ones": sb("ones", [P, P]),
        "ones_b": sb("ones_b", [P, P], BF16),
        "earlier_b": sb("earlier_b", [P, P], BF16),
        "eps5": sb("eps5", [P, 1]),
        "eps7": sb("eps7", [P, 1]),
        "countdown8": sb("countdown8", [P, EXPERTS]),
        "tile_starts": sb("tile_starts", [P, TILES]),
        "earlier8": sb("earlier8", [P, EXPERTS, EXPERTS]),
        "slot_ids": sb("slot_ids", [P, SLOTS]),
        "segment_ids": sb("segment_ids", [P, KNOTS]),
    }
    x_in = ctx.enter_context(nc.semaphore("x_in"))
    filled = ctx.enter_context(nc.semaphore("filled"))
    zero_ready = ctx.enter_context(nc.semaphore("zero_ready"))
    slots_cleared = ctx.enter_context(nc.semaphore("slots_cleared"))
    shaped = ctx.enter_context(nc.semaphore("shaped"))
    with nc.sbuf_tensor("c_zeros", [P, SLOTS, D], F32) as zeros, nc.Block() as block:

        @block.sync
        def _(sp):
            sp.dma_start(x[:, :, :], x_dram.rearrange("b (t p) d -> p (b t) d", p=P)).then_inc(x_in, 16)
            sp.wait_ge(zero_ready, 1)
            sp.dma_start(xs_dram.rearrange("(s p) d -> p s d", p=P), zeros[:, :, :]).then_inc(slots_cleared, 16)
            sp.wait_ge(x_in, 16)
            sp.wait_ge(slots_cleared, 16)

        @block.vector
        def _(dve):
            dve.memset(zeros[:, :, :], 0.0).then_inc(zero_ready, 1)
            dve.memset(c["ident"][:, :], 1.0).then_inc(filled, 1)
            dve.memset(c["ones"][:, :], 1.0).then_inc(filled, 1)
            dve.memset(c["ones_b"][:, :], 1.0).then_inc(filled, 1)
            dve.memset(c["earlier_b"][:, :], 1.0).then_inc(filled, 1)
            dve.memset(c["earlier8"][:, :, :], 1.0).then_inc(filled, 1)
            dve.memset(c["eps5"][:, :], 1e-5).then_inc(filled, 1)
            dve.memset(c["eps7"][:, :], 1e-7).then_inc(filled, 1)

        @block.gpsimd
        def _(pool):
            pool.iota(c["countdown8"][:, :], [[-1, EXPERTS]], base=EXPERTS, channel_multiplier=0,
                      allow_small_or_imprecise_dtypes=True)
            pool.iota(c["tile_starts"][:, :], [[P, TILES]], base=0, channel_multiplier=0,
                      allow_small_or_imprecise_dtypes=True)
            pool.iota(c["segment_ids"][:, :], [[1, KNOTS]], base=0, channel_multiplier=0,
                      allow_small_or_imprecise_dtypes=True)
            pool.iota(c["slot_ids"][:, :], [[1, SLOTS]], base=0, channel_multiplier=0,
                      allow_small_or_imprecise_dtypes=True).then_inc(shaped, 1)
            pool.wait_ge(filled, 7)
            pool.affine_select(c["ident"][:, :], c["ident"][:, :], compare_op=ALU.is_equal, fill=0.0,
                               base=0, pattern=[[-1, P]], channel_multiplier=1)
            pool.affine_select(c["earlier_b"][:, :], c["earlier_b"][:, :], compare_op=ALU.is_gt, fill=0.0,
                               base=0, pattern=[[1, P]], channel_multiplier=-1)
            pool.affine_select(c["earlier8"][:, :, :], c["earlier8"][:, :, :], compare_op=ALU.is_gt, fill=0.0,
                               base=0, pattern=[[1, EXPERTS], [-1, EXPERTS]], channel_multiplier=0).then_inc(shaped, 1)
            pool.wait_ge(shaped, 2)
    return c


def normalise_tokens(dve, done, x, scratch, eps, std_ready, var_ready):
    stats, mv, rstd, newton = scratch
    for t in range(TILES):
        last = dve.bn_stats(stats[:, t, :], x[:, t, :])
    done(last)
    for t in range(TILES):
        last = dve.bn_aggr(mv[:, t, :], stats[:, t, :])
    last.then_inc(var_ready, 1)
    dve.wait_ge(std_ready, 1)
    done(dve.reciprocal(rstd[:, :], newton[:, 0, :]))
    done(dve.tensor_tensor(newton[:, 1, :], rstd[:, :], rstd[:, :], ALU.mult))
    done(dve.scalar_tensor_tensor(newton[:, 2, :], mv[:, :, 1], eps, newton[:, 1, :], ALU.add, ALU.mult))
    done(dve.tensor_scalar(newton[:, 3, :], newton[:, 2, :], -0.5, 1.5, ALU.mult, ALU.add))
    done(dve.tensor_tensor(newton[:, 4, :], rstd[:, :], newton[:, 3, :], ALU.mult))


def two_back(sems, i, j):
    return sems[(j - 2) % UNROLL], i + (1 if j >= 2 else 0)


def chain_on(engine, sem):
    count = [0]

    def done(instruction):
        count[0] += 1
        instruction.then_inc(sem, 1)
        engine.wait_ge(sem, count[0])

    return done


def ffn_phase(nc, kept, name, x, consts, w, scratch_dram):
    c = consts
    xs_dram, ys_dram = scratch_dram
    with ExitStack() as ctx:
        own_sems = []

        def sb(n, shape, dt=F32):
            return ctx.enter_context(nc.sbuf_tensor(f"{name}_{n}", shape, dt))

        def ps(n, shape, dt=F32):
            return ctx.enter_context(nc.psum_tensor(f"{name}_{n}", shape, dt))

        def sem(n):
            own_sems.append(ctx.enter_context(nc.semaphore(f"{name}_{n}")))
            return own_sems[-1]

        def soft_dma_sem(n):
            return kept.enter_context(nc.semaphore(f"{name}_{n}"))

        w1 = sb("w1", [P, EXPERTS, FF])
        w2 = sb("w2", [P, EXPERTS, FC, D])
        b1 = sb("b1", [1, EXPERTS, FF])
        b2 = sb("b2", [1, EXPERTS, D])
        switch_w = sb("switch_w", [P, EXPERTS])
        switch_b = sb("switch_b", [P, EXPERTS])
        xn = sb("xn", [P, TILES, D])
        xnT = sb("xnT", [P, TILES, P])
        stats = sb("stats", [P, TILES, 6])
        mv = sb("mv", [P, TILES, 2])
        rstd = sb("rstd", [P, TILES])
        newton = sb("newton", [P, 5, TILES])
        logits = sb("logits", [P, TILES, EXPERTS])
        top = sb("top", [P, TILES])
        shifted = sb("shifted", [P, TILES, EXPERTS])
        exps = sb("exps", [P, TILES, EXPERTS])
        total = sb("total", [P, TILES])
        gate = sb("gate", [P, TILES])
        half_gate = sb("half_gate", [P, TILES])
        marks = sb("marks", [P, TILES, EXPERTS])
        first = sb("first", [P, TILES])
        onehot = sb("onehot", [P, TILES, EXPERTS])
        onehot_b = sb("onehot_b", [P, TILES, EXPERTS], BF16)
        over = sb("over", [P, EXPERTS, TILES])
        n_slots = sb("n_slots", [P, EXPERTS])
        before = sb("before", [P, EXPERTS, EXPERTS])
        base = sb("base", [P, EXPERTS])
        ends = sb("ends", [P, EXPERTS])
        place = sb("place", [P, TILES, EXPERTS])
        placed = sb("placed", [P, TILES, EXPERTS])
        pos = sb("pos", [P, TILES])
        pos_i = sb("pos_i", [P, TILES], I32)
        past = sb("past", [P, SLOTS, EXPERTS])
        owner = sb("owner", [P, SLOTS])
        owner_i = sb("owner_i", [P, SLOTS], I32)
        xs = sb("xs", [P, UNROLL, D])
        xsT = sb("xsT", [P, UNROLL, P])
        h = sb("h", [P, 2, FF])
        hT = sb("hT", [P, 2, FC, P])
        ys = sb("ys", [P, UNROLL, D])
        yg = sb("yg", [P, TILES, D])

        psT = ps("psT", [P, 2, 4, P])
        psR = ps("psR", [P, 512])
        psU = ps("psU", [P, 2, FF])
        psH = ps("psH", [P, 2, FC, P])
        psY = ps("psY", [P, 512])
        ps_logits = psR[:, 0:TILES * EXPERTS].rearrange("p (t e) -> p t e", t=TILES)
        ys_banks = [psR[:, 0:P], psY[:, 0:P]]
        ps_rank = psR[:, 256:256 + (TILES + 1) * EXPERTS].rearrange("p (t e) -> p t e", e=EXPERTS)

        weights_in = sem("weights_in")
        chain = sem("chain")
        var_ready, std_ready = sem("var_ready"), sem("std_ready")
        xn_ready, xnT_psum, xnT_ready = sem("xn_ready"), sem("xnT_psum"), sem("xnT_ready")
        logits_ready, shifted_ready, exps_ready = sem("logits_ready"), sem("shifted_ready"), sem("exps_ready")
        onehot_ready, rank_ready = sem("onehot_ready"), sem("rank_ready")
        pos_ready, owner_ready = sem("pos_ready"), sem("owner_ready")
        scattered = soft_dma_sem("scattered")
        def sems(n):
            return [sem(f"{n}{j}") for j in range(UNROLL)]

        xs_in, xsT_psum, xsT_ready, up_ready = sems("xs_in"), sems("xsT_psum"), sems("xsT_ready"), sems("up_ready")
        h_ready, hT_psum, hT_ready = sems("h_ready"), sems("hT_psum"), sems("hT_ready")
        down_ready, ys_ready = sems("down_ready"), sems("ys_ready")
        ys_out = [soft_dma_sem(f"ys_out{j}") for j in range(UNROLL)]
        gathered, x_updated = soft_dma_sem("gathered"), sem("x_updated")

        xs_rows = xs_dram.rearrange("(s p) d -> p s d", p=P)
        ys_rows = ys_dram.rearrange("(s p) d -> p s d", p=P)

        def rounds(engine, body):
            body(0, True)
            with engine.Fori(1, ROUNDS) as i:
                body(i, False)

        with nc.Block() as block:

            @block.sync
            def _(sp):
                sp.dma_start(switch_w[:, :], w["switch_w"]).then_inc(weights_in, 16)
                sp.dma_start(switch_b[:, :], w["switch_b"].unsqueeze(0).partition_broadcast(P)).then_inc(weights_in, 16)
                sp.dma_start(w1[:, :, :], w["w1"].rearrange("e d f -> d e f")).then_inc(weights_in, 16)
                sp.dma_start(w2[:, :, :, :], w["w2"].rearrange("e (k p) d -> p e k d", p=P)).then_inc(weights_in, 16)
                sp.dma_start(b1[:, :, :], w["b1"].unsqueeze(0)).then_inc(weights_in, 16)
                sp.dma_start(b2[:, :, :], w["b2"].unsqueeze(0)).then_inc(weights_in, 16)
                sp.wait_ge(scattered, 16 * TILES)

                def body(i, first):
                    for j in range(UNROLL):
                        if not first:
                            sp.wait_ge(xsT_psum[j], i)
                        sp.dma_start(xs[:, j, :], xs_rows[:, bass.ds(i * UNROLL + j, 1), :].rearrange("p a d -> p (a d)")).then_inc(xs_in[j], 16)

                rounds(sp, body)

            @block.gpsimd
            def _(pool):
                pool.wait_ge(pos_ready, 1)
                for t in range(TILES):
                    pool.indirect_dma_start(
                        xs_dram[:, :], bass.IndirectOffsetOnAxis(ap=pos_i[:, t:t + 1], axis=0),
                        xn[:, t, :], None).then_inc(scattered, 16)
                with pool.Fori(0, ROUNDS) as i:
                    for j in range(UNROLL):
                        pool.wait_ge(ys_ready[j], i + 1)
                        pool.dma_start(ys_rows[:, bass.ds(i * UNROLL + j, 1), :].rearrange("p a d -> p (a d)"), ys[:, j, :]).then_inc(ys_out[j], 16)
                for j in range(UNROLL):
                    pool.wait_ge(ys_out[j], 16 * ROUNDS)
                for t in range(TILES):
                    pool.indirect_dma_start(
                        yg[:, t, :], None, ys_dram[:, :],
                        bass.IndirectOffsetOnAxis(ap=pos_i[:, t:t + 1], axis=0)).then_inc(gathered, 16)

            @block.scalar
            def _(act):
                act.wait_ge(var_ready, 1)
                nc.scalar.activation(newton[:, 0, :], mv[:, :, 1], ACT.Sqrt, bias=c["eps5"][:, 0:1]).then_inc(std_ready, 1)
                for g in range(4):
                    act.wait_ge(xnT_psum, g + 1)
                    nc.scalar.copy(xnT[:, 4 * g:4 * g + 4, :], psT[:, g % 2, :, :]).then_inc(xnT_ready, 1)
                act.wait_ge(shifted_ready, 1)
                nc.scalar.activation(exps[:, :, :], shifted[:, :, :], ACT.Exp).then_inc(exps_ready, 1)

                def body(i, first):
                    for j in range(UNROLL):
                        act.wait_ge(up_ready[j], i + 1)
                        if not (first and j < 2):
                            act.wait_ge(*two_back(hT_psum, i, j))
                        nc.scalar.activation(h[:, j % 2, :], psU[:, j % 2, :], ACT.Gelu_apprx_tanh).then_inc(h_ready[j], 1)

                rounds(act, body)

            @block.vector
            def _(dve):
                done = chain_on(dve, chain)
                done(dve.memset(logits[:, :, :], 0.0))
                normalise_tokens(dve, done, x, (stats, mv, rstd, newton), 1e-5, std_ready, var_ready)
                for t in range(TILES):
                    dve.tensor_scalar(xn[:, t, :], x[:, t, :], mv[:, t, 0:1], newton[:, 4, t:t + 1],
                                      ALU.subtract, ALU.mult).then_inc(xn_ready, 1)
                dve.wait_ge(logits_ready, 1)
                dve.wait_ge(weights_in, 96)
                done(dve.tensor_tensor(logits[:, :, :], ps_logits,
                                       switch_b[:, :].unsqueeze(1).broadcast_to((P, TILES, EXPERTS)), ALU.add))
                done(dve.tensor_reduce(top[:, :], logits[:, :, :], AX.X, ALU.max))
                dve.tensor_tensor(shifted[:, :, :], logits[:, :, :],
                                  top[:, :].unsqueeze(2).broadcast_to((P, TILES, EXPERTS)), ALU.subtract).then_inc(shifted_ready, 1)
                dve.wait_ge(exps_ready, 1)
                done(dve.tensor_reduce(total[:, :], exps[:, :, :], AX.X, ALU.add))
                done(dve.reciprocal(gate[:, :], total[:, :]))
                rev = c["countdown8"][:, :].unsqueeze(1).broadcast_to((P, TILES, EXPERTS))
                done(dve.scalar_tensor_tensor(marks[:, :, :], exps[:, :, :], 1.0, rev, ALU.is_equal, ALU.mult))
                done(dve.tensor_reduce(first[:, :], marks[:, :, :], AX.X, ALU.max))
                firsts = first[:, :].unsqueeze(2).broadcast_to((P, TILES, EXPERTS))
                done(dve.tensor_tensor(onehot[:, :, :], rev, firsts, ALU.is_equal))
                dve.tensor_copy(onehot_b[:, :, :], onehot[:, :, :]).then_inc(onehot_ready, 1)
                dve.wait_ge(rank_ready, 1)
                done(dve.tensor_tensor(over[:, :, :], ps_rank[:, TILES, :].unsqueeze(2).broadcast_to((P, EXPERTS, TILES)),
                                       c["tile_starts"][:, :].unsqueeze(1).broadcast_to((P, EXPERTS, TILES)), ALU.is_gt))
                done(dve.tensor_reduce(n_slots[:, :], over[:, :, :], AX.X, ALU.add))
                done(dve.tensor_tensor(before[:, :, :], n_slots[:, :].unsqueeze(1).broadcast_to((P, EXPERTS, EXPERTS)),
                                       c["earlier8"][:, :, :], ALU.mult))
                done(dve.tensor_reduce(base[:, :], before[:, :, :], AX.X, ALU.add))
                done(dve.tensor_tensor(ends[:, :], base[:, :], n_slots[:, :], ALU.add))
                done(dve.scalar_tensor_tensor(place[:, :, :], base[:, :].unsqueeze(1).broadcast_to((P, TILES, EXPERTS)),
                                              float(P), ps_rank[:, 0:TILES, :], ALU.mult, ALU.add))
                done(dve.tensor_tensor(placed[:, :, :], place[:, :, :], onehot[:, :, :], ALU.mult))
                done(dve.tensor_reduce(pos[:, :], placed[:, :, :], AX.X, ALU.add))
                dve.tensor_copy(pos_i[:, :], pos[:, :]).then_inc(pos_ready, 1)
                done(dve.tensor_tensor(past[:, :, :], ends[:, :].unsqueeze(1).broadcast_to((P, SLOTS, EXPERTS)),
                                       c["slot_ids"][:, :].unsqueeze(2).broadcast_to((P, SLOTS, EXPERTS)), ALU.is_le))
                done(dve.tensor_reduce(owner[:, :], past[:, :, :], AX.X, ALU.add))
                dve.tensor_scalar(owner_i[:, :], owner[:, :], float(EXPERTS - 1), None, ALU.min).then_inc(owner_ready, 1)

                done(dve.tensor_scalar(half_gate[:, :], gate[:, :], 0.5, None, ALU.mult))

                def to_xsT(i, j, first):
                    dve.wait_ge(xsT_psum[j], i + 1)
                    if not first:
                        dve.wait_ge(up_ready[j], i)
                    dve.tensor_copy(xsT[:, j, :], psT[:, j % 2, 0, :]).then_inc(xsT_ready[j], 1)

                def to_hT(i, j, first):
                    dve.wait_ge(hT_psum[j], i + 1)
                    if not (first and j < 2):
                        dve.wait_ge(*two_back(down_ready, i, j))
                    dve.tensor_copy(hT[:, j % 2, :, :], psH[:, j % 2, :, :]).then_inc(hT_ready[j], 1)

                def to_ys(i, j, first):
                    dve.wait_ge(down_ready[j], i + 1)
                    if not first:
                        dve.wait_ge(ys_out[j], i * 16)
                    dve.tensor_copy(ys[:, j, :], ys_banks[j % 2]).then_inc(ys_ready[j], 1)

                def body(i, first):
                    for step, j in ROUND_ORDER:
                        if step == "turn":
                            to_xsT(i, j, first)
                        elif step == "turn_h":
                            to_hT(i, j, first)
                        elif step == "down":
                            to_ys(i, j, first)

                rounds(dve, body)
                dve.wait_ge(gathered, 16 * TILES)
                for t in range(TILES):
                    last = dve.scalar_tensor_tensor(x[:, t, :], yg[:, t, :], half_gate[:, t:t + 1], x[:, t, :],
                                                    ALU.mult, ALU.add)
                last.then_inc(x_updated, 1)

            @block.tensor
            def _(pe):
                for g in range(4):
                    for k in range(4):
                        t = 4 * g + k
                        pe.wait_ge(xn_ready, t + 1)
                        if g >= 2 and k == 0:
                            pe.wait_ge(xnT_ready, g - 1)
                        last = pe.transpose(psT[:, g % 2, k, :], xn[:, t, :], c["ident"][:, :])
                    last.then_inc(xnT_psum, 1)
                pe.wait_ge(weights_in, 96)
                pe.wait_ge(xnT_ready, 4)
                for t in range(TILES):
                    last = pe.matmul(ps_logits[:, t, :], xnT[:, t, :], switch_w[:, :], start=True, stop=True)
                last.then_inc(logits_ready, 1)
                pe.wait_ge(onehot_ready, 1)
                pe.matmul(ps_rank[:, 0:TILES, :], c["earlier_b"][:, :], onehot_b[:, :, :], start=True, stop=False,
                          skip_group_check=True)
                for t in range(TILES):
                    n = TILES - t
                    last = pe.matmul(ps_rank[:, t + 1:TILES + 1, :], c["ones_b"][:, :],
                                     onehot_b[:, t:t + 1, :].broadcast_to((P, n, EXPERTS)),
                                     start=False, stop=(t == TILES - 1), skip_group_check=True)
                last.then_inc(rank_ready, 1)
                pe.wait_ge(owner_ready, 1)

                def turn(i, j, first):
                    pe.wait_ge(xs_in[j], i * 16 + 16)
                    if not (first and j < 2):
                        pe.wait_ge(*two_back(xsT_ready, i, j))
                    pe.transpose(psT[:, j % 2, 0, :], xs[:, j, :], c["ident"][:, :]).then_inc(xsT_psum[j], 1)

                def up(i, j, expert, first):
                    pe.wait_ge(xsT_ready[j], i + 1)
                    if not (first and j < 2):
                        pe.wait_ge(*two_back(h_ready, i, j))
                    pe.matmul(psU[:, j % 2, :], c["ones"][0:1, :],
                              b1[:, bass.ds(expert, 1), :].rearrange("p a f -> p (a f)"), start=True, stop=False)
                    pe.matmul(psU[:, j % 2, :], xsT[:, j, :],
                              w1[:, bass.ds(expert, 1), :].rearrange("p a f -> p (a f)"),
                              start=False, stop=True).then_inc(up_ready[j], 1)

                def turn_h(i, j, first):
                    pe.wait_ge(h_ready[j], i + 1)
                    if not (first and j < 2):
                        pe.wait_ge(*two_back(hT_ready, i, j))
                    for k in range(FC):
                        last = pe.transpose(psH[:, j % 2, k, :], h[:, j % 2, k * P:(k + 1) * P], c["ident"][:, :])
                    last.then_inc(hT_psum[j], 1)

                def down(i, j, expert, first):
                    pe.wait_ge(hT_ready[j], i + 1)
                    if not (first and j < 2):
                        pe.wait_ge(*two_back(ys_ready, i, j))
                    pe.matmul(ys_banks[j % 2], c["ones"][0:1, :],
                              b2[:, bass.ds(expert, 1), :].rearrange("p a d -> p (a d)"), start=True, stop=False)
                    for k in range(FC):
                        last = pe.matmul(ys_banks[j % 2], hT[:, j % 2, k, :],
                                         w2[:, bass.ds(expert, 1), k, :].rearrange("p a d -> p (a d)"),
                                         start=False, stop=(k == FC - 1))
                    last.then_inc(down_ready[j], 1)

                def body(i, first):
                    experts = [pe.value_load(owner_i[0:1, bass.ds(i * UNROLL + j, 1)], min_val=0, max_val=EXPERTS - 1)
                               for j in range(UNROLL)]
                    for step, j in ROUND_ORDER:
                        if step == "turn":
                            turn(i, j, first)
                        elif step == "up":
                            up(i, j, experts[j], first)
                        elif step == "turn_h":
                            turn_h(i, j, first)
                        else:
                            down(i, j, experts[j], first)

                rounds(pe, body)

        clear_semaphores(nc, own_sems)


def relative_prepare(nc, kept, name, x, xn, consts, w, dram):
    c = consts
    inv = 1.0 / float(np.sqrt(np.float32(DH * 3)))
    with ExitStack() as ctx:
        own_sems = []

        def sb(n, shape, dt=F32):
            return ctx.enter_context(nc.sbuf_tensor(f"{name}_{n}", shape, dt))

        def ps(n, shape, dt=F32):
            return ctx.enter_context(nc.psum_tensor(f"{name}_{n}", shape, dt))

        def sem(n):
            own_sems.append(ctx.enter_context(nc.semaphore(f"{name}_{n}")))
            return own_sems[-1]

        def soft_dma_sem(n):
            return kept.enter_context(nc.semaphore(f"{name}_{n}"))

        wq, wk, wv = sb("wq", [P, D]), sb("wk", [P, D]), sb("wv", [P, D])
        bq, bk, bv = sb("bq", [P, 1]), sb("bk", [P, 1]), sb("bv", [P, D])
        rel = sb("rel", [2 * BUCKETS, D])
        relT = sb("relT", [P, 2 * BUCKETS])
        pos, pos_s = sb("pos", [P, 2 * BUCKETS]), sb("pos_s", [P, 2 * BUCKETS])
        own_head = sb("own_head", [P, HEADS])
        far_mask = sb("far_mask", [P, 2, NB])
        block_hot = sb("block_hot", [P, NB])
        hot_rows = sb("hot_rows", [P, S], BF16)
        tab_w = sb("tab_w", [P, 2, HEADS, NP_])
        far_w = sb("far_w", [P, 4, HEADS, NB])
        xnT = sb("xnT", [P, TILES, P])
        stats, mv = sb("stats", [P, TILES, 6]), sb("mv", [P, TILES, 2])
        rstd, newton = sb("rstd", [P, TILES]), sb("newton", [P, 5, TILES])
        whole = sb("whole", [P, 2, 4, S])
        far_l, far_r = sb("far_l", [P, 2, S]), sb("far_r", [P, 2, S])
        rest, rest2 = sb("rest", [P, 4, S]), sb("rest2", [P, 4, S])
        parts = sb("parts", [P, 2, 4, 3, S], BF16)
        rows = sb("rows", [P, 4, S])
        v_pad = sb("v_pad", [P, TILES, HEADS, 32])
        edge = sb("edge", [P, 64])

        psT = ps("psT", [P, 2, 4, P])
        ps_qk = ps("ps_qk", [P, 2, S])
        ps_far = ps("ps_far", [P, 2, S])
        ps_tab = ps("ps_tab", [P, 2, S])

        weights_in, chain = sem("weights_in"), sem("chain")
        rel_ready, relT_psum, relT_ready, pos_psum, shapes_ready = (
            sem("rel_ready"), sem("relT_psum"), sem("relT_ready"), sem("pos_psum"), sem("shapes_ready"))
        var_ready, std_ready = sem("var_ready"), sem("std_ready")
        xn_ready, xT_psum, xT_ready = sem("xn_ready"), sem("xT_psum"), sem("xT_ready")
        qk_psum, qk_ready, far_psum, far_ready = sem("qk_psum"), sem("qk_ready"), sem("far_psum"), sem("far_ready")
        hi_ready, rest_ready, mid_ready, lo_ready = sem("hi_ready"), sem("rest_ready"), sem("mid_ready"), sem("lo_ready")
        tab_psum, rows_ready = sem("tab_psum"), sem("rows_ready")
        rows_out = [soft_dma_sem(f"rows_out{k}") for k in range(4)]
        v_psum, v_ready = sem("v_psum"), sem("v_ready")
        parts_out = [sem(f"parts_out{k}") for k in range(2)]
        v_out, hot_out, edge_out = soft_dma_sem("v_out"), sem("hot_out"), sem("edge_out")

        n_rows = 2 * len(CHUNKS)

        with nc.Block() as block:

            @block.sync
            def _(sp):
                loads = [
                    (wq[:, :], w["Wq"]), (wk[:, :], w["Wk"]), (wv[:, :], w["Wv"]),
                    (bq[:, :], w["bq"].unsqueeze(1)), (bk[:, :], w["bk"].unsqueeze(1)),
                    (bv[:, :], w["bv"].unsqueeze(0).partition_broadcast(P)),
                    (rel[:, :], w["rel_embeddings"]), (own_head[:, :], w["own_head"]),
                    (far_mask[:, :, :], w["far_mask"]), (block_hot[:, :], w["block_hot"]),
                ]
                assert len(loads) == PREP_LOADS
                for dst, src in loads:
                    sp.dma_start(dst, src).then_inc(weights_in, 16)
                sp.wait_ge(shapes_ready, 1)
                for b in range(B):
                    for e in (0, 64 + S):
                        for h0, n in CHUNKS:
                            sp.dma_start(dram["tab_k"][b, h0 * NP_:(h0 + n) * NP_, e:e + 64], edge[0:n * NP_, :])\
                                .then_inc(edge_out, 16)
                    for dst, r in ((dram["k"], 6), (dram["k"], 7), (dram["k"], 8), (dram["q"], 9), (dram["q"], 10), (dram["q"], 11)):
                        sp.dma_start(dst[b, :, r, :], hot_rows[:, :]).then_inc(hot_out, 16)
                sp.wait_ge(edge_out, 16 * 2 * len(CHUNKS) * B)
                sp.wait_ge(hot_out, 16 * 6 * B)
                for b in range(B):
                    u = b % 2
                    sp.wait_ge(hi_ready, 4 * b + 4)
                    sp.wait_ge(mid_ready, 4 * b + 4)
                    sp.wait_ge(lo_ready, 4 * b + 4)
                    for dst, r, n, src in (("q", 0, 0, 0), ("q", 1, 0, 0), ("q", 2, 0, 0), ("q", 3, 0, 1), ("q", 4, 0, 1), ("q", 5, 0, 2),
                                           ("k", 0, 1, 0), ("k", 1, 1, 1), ("k", 2, 1, 2), ("k", 3, 1, 0), ("k", 4, 1, 1), ("k", 5, 1, 0),
                                           ("q", 6, 2, 0), ("q", 7, 2, 1), ("q", 8, 2, 2), ("k", 9, 3, 0), ("k", 10, 3, 1), ("k", 11, 3, 2)):
                        sp.dma_start(dram[dst][b, :, r, :], parts[:, u, n, src, :]).then_inc(parts_out[u], 16)
                for u in range(2):
                    sp.wait_ge(parts_out[u], 16 * 18 * (B // 2))

            @block.gpsimd
            def _(pool):
                for b in range(B):
                    for k in range(n_rows):
                        side, (h0, n) = k // len(CHUNKS), CHUNKS[k % len(CHUNKS)]
                        m = n_rows * b + k
                        pool.wait_ge(rows_ready, m + 1)
                        dst = dram["tab_k"][b, h0 * NP_:(h0 + n) * NP_, 64:64 + S] if side else \
                            dram["tab_q"][b, h0 * NP_:(h0 + n) * NP_, :]
                        pool.dma_start(dst, rows[0:n * NP_, m % 4, :]).then_inc(rows_out[m % 4], 16)
                    pool.wait_ge(v_ready, b + 1)
                    pool.dma_start(dram["v"][b].rearrange("g p (t k) -> p t g k", t=T4),
                                   v_pad[:, T4 * b:T4 * b + T4, :, :].rearrange("p t (g j) k -> p t g (j k)", g=GROUPS)).then_inc(v_out, 16)
                for k in range(4):
                    pool.wait_ge(rows_out[k], 16 * (n_rows * B // 4))
                pool.wait_ge(v_out, 16 * B)

            @block.scalar
            def _(act):
                act.wait_ge(var_ready, 1)
                nc.scalar.activation(newton[:, 0, :], mv[:, :, 1], ACT.Sqrt, bias=c["eps5"][:, 0:1]).then_inc(std_ready, 1)
                for g in range(4):
                    act.wait_ge(xT_psum, g + 1)
                    nc.scalar.copy(xnT[:, 4 * g:4 * g + 4, :], psT[:, g % 2, :, :]).then_inc(xT_ready, 1)
                for b in range(B):
                    u = b % 2
                    for n in range(4):
                        if n < 2:
                            act.wait_ge(qk_ready, 2 * b + n + 1)
                        else:
                            act.wait_ge(far_ready, 2 * b + n - 1)
                        if b >= 2:
                            act.wait_ge(parts_out[u], 16 * 18 * (b // 2))
                        nc.scalar.copy(parts[:, u, n, 0, :], whole[:, u, n, :]).then_inc(hi_ready, 1)
                    for n in range(4):
                        act.wait_ge(rest_ready, 4 * b + n + 1)
                        nc.scalar.copy(parts[:, u, n, 1, :], rest[:, n, :]).then_inc(mid_ready, 1)
                    for k in range(n_rows):
                        m = n_rows * b + k
                        n = CHUNKS[k % len(CHUNKS)][1]
                        act.wait_ge(tab_psum, m + 1)
                        if m >= 4:
                            act.wait_ge(rows_out[m % 4], 16 * (m // 4))
                        nc.scalar.copy(rows[0:n * NP_, m % 4, :], ps_tab[0:n * NP_, m % 2, :]).then_inc(rows_ready, 1)

            @block.vector
            def _(dve):
                done = chain_on(dve, chain)
                dve.memset(edge[:, :], 0.0)
                dve.memset(v_pad[:, :, :, :], 0.0)
                dve.wait_ge(weights_in, 16 * PREP_LOADS)
                done(dve.tensor_copy(hot_rows[:, :].rearrange("p (n k) -> p n k", n=NB),
                                     block_hot[:, :].unsqueeze(2).broadcast_to((P, NB, 64))))
                dve.wait_ge(relT_psum, 1)
                dve.tensor_copy(relT[:, :], psT[:, 0, 0, 0:2 * BUCKETS]).then_inc(relT_ready, 1)
                dve.wait_ge(pos_psum, 1)
                done(dve.tensor_scalar(pos[:, :], psT[:, 1, 0, 0:2 * BUCKETS], bk[:, 0:1], None, ALU.add))
                done(dve.tensor_scalar(pos_s[:, :], pos[:, :], inv, None, ALU.mult))
                for side, src in enumerate((pos, pos_s)):
                    for p0, n0, n in STRETCHES:
                        wide = (P, HEADS, n)
                        dve.tensor_tensor(tab_w[:, side, :, n0:n0 + n], src[:, p0:p0 + n].unsqueeze(1).broadcast_to(wide),
                                          own_head[:, :].unsqueeze(2).broadcast_to(wide), ALU.mult)
                    for far, row in enumerate((LEFT_ROWS[side], RIGHT_ROWS[side])):
                        last = dve.tensor_scalar(far_w[:, 2 * side + far, :, :], own_head[:, :].unsqueeze(2).broadcast_to((P, HEADS, NB)),
                                                 src[:, row:row + 1], None, ALU.mult)
                last.then_inc(shapes_ready, 1)
                normalise_tokens(dve, done, x, (stats, mv, rstd, newton), 1e-5, std_ready, var_ready)
                for t in range(TILES):
                    dve.tensor_scalar(xn[:, t, :], x[:, t, :], mv[:, t, 0:1], newton[:, 4, t:t + 1],
                                      ALU.subtract, ALU.mult).then_inc(xn_ready, 1)
                for b in range(B):
                    u = b % 2
                    dve.wait_ge(qk_psum, b + 1)
                    if b >= 2:
                        dve.wait_ge(hi_ready, 4 * (b - 1))
                        dve.wait_ge(tab_psum, n_rows * (b - 1))
                    dve.tensor_scalar(whole[:, u, 0, :], ps_qk[:, 0, :], bq[:, 0:1], inv, ALU.add, ALU.mult).then_inc(qk_ready, 1)
                    dve.tensor_scalar(whole[:, u, 1, :], ps_qk[:, 1, :], bk[:, 0:1], None, ALU.add).then_inc(qk_ready, 1)
                    for n in range(2):
                        dve.wait_ge(far_psum, 2 * b + n + 1)
                        for far, dst in enumerate((far_l, far_r)):
                            last = dve.tensor_tensor(dst[:, n, :].rearrange("p (i k) -> p i k", i=NB),
                                                     ps_far[:, far, :].rearrange("p (i k) -> p i k", i=NB),
                                                     far_mask[:, far if n == 0 else 1 - far, :].unsqueeze(2).broadcast_to((P, NB, 64)), ALU.mult)
                        done(last)
                        dve.tensor_tensor(whole[:, u, 2 + n, :], far_l[:, n, :], far_r[:, n, :], ALU.add).then_inc(far_ready, 1)
                    dve.wait_ge(v_psum, b + 1)
                    dve.tensor_tensor(v_pad[:, T4 * b:T4 * b + T4, :, 0:DH],
                                      psT[:, 0, :, :].rearrange("p t (h d) -> p t h d", h=HEADS),
                                      bv[:, :].rearrange("p (h d) -> p h d", h=HEADS).unsqueeze(1).broadcast_to((P, T4, HEADS, DH)),
                                      ALU.add).then_inc(v_ready, 1)
                    for n in range(4):
                        dve.wait_ge(hi_ready, 4 * b + n + 1)
                        if b:
                            dve.wait_ge(mid_ready, 4 * (b - 1) + n + 1)
                        dve.tensor_tensor(rest[:, n, :], whole[:, u, n, :], parts[:, u, n, 0, :], ALU.subtract).then_inc(rest_ready, 1)
                    for n in range(4):
                        dve.wait_ge(mid_ready, 4 * b + n + 1)
                        dve.wait_ge(rest_ready, 4 * b + n + 1)
                        dve.tensor_tensor(parts[:, u, n, 2, :], rest[:, n, :], parts[:, u, n, 1, :], ALU.subtract).then_inc(lo_ready, 1)

            @block.tensor
            def _(pe):
                pe.wait_ge(weights_in, 16 * PREP_LOADS)
                pe.transpose(psT[:, 0, 0, 0:2 * BUCKETS], rel[:, :], c["ident"][0:2 * BUCKETS, 0:2 * BUCKETS]).then_inc(relT_psum, 1)
                pe.wait_ge(relT_ready, 1)
                pe.matmul(psT[:, 1, 0, 0:2 * BUCKETS], wk[:, :], relT[:, :], start=True, stop=True).then_inc(pos_psum, 1)
                pe.wait_ge(shapes_ready, 1)
                for g in range(4):
                    for k in range(4):
                        t = 4 * g + k
                        pe.wait_ge(xn_ready, t + 1)
                        if g >= 2 and k == 0:
                            pe.wait_ge(xT_ready, g - 1)
                        last = pe.transpose(psT[:, g % 2, k, :], xn[:, t, :], c["ident"][:, :])
                    last.then_inc(xT_psum, 1)
                pe.wait_ge(xT_ready, 4)
                for b in range(B):
                    u = b % 2
                    tokens = xnT[:, T4 * b:T4 * b + T4, :].rearrange("p t q -> p (t q)")
                    if b:
                        pe.wait_ge(qk_ready, 2 * b)
                    pe.matmul(ps_qk[:, 0, :], wq[:, :], tokens, start=True, stop=True)
                    pe.matmul(ps_qk[:, 1, :], wk[:, :], tokens, start=True, stop=True).then_inc(qk_psum, 1)
                    if b:
                        pe.wait_ge(v_ready, b)
                    for t in range(T4):
                        last = pe.matmul(psT[:, 0, t, :], xnT[:, T4 * b + t, :], wv[:, :], start=True, stop=True)
                    last.then_inc(v_psum, 1)
                    for n in range(2):
                        pe.wait_ge(qk_ready, 2 * b + n + 1)
                        if 2 * b + n:
                            pe.wait_ge(far_ready, 2 * b + n)
                        for far in range(2):
                            last = pe.matmul(ps_far[:, far, :], far_w[:, 2 * n + far, :, :].rearrange("p h j -> p (h j)"),
                                             whole[:, u, n, :], start=True, stop=True)
                        last.then_inc(far_psum, 1)
                    for k in range(n_rows):
                        side, (h0, n) = k // len(CHUNKS), CHUNKS[k % len(CHUNKS)]
                        m = n_rows * b + k
                        if m >= 2:
                            pe.wait_ge(rows_ready, m - 1)
                        pe.matmul(ps_tab[0:n * NP_, m % 2, :], tab_w[:, side, h0:h0 + n, :].rearrange("p h r -> p (h r)"),
                                  whole[:, u, side, :], start=True, stop=True).then_inc(tab_psum, 1)

        clear_semaphores(nc, own_sems)


def relative_attend(nc, kept, name, heads_out, w, dram):
    with ExitStack() as ctx:
        own_sems = []

        def sb(n, shape, dt=F32):
            return ctx.enter_context(nc.sbuf_tensor(f"{name}_{n}", shape, dt))

        def ps(n, shape, dt=F32):
            return ctx.enter_context(nc.psum_tensor(f"{name}_{n}", shape, dt))

        def sem(n):
            own_sems.append(ctx.enter_context(nc.semaphore(f"{name}_{n}")))
            return own_sems[-1]

        def soft_dma_sem(n):
            return kept.enter_context(nc.semaphore(f"{name}_{n}"))

        HALF = 32
        K = 8 * ROWS
        UNITS = GROUP * T4
        DVE_TILES = T4 - 1
        PITCH = 6 * P
        ident = w["ident"]
        rows_q, rows_k = sb("rows_q", [P, NP_ * 64]), sb("rows_k", [P, NP_ * WIN])
        near = sb("near", [P, HALF * WIN])
        qs, ks = sb("qs", [K, GROUP, S], BF16), sb("ks", [K, GROUP, S], BF16)
        bias = sb("bias", [P, 2, T4 * PITCH])
        v = sb("v", [P, T4, GROUP, 32])
        neg = sb("neg", [P, 2, S])
        neg_top, total, rate = sb("neg_top", [P, GROUP, T4]), sb("total", [P, GROUP, T4]), sb("rate", [P, GROUP, T4])
        prob = sb("prob", [P, 4, S])
        probT = sb("probT", [P, GROUP, T4, S])
        headT = sb("headT", [P, S])

        ps_s = ps("ps_s", [P, 4, S])
        ps_t = ps("ps_t", [P, 2, T4, P])
        ps_c = ps("ps_c", [P, S])
        ps_ct = ps("ps_ct", [P, T4, P])

        cleared, units_begun = sem("cleared"), sem("units_begun")
        rows_in, rows_free, near_steps, near_out = sem("rows_in"), sem("rows_free"), sem("near_steps"), soft_dma_sem("near_out")
        qk_in = [sem(f"qk_in{j}") for j in range(GROUP)]
        bias_in = [sem(f"bias_in{j}") for j in range(2)]
        v_in = sem("v_in")
        scores_psum, neg_ready, prob_ready, turned_psum = (
            sem("scores_psum"), sem("neg_ready"), sem("prob_ready"), sem("turned_psum"))
        dve_copied, act_copied = sem("dve_copied"), sem("act_copied")
        rates_ready, heads_psum, headT_ready, heads_turned, heads_ready = (
            sem("rates_ready"), sem("heads_psum"), sem("headT_ready"), sem("heads_turned"), sem("heads_ready"))

        def copied(n, u):
            j, t = u // T4, u % T4
            if t < DVE_TILES:
                return dve_copied, n * (GROUP * DVE_TILES) + (j * DVE_TILES + t + 1)
            return act_copied, n * GROUP + (j + 1)

        def earlier(n, u, back):
            return (n, u - back) if u >= back else (n - 1, u - back + UNITS)

        def groups(engine, body):
            body(0, True)
            with engine.Fori(1, B * GROUPS) as n:
                body(n, False)

        with nc.Block() as block:

            @block.sync
            def _(sp):
                sp.wait_ge(cleared, 1)

                def load_rows(b):
                    for g in range(NB):
                        dst = bass.AP(rows_q[:, :].tensor, g * NP_ * 64, [(NB * NP_ * 64, HEADS), (64, NP_), (1, 64)])
                        src = bass.AP(dram["tab_q"].tensor, b * (HEADS * NP_ * S) + g * 64, [(NP_ * S, HEADS), (S, NP_), (1, 64)])
                        sp.dma_start(dst, src).then_inc(rows_in, 16)
                        dst = bass.AP(rows_k[:, :].tensor, g * NP_ * WIN, [(NB * NP_ * WIN, HEADS), (WIN, NP_), (1, WIN)])
                        src = bass.AP(dram["tab_k"].tensor, b * (HEADS * NP_ * QUOTA) + g * 64,
                                      [(NP_ * QUOTA, HEADS), (QUOTA, NP_), (1, WIN)])
                        sp.dma_start(dst, src).then_inc(rows_in, 16)

                def load_group(b, g, first):
                    n = b * GROUPS + g
                    for j in range(GROUP):
                        head = b * HEADS + (g * GROUP + j)
                        if not first:
                            sp.wait_ge(scores_psum, n * UNITS + (T4 * (j + 1) - UNITS))
                        for side, dst in (("q", qs), ("k", ks)):
                            src = bass.AP(dram[side].tensor, head * (K * S), [(S, K), (1, S)])
                            sp.dma_start(dst[:, j, :], src).then_inc(qk_in[j], 16)
                        if not (first and j < 2):
                            sp.wait_ge(neg_ready, n * UNITS + T4 * (j - 1))
                        for s in range(2):
                            src = bass.AP(dram["near"].tensor, head * (NB * 64 * WIN) + s * (64 * WIN),
                                          [(WIN, 64), (P * WIN, T4), (1, WIN)])
                            dst = bias[64 * s:64 * s + 64, j % 2, :].rearrange("p (t k) -> p t k", k=PITCH)[:, :, 64 * s:64 * s + WIN]
                            sp.dma_start(dst, src).then_inc(bias_in[j % 2], 16)
                    if not first:
                        sp.wait_ge(heads_psum, n)
                    src = bass.AP(dram["v"].tensor, n * (P * T4 * P), [(T4 * P, P), (1, T4 * P)])
                    sp.dma_start(v[:, :, :, :].rearrange("p t j k -> p (t j k)"), src).then_inc(v_in, 16)

                def batch(b, first):
                    sp.wait_ge(near_out, b * 32 + 32)
                    for g in range(GROUPS):
                        load_group(b, g, first and g == 0)

                load_rows(0)
                sp.wait_ge(rows_free, 1)
                load_rows(1)
                batch(0, True)
                with sp.Fori(1, B - 1) as b:
                    sp.wait_ge(rows_free, b + 1)
                    load_rows(b + 1)
                    batch(b, False)
                batch(B - 1, False)

            @block.gpsimd
            def _(pool):
                def view(buffer, offset, *dims):
                    t = buffer[:, :].tensor
                    return bass.AP(t, offset, [(t.shape[1], P), *dims])

                def lay_out(b, first):
                    pool.wait_ge(rows_in, b * (32 * NB) + 32 * NB)
                    for half in range(2):
                        q0 = HALF * half
                        if not (first and half == 0):
                            pool.wait_ge(near_out, b * 32 + 16 * half)

                        def far(rows, c0, c1):
                            rq, rk = (ROW_OF[r] for r in rows)
                            return pool.tensor_tensor(
                                view(near, c0, (WIN, HALF), (1, c1 - c0)), view(rows_q, rq * 64 + q0, (1, HALF), (0, c1 - c0)),
                                view(rows_k, rk * WIN + c0, (0, HALF), (1, c1 - c0)), ALU.add)

                        far(LEFT_ROWS, 0, q0 + HALF + 64 - LEFT)
                        far(RIGHT_ROWS, q0 + 64 - RIGHT, WIN).then_inc(near_steps, 1)
                        pool.wait_ge(near_steps, b * 4 + (2 * half + 1))
                        for d0, d1, pq, pk in RUNS:
                            at, width = q0 + 64 - d1, d1 - d0 + 1
                            last = pool.tensor_tensor(
                                view(near, at, (WIN + 1, HALF), (1, width)), view(rows_q, ROW_OF[pq] * 64 + q0, (1, HALF), (0, width)),
                                view(rows_k, ROW_OF[pk] * WIN + at, (1, HALF), (1, width)), ALU.add)
                        last.then_inc(near_steps, 1)
                        pool.wait_ge(near_steps, b * 4 + (2 * half + 2))
                        dst = bass.AP(dram["near"].tensor, b * (P * 64 * WIN) + q0 * WIN, [(64 * WIN, P), (1, HALF * WIN)])
                        pool.dma_start(dst, near[:, :]).then_inc(near_out, 16)
                    pool.engine_nop().then_inc(rows_free, 1)

                lay_out(0, True)
                with pool.Fori(1, B) as b:
                    lay_out(b, False)
                pool.wait_ge(near_out, 32 * B)

            @block.scalar
            def _(act):
                def exp(n, u, first):
                    j, t = u // T4, u % T4
                    act.wait_ge(neg_ready, n * UNITS + (u + 1))
                    if not (first and u < 4):
                        act.wait_ge(turned_psum, n * UNITS + (u - 3))
                    if u == 0 and not first:
                        act.wait_ge(rates_ready, n)
                    nc.scalar.activation(prob[:, u % 4, :], neg[:, u % 2, :], ACT.Exp, bias=neg_top[:, j, t:t + 1], scale=-1.0,
                                         accum_out=total[:, j, t:t + 1]).then_inc(prob_ready, 1)

                def copy_turned(n, u, first_of_all):
                    j, t = u // T4, u % T4
                    if t < DVE_TILES:
                        return
                    act.wait_ge(turned_psum, n * UNITS + (u + 1))
                    if not first_of_all:
                        act.wait_ge(heads_psum, n)
                    nc.scalar.copy(probT[:, j, :, t * P:(t + 1) * P], ps_t[:, u % 2, :, :]).then_inc(act_copied, 1)

                def copy_heads(n, first_of_all):
                    act.wait_ge(heads_psum, n + 1)
                    if not first_of_all:
                        act.wait_ge(heads_turned, n)
                    nc.scalar.copy(headT[:, :], ps_c[:, :]).then_inc(headT_ready, 1)

                def body(n, first):
                    for u in range(UNITS):
                        exp(n, u, first)
                        if u >= COPY_LAG:
                            copy_turned(n, u - COPY_LAG, first)
                        elif not first:
                            copy_turned(n - 1, u - COPY_LAG + UNITS, False)
                        if u == HEADS_AT and not first:
                            copy_heads(n - 1, False)

                groups(act, body)
                for u in range(UNITS - COPY_LAG, UNITS):
                    copy_turned(B * GROUPS - 1, u, False)
                copy_heads(B * GROUPS - 1, False)

            @block.vector
            def _(dve):
                dve.memset(bias[:, :, :], 0.0).then_inc(cleared, 1)
                dve.wait_ge(cleared, 1)

                def add_terms(n, u, first):
                    j, t = u // T4, u % T4
                    dve.wait_ge(scores_psum, n * UNITS + (u + 1))
                    if t == 0:
                        dve.wait_ge(bias_in[j % 2], n * 64 + 32 * (j // 2 + 1))
                    if not (first and u < 2):
                        dve.wait_ge(prob_ready, n * UNITS + (u - 1))
                    dve.sem_inc(units_begun, 1)
                    at = t * (PITCH - P) + 64
                    dve.tensor_tensor_reduce(out=neg[:, u % 2, :], in0=ps_s[:, u % 4, :], in1=bias[:, j % 2, at:at + S], scale=-1.0,
                                             scalar=HUGE, op0=ALU.add, op1=ALU.min,
                                             accum_out=neg_top[:, j, t:t + 1]).then_inc(neg_ready, 1)

                def copy_turned(n, u, first_of_all):
                    j, t = u // T4, u % T4
                    if t >= DVE_TILES:
                        return
                    dve.wait_ge(turned_psum, n * UNITS + (u + 1))
                    if t == 0 and not first_of_all:
                        dve.wait_ge(heads_psum, n)
                    dve.tensor_copy(probT[:, j, :, t * P:(t + 1) * P], ps_t[:, u % 2, :, :]).then_inc(dve_copied, 1)

                def invert_totals(n):
                    dve.wait_ge(prob_ready, n * UNITS + UNITS)
                    dve.reciprocal(rate[:, :, :], total[:, :, :]).then_inc(rates_ready, 1)

                def normalise_heads(n):
                    dve.wait_ge(heads_turned, n + 1)
                    dve.wait_ge(rates_ready, n + 1)
                    dve.tensor_tensor(heads_out[:, :, bass.ds(n, 1), :].rearrange("p t a (j d) -> p (t a) j d", j=GROUP),
                                      ps_ct[:, :, :].rearrange("p t (j k) -> p t j k", j=GROUP)[:, :, :, 0:DH],
                                      rate[:, :, :].rearrange("p j t -> p t j").unsqueeze(3).broadcast_to((P, T4, GROUP, DH)),
                                      ALU.mult).then_inc(heads_ready, 1)

                def body(n, first):
                    for u in range(UNITS):
                        add_terms(n, u, first)
                        if u == 0 and not first:
                            invert_totals(n - 1)
                        if u >= COPY_LAG:
                            copy_turned(n, u - COPY_LAG, first)
                        elif not first:
                            copy_turned(n - 1, u - COPY_LAG + UNITS, False)
                        if u == TURN_AT and not first:
                            normalise_heads(n - 1)

                groups(dve, body)
                last = B * GROUPS - 1
                invert_totals(last)
                for u in range(UNITS - COPY_LAG, UNITS):
                    copy_turned(last, u, False)
                normalise_heads(last)

            @block.tensor
            def _(pe):
                def score(n, u, first):
                    j, t = u // T4, u % T4
                    if t == 0:
                        pe.wait_ge(qk_in[j], n * 32 + 32)
                    if not (first and u < 4):
                        pe.wait_ge(neg_ready, n * UNITS + (u - 3))
                    pe.matmul(ps_s[:, u % 4, :], qs[:, j, t * P:(t + 1) * P], ks[:, j, :], start=True, stop=True)\
                        .then_inc(scores_psum, 1)

                def turn(n, u, first):
                    pe.wait_ge(prob_ready, n * UNITS + (u + 1))
                    if not (first and u < 2):
                        pe.wait_ge(*copied(*earlier(n, u, 2)))
                    for k in range(T4):
                        last = pe.transpose(ps_t[:, u % 2, k, :], prob[:, u % 4, k * P:(k + 1) * P], ident[:, :])
                    last.then_inc(turned_psum, 1)

                def weigh(n, first_of_all):
                    pe.wait_ge(dve_copied, n * (GROUP * DVE_TILES) + GROUP * DVE_TILES)
                    pe.wait_ge(act_copied, n * GROUP + GROUP)
                    pe.wait_ge(v_in, n * 16 + 16)
                    if not first_of_all:
                        pe.wait_ge(headT_ready, n)
                    for k in range(T4):
                        for j in range(GROUP):
                            last = pe.matmul(ps_c[32 * j:32 * j + 32, :], v[:, k, j, :], probT[:, j, k, :], start=(k == 0),
                                             stop=(k == T4 - 1), tile_position=(0, 32 * j))
                    last.then_inc(heads_psum, 1)

                def turn_heads(n, first_of_all):
                    pe.wait_ge(headT_ready, n + 1)
                    if not first_of_all:
                        pe.wait_ge(heads_ready, n)
                    for t in range(T4):
                        last = pe.transpose(ps_ct[:, t, :], headT[:, t * P:(t + 1) * P], ident[:, :])
                    last.then_inc(heads_turned, 1)

                def body(n, first):
                    for u in range(UNITS):
                        score(n, u, first)
                        if u >= TURN_LAG:
                            turn(n, u - TURN_LAG, first)
                        elif not first:
                            turn(n - 1, u - TURN_LAG + UNITS, False)
                        if u == WEIGH_AT and not first:
                            weigh(n - 1, False)
                        if u == TURN_AT and not first:
                            turn_heads(n - 1, False)

                groups(pe, body)
                last = B * GROUPS - 1
                for u in range(UNITS - TURN_LAG, UNITS):
                    turn(last, u, False)
                weigh(last, False)
                turn_heads(last, False)

        clear_semaphores(nc, own_sems)


def relative_finish(nc, name, x, xn, heads, consts, w):
    c = consts
    with ExitStack() as ctx:
        own_sems = []

        def sb(n, shape, dt=F32):
            return ctx.enter_context(nc.sbuf_tensor(f"{name}_{n}", shape, dt))

        def ps(n, shape, dt=F32):
            return ctx.enter_context(nc.psum_tensor(f"{name}_{n}", shape, dt))

        def sem(n):
            own_sems.append(ctx.enter_context(nc.semaphore(f"{name}_{n}")))
            return own_sems[-1]

        wo, bo = sb("wo", [P, D]), sb("bo", [P, D])
        ln_scale, ln_bias = sb("ln_scale", [P, D]), sb("ln_bias", [P, D])
        headsT = sb("headsT", [P, TILES, P])
        y, scaled = sb("y", [P, TILES, D]), sb("scaled", [P, TILES, D])
        stats, mv = sb("stats", [P, TILES, 6]), sb("mv", [P, TILES, 2])
        rstd, newton = sb("rstd", [P, TILES]), sb("newton", [P, 5, TILES])
        psT, ps_y = ps("psT", [P, 2, 4, P]), ps("ps_y", [P, 4, 4, P])
        weights_in, chain = sem("weights_in"), sem("chain")
        turned, headsT_ready, y_psum = sem("turned"), sem("headsT_ready"), sem("y_psum")
        var_ready, std_ready = sem("var_ready"), sem("std_ready")

        with nc.Block() as block:

            @block.sync
            def _(sp):
                for dst, src in ((wo, w["Wo"]), (bo, w["bo"].unsqueeze(0).partition_broadcast(P)),
                                 (ln_scale, w["ln_scale"].unsqueeze(0).partition_broadcast(P)),
                                 (ln_bias, w["ln_bias"].unsqueeze(0).partition_broadcast(P))):
                    sp.dma_start(dst[:, :], src).then_inc(weights_in, 16)

            @block.scalar
            def _(act):
                for b in range(B):
                    act.wait_ge(turned, b + 1)
                    nc.scalar.copy(headsT[:, T4 * b:T4 * b + T4, :], psT[:, b % 2, :, :]).then_inc(headsT_ready, 1)
                act.wait_ge(var_ready, 1)
                nc.scalar.activation(newton[:, 0, :], mv[:, :, 1], ACT.Sqrt, bias=c["eps7"][:, 0:1]).then_inc(std_ready, 1)

            @block.tensor
            def _(pe):
                pe.wait_ge(weights_in, 64)
                for b in range(B):
                    if b >= 2:
                        pe.wait_ge(headsT_ready, b - 1)
                    for t in range(T4):
                        last = pe.transpose(psT[:, b % 2, t, :], heads[:, t, b * GROUPS:(b + 1) * GROUPS, :].rearrange("p g k -> p (g k)"), c["ident"][:, :])
                    last.then_inc(turned, 1)
                for b in range(B):
                    pe.wait_ge(headsT_ready, b + 1)
                    for t in range(T4):
                        last = pe.matmul(ps_y[:, b, t, :], headsT[:, T4 * b + t, :], wo[:, :], start=True, stop=True)
                    last.then_inc(y_psum, 1)

            @block.vector
            def _(dve):
                done = chain_on(dve, chain)
                dve.wait_ge(weights_in, 64)
                for b in range(B):
                    dve.wait_ge(y_psum, b + 1)
                    rows = slice(T4 * b, T4 * b + T4)
                    done(dve.tensor_tensor(scaled[:, rows, :], ps_y[:, b, :, :],
                                           bo[:, :].unsqueeze(1).broadcast_to((P, T4, D)), ALU.add))
                    done(dve.tensor_tensor(y[:, rows, :], scaled[:, rows, :], xn[:, rows, :], ALU.add))
                normalise_tokens(dve, done, y, (stats, mv, rstd, newton), 1e-7, std_ready, var_ready)
                for t in range(TILES):
                    last = dve.tensor_scalar(scaled[:, t, :], y[:, t, :], mv[:, t, 0:1], newton[:, 4, t:t + 1],
                                             ALU.subtract, ALU.mult)
                done(last)
                full = (P, TILES, D)
                done(dve.tensor_tensor(y[:, :, :], scaled[:, :, :], ln_scale[:, :].unsqueeze(1).broadcast_to(full), ALU.mult))
                done(dve.tensor_tensor(scaled[:, :, :], y[:, :, :], ln_bias[:, :].unsqueeze(1).broadcast_to(full), ALU.add))
                done(dve.tensor_tensor(x[:, :, :], scaled[:, :, :], x[:, :, :], ALU.add))

        clear_semaphores(nc, own_sems)


def relative_phase(nc, kept, name, x, consts, w, dram):
    with ExitStack() as ctx:
        xn = ctx.enter_context(nc.sbuf_tensor(f"{name}_xn", [P, TILES, D], F32))
        heads = ctx.enter_context(nc.sbuf_tensor(f"{name}_heads", [P, T4, B * GROUPS, GROUP * DH], F32))
        relative_prepare(nc, kept, f"{name}p", x, xn, consts, w, dram)
        relative_attend(nc, kept, f"{name}m", heads, consts, dram)
        relative_finish(nc, f"{name}f", x, xn, heads, consts, w)


def spline_phase(nc, name, x, consts, w):
    c = consts
    with ExitStack() as ctx:
        own_sems = []

        def sb(n, shape, dt=F32):
            return ctx.enter_context(nc.sbuf_tensor(f"{name}_{n}", shape, dt))

        def ps(n, shape, dt=F32):
            return ctx.enter_context(nc.psum_tensor(f"{name}_{n}", shape, dt))

        def sem(n):
            own_sems.append(ctx.enter_context(nc.semaphore(f"{name}_{n}")))
            return own_sems[-1]

        raw = sb("raw", [SIGS, D])
        above = sb("above", [SIGS, D])
        below = sb("below", [SIGS, D])
        ternary = sb("ternary", [SIGS, D])
        change = sb("change", [SIGS, D])
        sigs = sb("sigs", [SIGS, D])
        score_w = sb("score_w", [P, SCORES])
        cluster_sum = sb("cluster_sum", [P, CLUSTERS])
        cluster_neg = sb("cluster_neg", [P, CLUSTERS])
        cluster_pos = sb("cluster_pos", [P, CLUSTERS])
        table = sb("table", [SIGS, PARAMS])
        cw1, cb1, cw2 = sb("cw1", [P, COMP]), sb("cb1", [COMP, 1]), sb("cw2", [COMP, 2])
        cb2 = sb("cb2", [P, 2])
        knots, temp, divisor = sb("knots", [P, KNOTS]), sb("temp", [P, 1]), sb("divisor", [P, 1])
        rate, neg_rate = sb("rate", [P, 1]), sb("neg_rate", [P, 1])
        gamma, beta, out_scale = sb("gamma", [P, D]), sb("beta", [P, D]), sb("out_scale", [P, 1])
        xn = sb("xn", [P, TILES, D])
        xnT = sb("xnT", [P, TILES, P])
        stats, mv = sb("stats", [P, TILES, 6]), sb("mv", [P, TILES, 2])
        rstd, newton = sb("rstd", [P, TILES]), sb("newton", [P, 5, TILES])
        picks = sb("picks", [P, 2, TILES, 8])
        e = sb("e", [P, 2, TILES, 8])
        at = sb("at", [P, TILES * 8])
        reach = sb("reach", [P, TILES * 8, KNOTS - 2])
        low, frac = sb("low", [P, TILES * 8]), sb("frac", [P, TILES * 8])
        seg = sb("seg", [P, TILES * 8, KNOTS - 1])
        picked = sb("picked", [P, TILES * 8, KNOTS - 1])
        v_low, v_high = sb("v_low", [P, TILES * 8]), sb("v_high", [P, TILES * 8])
        rise = sb("rise", [P, TILES * 8])
        gates = sb("gates", [P, TILES, 8])
        best, marks, first = sb("best", [P, TILES]), sb("marks", [P, TILES, 8]), sb("first", [P, TILES])
        chosen = sb("chosen", [P, 2, TILES, 8])
        masked = sb("masked", [P, TILES, CLUSTERS, PER])
        tile_hot = sb("tile_hot", [P, TILES, SIGS])
        tile_hotT = sb("tile_hotT", [SIGS, TILES, P])
        hT = sb("hT", [COMP, TILES, P])
        comp_in, comp = sb("comp_in", [P, TILES, 2]), sb("comp", [P, TILES, 2])
        par = sb("par", [P, TILES, PARAMS])
        term0, term1 = sb("term0", [P, TILES, GRID]), sb("term1", [P, TILES, GRID])
        mag = sb("mag", [P, TILES])
        y, scaled = sb("y", [P, TILES, D]), sb("scaled", [P, TILES, D])

        banks = ps("banks", [P, 8, 512])
        psT = banks[:, 0:2, :].rearrange("p b (k q) -> p b k q", k=4)
        ps_scores = banks[:, 2:6, 0:4 * SCORES].rearrange("p b (k s) -> p b k s", k=4)
        ps_h = banks[:, 6:8, :]
        ps_comp = banks[:, 0, 0:2 * TILES].rearrange("p (t o) -> p t o", o=2)
        ps_sigs = banks[:, 1, 0:SIGS]
        ps_par = banks[:, 2:8, 0:2 * PARAMS].rearrange("p b (k n) -> p b k n", k=2)

        weights_in, sigs_ready, sigsT_psum = sem("weights_in"), sem("sigs_ready"), sem("sigsT_psum")
        score_w_ready = sem("score_w_ready")
        chain = sem("chain")
        var_ready, std_ready = sem("var_ready"), sem("std_ready")
        xn_ready, xnT_psum, xnT_ready = sem("xn_ready"), sem("xnT_psum"), sem("xnT_ready")
        picks_ready = sem("picks_ready")
        scores_ready, e_ready = sem("scores_ready"), sem("e_ready")
        h_psum, h_ready, comp_psum = sem("h_psum"), sem("h_ready"), sem("comp_psum")
        comp_in_ready, comp_ready = sem("comp_in_ready"), sem("comp_ready")
        hot_ready, hotT_psum, hotT_ready = sem("hot_ready"), sem("hotT_psum"), sem("hotT_ready")
        par_psum, par_ready = sem("par_psum"), sem("par_ready")
        var2_ready, std2_ready = sem("var2_ready"), sem("std2_ready")

        with nc.Block() as block:

            @block.sync
            def _(sp):
                loads = [
                    (raw[:, :], w["signatures_raw"]),
                    (cw1[:, :], w["compress_w1"]),
                    (cb1[:, :], w["compress_b1"].unsqueeze(1)),
                    (cw2[:, :], w["compress_w2"]),
                    (cb2[:, :], w["compress_b2"].unsqueeze(0).partition_broadcast(P)),
                    (knots[:, :], w["knot_values"].unsqueeze(0).partition_broadcast(P)),
                    (temp[:, :], w["temperature"].unsqueeze(0).partition_broadcast(P)),
                    (gamma[:, :], w["norm_gamma"].unsqueeze(0).partition_broadcast(P)),
                    (beta[:, :], w["norm_beta"].unsqueeze(0).partition_broadcast(P)),
                    (out_scale[:, :], w["output_scale"].unsqueeze(0).partition_broadcast(P)),
                    (table[:, W1_AT:B1_AT], w["spline_w1"].rearrange("s i g -> s (i g)")),
                    (table[:, B1_AT:W2_AT], w["spline_b1"]),
                    (table[:, W2_AT:B2_AT], w["spline_w2"].rearrange("s g o -> s (g o)")),
                    (table[:, B2_AT:DIR_AT], w["spline_b2"]),
                    (table[:, DIR_AT:PARAMS], w["directions"]),
                ]
                assert len(loads) == SPLINE_LOADS
                for dst, src in loads:
                    sp.dma_start(dst, src).then_inc(weights_in, 16)

            @block.scalar
            def _(act):
                act.wait_ge(var_ready, 1)
                nc.scalar.activation(newton[:, 0, :], mv[:, :, 1], ACT.Sqrt, bias=c["eps5"][:, 0:1]).then_inc(std_ready, 1)
                for g in range(4):
                    act.wait_ge(xnT_psum, g + 1)
                    nc.scalar.copy(xnT[:, 4 * g:4 * g + 4, :], psT[:, g % 2, :, :]).then_inc(xnT_ready, 1)
                for n in range(2):
                    act.wait_ge(picks_ready, n + 1)
                    nc.scalar.activation(e[:, n, :, :], picks[:, n, :, :], ACT.Exp, scale=neg_rate[:, 0:1]).then_inc(e_ready, 1)
                act.wait_ge(weights_in, 16 * SPLINE_LOADS)
                for g in range(4):
                    act.wait_ge(h_psum, g + 1)
                    nc.scalar.activation(hT[:, 4 * g:4 * g + 4, :].rearrange("p k q -> p (k q)"), ps_h[0:COMP, g % 2, :],
                                         ACT.Gelu, bias=cb1[:, 0:1]).then_inc(h_ready, 1)
                act.wait_ge(comp_in_ready, 1)
                nc.scalar.activation(comp[:, :, :], comp_in[:, :, :], ACT.Tanh).then_inc(comp_ready, 1)
                for g in range(8):
                    act.wait_ge(par_psum, g + 1)
                    nc.scalar.copy(par[:, 2 * g:2 * g + 2, :], ps_par[:, g % 6, :, :]).then_inc(par_ready, 1)
                act.wait_ge(var2_ready, 1)
                nc.scalar.activation(newton[:, 0, :], mv[:, :, 1], ACT.Sqrt, bias=c["eps5"][:, 0:1]).then_inc(std2_ready, 1)

            @block.vector
            def _(dve):
                done = chain_on(dve, chain)
                dve.wait_ge(weights_in, 16 * SPLINE_LOADS)
                done(dve.tensor_scalar(above[:, :], raw[:, :], 0.3, None, ALU.is_gt))
                done(dve.tensor_scalar(below[:, :], raw[:, :], -0.3, -1.0, ALU.is_lt, ALU.mult))
                done(dve.tensor_tensor(ternary[:, :], above[:, :], below[:, :], ALU.add))
                done(dve.tensor_tensor(change[:, :], ternary[:, :], raw[:, :], ALU.subtract))
                dve.tensor_tensor(sigs[:, :], raw[:, :], change[:, :], ALU.add).then_inc(sigs_ready, 1)
                done(dve.tensor_scalar(divisor[:, :], temp[:, :], 1e-6, None, ALU.add))
                done(dve.reciprocal(rate[:, :], divisor[:, :]))
                done(dve.tensor_scalar(neg_rate[:, :], rate[:, :], -1.0, None, ALU.mult))
                dve.wait_ge(sigsT_psum, 1)
                done(dve.tensor_copy(score_w[:, CLUSTERS:], ps_sigs))
                done(dve.tensor_reduce(cluster_sum[:, :], score_w[:, CLUSTERS:].rearrange("p (c j) -> p c j", c=CLUSTERS),
                                       AX.X, ALU.add))
                done(dve.tensor_scalar(cluster_pos[:, :], cluster_sum[:, :], 0.0, None, ALU.is_gt))
                done(dve.tensor_scalar(cluster_neg[:, :], cluster_sum[:, :], 0.0, None, ALU.is_lt))
                dve.tensor_tensor(score_w[:, 0:CLUSTERS], cluster_pos[:, :], cluster_neg[:, :], ALU.subtract)\
                    .then_inc(score_w_ready, 1)
                normalise_tokens(dve, done, x, (stats, mv, rstd, newton), 1e-5, std_ready, var_ready)
                for t in range(TILES):
                    dve.tensor_scalar(xn[:, t, :], x[:, t, :], mv[:, t, 0:1], newton[:, 4, t:t + 1],
                                      ALU.subtract, ALU.mult).then_inc(xn_ready, 1)

                def calibrate(n):
                    flat = (P, TILES * 8)
                    ev = e[:, n, :, :].rearrange("p t k -> p (t k)")
                    done(dve.tensor_scalar(at[:, :], ev, 1.0, None, ALU.add))
                    done(dve.reciprocal(low[:, :], at[:, :]))
                    done(dve.tensor_scalar(at[:, :], low[:, :], float(KNOTS - 1), None, ALU.mult))
                    done(dve.tensor_tensor(reach[:, :, :], at[:, :].unsqueeze(2).broadcast_to((*flat, KNOTS - 2)),
                                           c["segment_ids"][:, 1:KNOTS - 1].unsqueeze(1).broadcast_to((*flat, KNOTS - 2)),
                                           ALU.is_ge))
                    done(dve.tensor_reduce(low[:, :], reach[:, :, :], AX.X, ALU.add))
                    done(dve.tensor_tensor(frac[:, :], at[:, :], low[:, :], ALU.subtract))
                    done(dve.tensor_tensor(seg[:, :, :], low[:, :].unsqueeze(2).broadcast_to((*flat, KNOTS - 1)),
                                           c["segment_ids"][:, 0:KNOTS - 1].unsqueeze(1).broadcast_to((*flat, KNOTS - 1)),
                                           ALU.is_equal))
                    for value, k in ((v_low, 0), (v_high, 1)):
                        done(dve.tensor_tensor(picked[:, :, :], seg[:, :, :],
                                               knots[:, k:k + KNOTS - 1].unsqueeze(1).broadcast_to((*flat, KNOTS - 1)),
                                               ALU.mult))
                        done(dve.tensor_reduce(value[:, :], picked[:, :, :], AX.X, ALU.add))
                    done(dve.tensor_tensor(rise[:, :], v_high[:, :], v_low[:, :], ALU.subtract))
                    done(dve.tensor_tensor(rise[:, :], frac[:, :], rise[:, :], ALU.mult))
                    done(dve.tensor_tensor(gates[:, :, :].rearrange("p t k -> p (t k)"), v_low[:, :], rise[:, :], ALU.add))

                def choose(n):
                    wide = (P, TILES, 8)
                    rev = c["countdown8"][:, :].unsqueeze(1).broadcast_to(wide)
                    done(dve.tensor_reduce(best[:, :], gates[:, :, :], AX.X, ALU.max))
                    done(dve.tensor_tensor(marks[:, :, :], gates[:, :, :], best[:, :].unsqueeze(2).broadcast_to(wide),
                                           ALU.is_equal))
                    done(dve.tensor_tensor(marks[:, :, :], marks[:, :, :], rev, ALU.mult))
                    done(dve.tensor_reduce(first[:, :], marks[:, :, :], AX.X, ALU.max))
                    done(dve.tensor_tensor(chosen[:, n, :, :], rev, first[:, :].unsqueeze(2).broadcast_to(wide),
                                           ALU.is_equal))

                dve.wait_ge(scores_ready, 4)
                for g in range(4):
                    last = dve.tensor_copy(picks[:, 0, 4 * g:4 * g + 4, :], ps_scores[:, g, :, 0:CLUSTERS])
                last.then_inc(picks_ready, 1)
                dve.wait_ge(e_ready, 1)
                calibrate(0)
                choose(0)
                for g in range(4):
                    for k in range(4):
                        t = 4 * g + k
                        last = dve.tensor_tensor(masked[:, t, :, :],
                                                 ps_scores[:, g, k, CLUSTERS:].rearrange("p (c j) -> p c j", c=CLUSTERS),
                                                 chosen[:, 0, t, :].unsqueeze(2).broadcast_to((P, CLUSTERS, PER)), ALU.mult)
                done(last)
                dve.tensor_reduce(picks[:, 1, :, :], masked[:, :, :, :].rearrange("p t c j -> p t j c"), AX.X, ALU.add)\
                    .then_inc(picks_ready, 1)
                dve.wait_ge(e_ready, 2)
                calibrate(1)
                choose(1)
                for half in range(2):
                    ts = slice(8 * half, 8 * half + 8)
                    dve.tensor_tensor(tile_hot[:, ts, :].rearrange("p t (c j) -> p t c j", c=CLUSTERS),
                                      chosen[:, 0, ts, :].unsqueeze(3).broadcast_to((P, 8, CLUSTERS, PER)),
                                      chosen[:, 1, ts, :].unsqueeze(2).broadcast_to((P, 8, CLUSTERS, PER)),
                                      ALU.mult).then_inc(hot_ready, 1)
                for g in range(4):
                    dve.wait_ge(hotT_psum, g + 1)
                    dve.tensor_copy(tile_hotT[:, 4 * g:4 * g + 4, :], psT[0:SIGS, g % 2, :, :]).then_inc(hotT_ready, 1)
                dve.wait_ge(comp_psum, 1)
                dve.tensor_tensor(comp_in[:, :, :], ps_comp, cb2[:, :].unsqueeze(1).broadcast_to((P, TILES, 2)), ALU.add)\
                    .then_inc(comp_in_ready, 1)
                dve.wait_ge(comp_ready, 1)
                dve.wait_ge(par_ready, 8)
                grid = (P, TILES, GRID)
                done(dve.tensor_tensor(term0[:, :, :], par[:, :, 0:GRID], comp[:, :, 0:1].broadcast_to(grid), ALU.mult))
                done(dve.tensor_tensor(term1[:, :, :], par[:, :, GRID:B1_AT], comp[:, :, 1:2].broadcast_to(grid), ALU.mult))
                done(dve.tensor_tensor(term0[:, :, :], term0[:, :, :], term1[:, :, :], ALU.add))
                done(dve.tensor_tensor(term0[:, :, :], term0[:, :, :], par[:, :, B1_AT:W2_AT], ALU.add))
                done(dve.scalar_tensor_tensor(term1[:, :, :], term0[:, :, :], 0.0, par[:, :, W2_AT:B2_AT], ALU.max, ALU.mult))
                done(dve.tensor_reduce(mag[:, :], term1[:, :, :], AX.X, ALU.add))
                done(dve.tensor_tensor(mag[:, :].unsqueeze(2), mag[:, :].unsqueeze(2), par[:, :, B2_AT:DIR_AT], ALU.add))
                for t in range(TILES):
                    last = dve.tensor_scalar(scaled[:, t, :], par[:, t, DIR_AT:], mag[:, t:t + 1], out_scale[:, 0:1],
                                             ALU.mult, ALU.mult)
                done(last)
                done(dve.tensor_tensor(y[:, :, :], scaled[:, :, :], xn[:, :, :], ALU.add))
                normalise_tokens(dve, done, y, (stats, mv, rstd, newton), 1e-5, std2_ready, var2_ready)
                for t in range(TILES):
                    last = dve.tensor_scalar(scaled[:, t, :], y[:, t, :], mv[:, t, 0:1], newton[:, 4, t:t + 1],
                                             ALU.subtract, ALU.mult)
                done(last)
                full = (P, TILES, D)
                done(dve.tensor_tensor(y[:, :, :], scaled[:, :, :], gamma[:, :].unsqueeze(1).broadcast_to(full), ALU.mult))
                done(dve.tensor_tensor(scaled[:, :, :], y[:, :, :], beta[:, :].unsqueeze(1).broadcast_to(full), ALU.add))
                done(dve.scalar_tensor_tensor(x[:, :, :], scaled[:, :, :], 0.5, x[:, :, :], ALU.mult, ALU.add))

            @block.tensor
            def _(pe):
                pe.wait_ge(sigs_ready, 1)
                pe.transpose(ps_sigs, sigs[:, :], c["ident"][0:SIGS, 0:SIGS]).then_inc(sigsT_psum, 1)
                pe.wait_ge(score_w_ready, 1)
                for g in range(4):
                    for k in range(4):
                        t = 4 * g + k
                        pe.wait_ge(xn_ready, t + 1)
                        if g >= 2 and k == 0:
                            pe.wait_ge(xnT_ready, g - 1)
                        last = pe.transpose(psT[:, g % 2, k, :], xn[:, t, :], c["ident"][:, :])
                    last.then_inc(xnT_psum, 1)
                for g in range(4):
                    pe.wait_ge(xnT_ready, g + 1)
                    for k in range(4):
                        last = pe.matmul(ps_scores[:, g, k, :], xnT[:, 4 * g + k, :], score_w[:, :], start=True, stop=True)
                    last.then_inc(scores_ready, 1)
                for g in range(4):
                    if g >= 2:
                        pe.wait_ge(h_ready, g - 1)
                    pe.matmul(ps_h[0:COMP, g % 2, :], cw1[:, :], xnT[:, 4 * g:4 * g + 4, :].rearrange("p k q -> p (k q)"),
                              start=True, stop=True).then_inc(h_psum, 1)
                for g in range(4):
                    for k in range(4):
                        t = 4 * g + k
                        if k == 0:
                            pe.wait_ge(hot_ready, t // 8 + 1)
                            if g >= 2:
                                pe.wait_ge(hotT_ready, g - 1)
                        last = pe.transpose(psT[0:SIGS, g % 2, k, :], tile_hot[:, t, :], c["ident"][:, :])
                    last.then_inc(hotT_psum, 1)
                pe.wait_ge(h_ready, 4)
                pe.wait_ge(hotT_ready, 3)
                for t in range(TILES):
                    last = pe.matmul(ps_comp[:, t, :], hT[:, t, :], cw2[:, :], start=True, stop=True)
                last.then_inc(comp_psum, 1)
                for g in range(8):
                    pe.wait_ge(hotT_ready, g // 2 + 1)
                    if g >= 6:
                        pe.wait_ge(par_ready, g - 5)
                    for k in range(2):
                        last = pe.matmul(ps_par[:, g % 6, k, :], tile_hotT[:, 2 * g + k, :], table[:, :], start=True, stop=True)
                    last.then_inc(par_psum, 1)

        clear_semaphores(nc, own_sems)


def causal_phase(nc, name, x, consts, w):
    c = consts
    scale = float(D) ** -0.5
    with ExitStack() as ctx:
        own_sems = []

        def sb(n, shape, dt=F32):
            return ctx.enter_context(nc.sbuf_tensor(f"{name}_{n}", shape, dt))

        def ps(n, shape, dt=F32):
            return ctx.enter_context(nc.psum_tensor(f"{name}_{n}", shape, dt))

        def sem(n):
            own_sems.append(ctx.enter_context(nc.semaphore(f"{name}_{n}")))
            return own_sems[-1]

        T = S // P
        w_kqv, b_kqv = sb("w_kqv", [P, 3, D]), sb("b_kqv", [P, 3, D])
        w_p, b_p = sb("w_p", [P, D]), sb("b_p", [P, D])
        cos, sin = sb("cos", [P, T, D // 2]), sb("sin", [P, T, D // 2])
        xn = sb("xn", [P, TILES, D])
        xnT = sb("xnT", [P, TILES, P])
        stats, mv = sb("stats", [P, TILES, 6]), sb("mv", [P, TILES, 2])
        rstd, newton = sb("rstd", [P, TILES]), sb("newton", [P, 5, TILES])
        kqv = sb("kqv", [P, TILES, 3, D])
        half_a, half_b = sb("half_a", [P, 2, T, 2, D // 2]), sb("half_b", [P, 2, T, 2, D // 2])
        half_c, half_d = sb("half_c", [P, 2, T, 2, D // 2]), sb("half_d", [P, 2, T, 2, D // 2])
        turned = sb("turned", [P, TILES, 2, D])
        kT, qT = sb("kT", [P, TILES, P]), sb("qT", [P, TILES, P])
        size = sb("size", [P, 2, S])
        tail = sb("tail", [P, 2, S])
        soft = sb("soft", [P, 2, S])
        over = sb("over", [P, 2, S])
        weiT = sb("weiT", [P, T, S])
        outT = sb("outT", [P, 2, S])

        ps_kqv = ps("ps_kqv", [P, 2, 512])
        psT = ps("psT", [P, 2, 4, P])
        ps_wei = ps("ps_wei", [P, 2, S])
        ps_out = ps("ps_out", [P, S])
        ps_y = ps("ps_y", [P, T, D])

        weights_in, chain = sem("weights_in"), sem("chain")
        var_ready, std_ready = sem("var_ready"), sem("std_ready")
        xn_ready, xT_psum, xT_ready = sem("xn_ready"), sem("xT_psum"), sem("xT_ready")
        kqv_psum, kqv_ready = sem("kqv_psum"), sem("kqv_ready")
        parts_ready, turned_ready = sem("parts_ready"), sem("turned_ready")
        kq_psum, kq_ready = sem("kq_psum"), sem("kq_ready")
        wei_psum, size_ready, tail_ready, soft_ready = sem("wei_psum"), sem("size_ready"), sem("tail_ready"), sem("soft_ready")
        over_ready, wei_ready, wei_masked = sem("over_ready"), sem("wei_ready"), sem("wei_masked")
        out_psum, out_ready, y_psum, y_added = sem("out_psum"), sem("out_ready"), sem("y_psum"), sem("y_added")

        with nc.Block() as block:

            @block.sync
            def _(sp):
                loads = [(w_kqv[:, n, :], w[k]) for n, k in enumerate(("Wk", "Wq", "Wv"))]
                loads += [(b_kqv[:, n, :], w[k].unsqueeze(0).partition_broadcast(P)) for n, k in enumerate(("bk", "bq", "bv"))]
                loads += [(w_p[:, :], w["Wp"]), (b_p[:, :], w["bp"].unsqueeze(0).partition_broadcast(P)),
                          (cos[:, :, :], w["cos"].rearrange("(t p) f -> p t f", p=P)),
                          (sin[:, :, :], w["sin"].rearrange("(t p) f -> p t f", p=P))]
                assert len(loads) == CAUSAL_LOADS
                for dst, src in loads:
                    sp.dma_start(dst, src).then_inc(weights_in, 16)

            @block.scalar
            def _(act):
                act.wait_ge(var_ready, 1)
                nc.scalar.activation(newton[:, 0, :], mv[:, :, 1], ACT.Sqrt, bias=c["eps5"][:, 0:1]).then_inc(std_ready, 1)
                for g in range(4):
                    act.wait_ge(xT_psum, g + 1)
                    nc.scalar.copy(xnT[:, 4 * g:4 * g + 4, :], psT[:, g % 2, :, :]).then_inc(xT_ready, 1)
                for b in range(B):
                    for n, dst in enumerate((kT, qT)):
                        act.wait_ge(kq_psum, 2 * b + n + 1)
                        nc.scalar.copy(dst[:, T * b:T * b + T, :], psT[:, n, :, :]).then_inc(kq_ready, 1)
                for b in range(B):
                    for j in range(T):
                        k, u = T * b + j, j % 2
                        cols = slice(P * j, S)
                        act.wait_ge(wei_psum, k + 1)
                        if k >= 2:
                            act.wait_ge(wei_ready, k - 1)
                        nc.scalar.activation(size[:, u, cols], ps_wei[:, u, cols], ACT.Abs, scale=scale).then_inc(size_ready, 1)
                        act.wait_ge(size_ready, k + 1)
                        nc.scalar.activation(tail[:, u, cols], size[:, u, cols], ACT.Exp, scale=-1.0).then_inc(tail_ready, 1)
                        act.wait_ge(tail_ready, k + 1)
                        nc.scalar.activation(soft[:, u, cols], tail[:, u, cols], ACT.Ln, bias=1.0).then_inc(soft_ready, 1)
                    act.wait_ge(out_psum, b + 1)
                    if b >= 2:
                        act.wait_ge(y_psum, b - 1)
                    nc.scalar.copy(outT[:, b % 2, :], ps_out[:, :]).then_inc(out_ready, 1)

            @block.gpsimd
            def _(pool):
                for b in range(B):
                    pool.wait_ge(kqv_ready, T * b + T)
                    if b >= 2:
                        pool.wait_ge(turned_ready, b - 1)
                    pair = kqv[:, T * b:T * b + T, 0:2, :].rearrange("p t n (f two) -> p t n f two", two=2)
                    wide = (P, T, 2, D // 2)
                    cs, sn = cos[:, :, :].unsqueeze(2).broadcast_to(wide), sin[:, :, :].unsqueeze(2).broadcast_to(wide)
                    pool.tensor_tensor(half_c[:, b % 2, :, :, :], pair[:, :, :, :, 0], sn, ALU.mult)
                    pool.tensor_tensor(half_d[:, b % 2, :, :, :], pair[:, :, :, :, 1], cs, ALU.mult).then_inc(parts_ready, 1)
                for b in range(B):
                    for j in range(T):
                        pool.wait_ge(wei_ready, T * b + j + 1)
                        block_ = weiT[:, j, P * j:P * j + P]
                        pool.affine_select(block_, block_, compare_op=ALU.is_ge, fill=0.0, base=0,
                                           pattern=[[1, P]], channel_multiplier=-1).then_inc(wei_masked, 1)

            @block.vector
            def _(dve):
                done = chain_on(dve, chain)

                def add_y(b):
                    dve.wait_ge(y_psum, b + 1)
                    xb = x[:, T * b:T * b + T, :]
                    dve.tensor_tensor(xb, ps_y[:, :, :], xb, ALU.add).then_inc(y_added, 1)
                    dve.wait_ge(y_added, b + 1)
                    done(dve.tensor_tensor(xb, xb, b_p[:, :].unsqueeze(1).broadcast_to((P, T, D)), ALU.add))

                normalise_tokens(dve, done, x, (stats, mv, rstd, newton), 1e-5, std_ready, var_ready)
                for t in range(TILES):
                    dve.tensor_scalar(xn[:, t, :], x[:, t, :], mv[:, t, 0:1], newton[:, 4, t:t + 1],
                                      ALU.subtract, ALU.mult).then_inc(xn_ready, 1)
                dve.wait_ge(weights_in, 16 * CAUSAL_LOADS)
                for b in range(B):
                    for t in range(T * b, T * b + T):
                        dve.wait_ge(kqv_psum, t + 1)
                        dve.tensor_tensor(kqv[:, t, :, :], ps_kqv[:, t % 2, 0:3 * D].rearrange("p (n d) -> p n d", n=3),
                                          b_kqv[:, :, :], ALU.add).then_inc(kqv_ready, 1)
                    dve.wait_ge(kqv_ready, T * b + T)
                    pair = kqv[:, T * b:T * b + T, 0:2, :].rearrange("p t n (f two) -> p t n f two", two=2)
                    out = turned[:, T * b:T * b + T, :, :].rearrange("p t n (f two) -> p t n f two", two=2)
                    wide = (P, T, 2, D // 2)
                    cs, sn = cos[:, :, :].unsqueeze(2).broadcast_to(wide), sin[:, :, :].unsqueeze(2).broadcast_to(wide)
                    dve.tensor_tensor(half_a[:, b % 2, :, :, :], pair[:, :, :, :, 0], cs, ALU.mult)
                    done(dve.tensor_tensor(half_b[:, b % 2, :, :, :], pair[:, :, :, :, 1], sn, ALU.mult))
                    dve.tensor_tensor(out[:, :, :, :, 0], half_a[:, b % 2, :, :, :], half_b[:, b % 2, :, :, :], ALU.add)
                    dve.wait_ge(parts_ready, b + 1)
                    dve.tensor_tensor(out[:, :, :, :, 1], half_d[:, b % 2, :, :, :], half_c[:, b % 2, :, :, :], ALU.subtract)\
                        .then_inc(turned_ready, 1)
                for b in range(B):
                    for j in range(T):
                        k, u = T * b + j, j % 2
                        cols = slice(P * j, S)
                        dve.wait_ge(size_ready, k + 1)
                        dve.tensor_scalar(over[:, u, cols], ps_wei[:, u, cols], scale, 0.0, ALU.mult, ALU.max).then_inc(over_ready, 1)
                        dve.wait_ge(over_ready, k + 1)
                        dve.wait_ge(soft_ready, k + 1)
                        if b:
                            dve.wait_ge(out_psum, b)
                        dve.tensor_tensor(weiT[:, j, cols], over[:, u, cols], soft[:, u, cols], ALU.add).then_inc(wei_ready, 1)
                    if b:
                        add_y(b - 1)
                add_y(B - 1)

            @block.tensor
            def _(pe):
                for g in range(4):
                    for k in range(4):
                        t = 4 * g + k
                        pe.wait_ge(xn_ready, t + 1)
                        if g >= 2 and k == 0:
                            pe.wait_ge(xT_ready, g - 1)
                        last = pe.transpose(psT[:, g % 2, k, :], xn[:, t, :], c["ident"][:, :])
                    last.then_inc(xT_psum, 1)
                pe.wait_ge(weights_in, 16 * CAUSAL_LOADS)

                def turn(b):
                    pe.wait_ge(turned_ready, b + 1)
                    for n in range(2):
                        pe.wait_ge(*((xT_ready, 4) if b == 0 else (kq_ready, 2 * b - 1 + n)))
                        for k in range(T):
                            last = pe.transpose(psT[:, n, k, :], turned[:, T * b + k, n, :], c["ident"][:, :])
                        last.then_inc(kq_psum, 1)

                for t in range(TILES):
                    pe.wait_ge(xT_ready, t // 4 + 1)
                    if t >= 2:
                        pe.wait_ge(kqv_ready, t - 1)
                    pe.matmul(ps_kqv[:, t % 2, 0:3 * D], xnT[:, t, :], w_kqv[:, :, :].rearrange("p n d -> p (n d)"),
                              start=True, stop=True).then_inc(kqv_psum, 1)
                    if t % T == T - 1 and t // T:
                        turn(t // T - 1)
                turn(B - 1)

                def project(b):
                    pe.wait_ge(out_ready, b + 1)
                    if b:
                        pe.wait_ge(y_added, b)
                    for k in range(T):
                        last = pe.matmul(ps_y[:, k, :], outT[:, b % 2, k * P:(k + 1) * P], w_p[:, :], start=True, stop=True)
                    last.then_inc(y_psum, 1)

                for b in range(B):
                    for j in range(T):
                        k = T * b + j
                        pe.wait_ge(kq_ready, 2 * b + 2)
                        if k >= 2:
                            pe.wait_ge(over_ready, k - 1)
                        pe.matmul(ps_wei[:, j % 2, P * j:S], qT[:, k, :],
                                  kT[:, k:T * b + T, :].rearrange("p t q -> p (t q)"), start=True, stop=True).then_inc(wei_psum, 1)
                    if b:
                        project(b - 1)
                    for j in range(T):
                        pe.wait_ge(wei_masked, T * b + j + 1)
                        if b and j == 0:
                            pe.wait_ge(out_ready, b)
                        last = pe.matmul(ps_out[:, P * j:S], kqv[:, T * b + j, 2, :], weiT[:, j, P * j:S],
                                         start=(j == 0), stop=(j == T - 1), skip_group_check=True)
                    last.then_inc(out_psum, 1)
                project(B - 1)

        clear_semaphores(nc, own_sems)


def network(nc, inputs, out, tables):
    def weights(prefix, *more):
        names = {n[len(prefix):]: a for n, a in inputs.items() if n.startswith(prefix)}
        return {**names, **{n: tables[n] for n in more}}

    sorted_tokens = nc.dram_tensor("sorted_tokens", (SLOTS * P, D), F32).ap()
    sorted_results = nc.dram_tensor("sorted_results", (SLOTS * P, D), F32).ap()
    with ExitStack() as ctx:
        x = ctx.enter_context(nc.sbuf_tensor("x_tokens", [P, TILES, D], F32))
        c = constants_phase(nc, ctx, x, inputs["L0_attn_hidden_states"], sorted_tokens)
        ffn_phase(nc, ctx, "l0f0", x, c, weights("L0_ffn_"), (sorted_tokens, sorted_results))
        relative_phase(nc, ctx, "l0a", x, c, weights("L0_attn_", "own_head", "far_mask", "block_hot"), attention_dram(nc))
        ffn_phase(nc, ctx, "l0f1", x, c, weights("L0_ffn_"), (sorted_tokens, sorted_results))
        spline_phase(nc, "l1f0", x, c, weights("L1_ffn_"))
        causal_phase(nc, "l1a", x, c, weights("L1_attn_", "cos", "sin"))
        spline_phase(nc, "l1f1", x, c, weights("L1_ffn_"))
        x_out = ctx.enter_context(nc.semaphore("x_out"))
        with nc.Block() as block:

            @block.sync
            def _(sp):
                sp.dma_start(out.rearrange("b (t p) d -> p (b t) d", p=P), x[:, :, :]).then_inc(x_out, 16)
                sp.wait_ge(x_out, 16)


def kernel(**inputs):
    import concourse.bacc as _bacc
    from concourse.bass_utils import run_bass_kernel_spmd as _run

    nc = _bacc.Bacc("TRN2", target_bir_lowering=False, num_devices=1)
    arrays, handles = {}, {}
    for name, a in {**inputs, **host_tables()}.items():
        if name == "L0_attn_attention_mask":
            continue
        arrays[f"in_{name}"] = np.ascontiguousarray(a)
        handles[name] = nc.dram_tensor(f"in_{name}", a.shape, F32, kind="ExternalInput").ap()
    out = nc.dram_tensor("out", (B, S, D), F32, kind="ExternalOutput").ap()
    tables = {name: handles.pop(name) for name in host_tables()}
    network(nc, handles, out, tables)
    r = _run(nc, [arrays], core_ids=[0])
    return r.results[0]["out"]
```

```python
from contextlib import ExitStack

import numpy as np

import concourse.bass as bass
from concourse import mybir

F32 = mybir.dt.float32
BF16 = mybir.dt.bfloat16
I32 = mybir.dt.int32
ALU = mybir.AluOpType
ACT = mybir.ActivationFunctionType
AX = mybir.AxisListType

P = 128
B, S, D = 4, 512, 128
TILES = B * S // P
EXPERTS, FF = 8, 512
FC = FF // P
UNROLL = 4
SLOTS = -(-(TILES + EXPERTS - 1) // UNROLL) * UNROLL
ROUNDS = SLOTS // UNROLL
ROUND_ORDER = [("turn", 0), ("turn", 1), ("up", 0), ("turn", 2), ("up", 1), ("turn_h", 0), ("turn", 3), ("up", 2),
               ("down", 0), ("turn_h", 1), ("up", 3), ("down", 1), ("turn_h", 2), ("down", 2), ("turn_h", 3),
               ("down", 3)]

SIGS, CLUSTERS = 64, 8
PER = SIGS // CLUSTERS
KNOTS, GRID, COMP = 8, 16, 32
SCORES = CLUSTERS + SIGS
W1_AT, B1_AT, W2_AT, B2_AT, DIR_AT = 0, 2 * GRID, 3 * GRID, 4 * GRID, 4 * GRID + 1
PARAMS = DIR_AT + D
SPLINE_LOADS = 15
CAUSAL_LOADS = 10

HEADS, DH = 16, 8
BUCKETS, MAX_REL = 32, 64
NB = S // 64
WIN = 192
GROUP = 4
GROUPS = HEADS // GROUP
T4 = S // P
QUOTA = S + 2 * 64
ROWS = 12


def bucket(d):
    mid = BUCKETS // 2
    size = mid - 1 if -mid < d < mid else abs(d)
    if size <= mid:
        return size
    f = np.float32
    far = np.ceil(np.log(f(size) / f(mid)) / np.log(f((MAX_REL - 1) / mid)) * f(mid - 1)) + f(mid)
    return int(far) * (1 if d > 0 else -1)


def clipped(v):
    return min(max(v, 0), 2 * BUCKETS - 1)


def bucket_runs():
    pair = {d: (clipped(bucket(d) + BUCKETS), clipped(BUCKETS - bucket(-d))) for d in range(1 - S, S)}
    right = max(d for d in pair if all(pair[k] == pair[1 - S] for k in range(1 - S, d + 1)))
    left = min(d for d in pair if all(pair[k] == pair[S - 1] for k in range(d, S)))
    assert left <= 64 and right >= -64
    runs = []
    for d in range(right + 1, left):
        if runs and runs[-1][2:] == pair[d]:
            runs[-1] = (runs[-1][0], d, *pair[d])
        else:
            runs.append((d, d, *pair[d]))
    return runs, left, right, pair[S - 1], pair[1 - S]


RUNS, LEFT, RIGHT, LEFT_ROWS, RIGHT_ROWS = bucket_runs()
USED = sorted({r for run in RUNS for r in run[2:]} | set(LEFT_ROWS) | set(RIGHT_ROWS))
CUT = next(n for n in range(1, len(USED)) if USED[n] != USED[n - 1] + 1)
STRETCHES = [(USED[0], 0, CUT), (USED[CUT], CUT, len(USED) - CUT)]
NP_ = len(USED)
ROW_OF = {p: n for n, p in enumerate(USED)}
PER_CHUNK = P // NP_
CHUNKS = [(h, min(PER_CHUNK, HEADS - h)) for h in range(0, HEADS, PER_CHUNK)]

PREP_LOADS = 10
HUGE = 3.0e38
TURN_LAG, COPY_LAG, WEIGH_LAG = 3, 4, 8
HEADS_LAG, BACK_LAG, RATE_LAG = 12, 13, 14


def host_tables():
    p = np.arange(P)
    i = np.arange(NB)
    mine = (p % NB)[:, None]
    angle = np.outer(np.arange(S, dtype=np.float32), np.arange(D // 2, dtype=np.float32))[::-1].astype(np.float64)
    return {
        "own_head": (p[:, None] // DH == np.arange(HEADS)).astype(np.float32),
        "far_mask": np.stack([mine < i - 1, mine > i + 1], 1).astype(np.float32),
        "block_hot": (mine == i).astype(np.float32),
        "cos": np.cos(angle).astype(np.float32),
        "sin": np.sin(angle).astype(np.float32),
    }


def attention_dram(nc):
    def dram(n, shape, dt=F32):
        return nc.dram_tensor(n, shape, dt).ap()

    return {
        "q": dram("stacked_q", (B, P, ROWS, S), BF16),
        "k": dram("stacked_k", (B, P, ROWS, S), BF16),
        "tab_q": dram("position_q", (B, HEADS * NP_, S)),
        "tab_k": dram("position_k", (B, HEADS * NP_, QUOTA)),
        "v": dram("values", (B, GROUPS, P, T4 * P)),
        "near": dram("near_terms", (B, P, 64, WIN)),
    }


def clear_semaphores(nc, sems):
    numbers = sorted(s.num for s in sems)
    starts = [n for n in numbers if n - 1 not in numbers]
    ends = [n + 1 for n in numbers if n + 1 not in numbers]
    with nc.Block() as block:

        @block.sync
        def _(sp):
            for first, end in zip(starts, ends):
                sp.sem_clear(range(first, end))


def constants_phase(nc, ctx, x, x_dram, xs_dram):
    def sb(n, shape, dt=F32):
        return ctx.enter_context(nc.sbuf_tensor(f"c_{n}", shape, dt))

    c = {
        "ident": sb("ident", [P, P]),
        "ones": sb("ones", [P, P]),
        "ones_b": sb("ones_b", [P, P], BF16),
        "earlier_b": sb("earlier_b", [P, P], BF16),
        "eps5": sb("eps5", [P, 1]),
        "eps7": sb("eps7", [P, 1]),
        "countdown8": sb("countdown8", [P, EXPERTS]),
        "tile_starts": sb("tile_starts", [P, TILES]),
        "earlier8": sb("earlier8", [P, EXPERTS, EXPERTS]),
        "slot_ids": sb("slot_ids", [P, SLOTS]),
        "segment_ids": sb("segment_ids", [P, KNOTS]),
    }
    x_in = ctx.enter_context(nc.semaphore("x_in"))
    filled = ctx.enter_context(nc.semaphore("filled"))
    zero_ready = ctx.enter_context(nc.semaphore("zero_ready"))
    slots_cleared = ctx.enter_context(nc.semaphore("slots_cleared"))
    shaped = ctx.enter_context(nc.semaphore("shaped"))
    with nc.sbuf_tensor("c_zeros", [P, SLOTS, D], F32) as zeros, nc.Block() as block:

        @block.sync
        def _(sp):
            sp.dma_start(x[:, :, :], x_dram.rearrange("b (t p) d -> p (b t) d", p=P)).then_inc(x_in, 16)
            sp.wait_ge(zero_ready, 1)
            sp.dma_start(xs_dram.rearrange("(s p) d -> p s d", p=P), zeros[:, :, :]).then_inc(slots_cleared, 16)
            sp.wait_ge(x_in, 16)
            sp.wait_ge(slots_cleared, 16)

        @block.vector
        def _(dve):
            dve.memset(zeros[:, :, :], 0.0).then_inc(zero_ready, 1)
            dve.memset(c["ident"][:, :], 1.0).then_inc(filled, 1)
            dve.memset(c["ones"][:, :], 1.0).then_inc(filled, 1)
            dve.memset(c["ones_b"][:, :], 1.0).then_inc(filled, 1)
            dve.memset(c["earlier_b"][:, :], 1.0).then_inc(filled, 1)
            dve.memset(c["earlier8"][:, :, :], 1.0).then_inc(filled, 1)
            dve.memset(c["eps5"][:, :], 1e-5).then_inc(filled, 1)
            dve.memset(c["eps7"][:, :], 1e-7).then_inc(filled, 1)

        @block.gpsimd
        def _(pool):
            pool.iota(c["countdown8"][:, :], [[-1, EXPERTS]], base=EXPERTS, channel_multiplier=0,
                      allow_small_or_imprecise_dtypes=True)
            pool.iota(c["tile_starts"][:, :], [[P, TILES]], base=0, channel_multiplier=0,
                      allow_small_or_imprecise_dtypes=True)
            pool.iota(c["segment_ids"][:, :], [[1, KNOTS]], base=0, channel_multiplier=0,
                      allow_small_or_imprecise_dtypes=True)
            pool.iota(c["slot_ids"][:, :], [[1, SLOTS]], base=0, channel_multiplier=0,
                      allow_small_or_imprecise_dtypes=True).then_inc(shaped, 1)
            pool.wait_ge(filled, 7)
            pool.affine_select(c["ident"][:, :], c["ident"][:, :], compare_op=ALU.is_equal, fill=0.0,
                               base=0, pattern=[[-1, P]], channel_multiplier=1)
            pool.affine_select(c["earlier_b"][:, :], c["earlier_b"][:, :], compare_op=ALU.is_gt, fill=0.0,
                               base=0, pattern=[[1, P]], channel_multiplier=-1)
            pool.affine_select(c["earlier8"][:, :, :], c["earlier8"][:, :, :], compare_op=ALU.is_gt, fill=0.0,
                               base=0, pattern=[[1, EXPERTS], [-1, EXPERTS]], channel_multiplier=0).then_inc(shaped, 1)
            pool.wait_ge(shaped, 2)
    return c


def normalise_tokens(dve, done, x, scratch, eps, std_ready, var_ready):
    stats, mv, rstd, newton = scratch
    for t in range(TILES):
        last = dve.bn_stats(stats[:, t, :], x[:, t, :])
    done(last)
    for t in range(TILES):
        last = dve.bn_aggr(mv[:, t, :], stats[:, t, :])
    last.then_inc(var_ready, 1)
    dve.wait_ge(std_ready, 1)
    done(dve.reciprocal(rstd[:, :], newton[:, 0, :]))
    done(dve.tensor_tensor(newton[:, 1, :], rstd[:, :], rstd[:, :], ALU.mult))
    done(dve.scalar_tensor_tensor(newton[:, 2, :], mv[:, :, 1], eps, newton[:, 1, :], ALU.add, ALU.mult))
    done(dve.tensor_scalar(newton[:, 3, :], newton[:, 2, :], -0.5, 1.5, ALU.mult, ALU.add))
    done(dve.tensor_tensor(newton[:, 4, :], rstd[:, :], newton[:, 3, :], ALU.mult))


def two_back(sems, i, j):
    return sems[(j - 2) % UNROLL], i + (1 if j >= 2 else 0)


def chain_on(engine, sem):
    count = [0]

    def done(instruction):
        count[0] += 1
        instruction.then_inc(sem, 1)
        engine.wait_ge(sem, count[0])

    return done


def ffn_phase(nc, kept, name, x, consts, w, scratch_dram):
    c = consts
    xs_dram, ys_dram = scratch_dram
    with ExitStack() as ctx:
        own_sems = []

        def sb(n, shape, dt=F32):
            return ctx.enter_context(nc.sbuf_tensor(f"{name}_{n}", shape, dt))

        def ps(n, shape, dt=F32):
            return ctx.enter_context(nc.psum_tensor(f"{name}_{n}", shape, dt))

        def sem(n):
            own_sems.append(ctx.enter_context(nc.semaphore(f"{name}_{n}")))
            return own_sems[-1]

        def soft_dma_sem(n):
            return kept.enter_context(nc.semaphore(f"{name}_{n}"))

        w1 = sb("w1", [P, EXPERTS, FF])
        w2 = sb("w2", [P, EXPERTS, FC, D])
        b1 = sb("b1", [1, EXPERTS, FF])
        b2 = sb("b2", [1, EXPERTS, D])
        switch_w = sb("switch_w", [P, EXPERTS])
        switch_b = sb("switch_b", [P, EXPERTS])
        xn = sb("xn", [P, TILES, D])
        xnT = sb("xnT", [P, TILES, P])
        stats = sb("stats", [P, TILES, 6])
        mv = sb("mv", [P, TILES, 2])
        rstd = sb("rstd", [P, TILES])
        newton = sb("newton", [P, 5, TILES])
        logits = sb("logits", [P, TILES, EXPERTS])
        top = sb("top", [P, TILES])
        shifted = sb("shifted", [P, TILES, EXPERTS])
        exps = sb("exps", [P, TILES, EXPERTS])
        total = sb("total", [P, TILES])
        gate = sb("gate", [P, TILES])
        half_gate = sb("half_gate", [P, TILES])
        marks = sb("marks", [P, TILES, EXPERTS])
        first = sb("first", [P, TILES])
        onehot = sb("onehot", [P, TILES, EXPERTS])
        onehot_b = sb("onehot_b", [P, TILES, EXPERTS], BF16)
        over = sb("over", [P, EXPERTS, TILES])
        n_slots = sb("n_slots", [P, EXPERTS])
        before = sb("before", [P, EXPERTS, EXPERTS])
        base = sb("base", [P, EXPERTS])
        ends = sb("ends", [P, EXPERTS])
        place = sb("place", [P, TILES, EXPERTS])
        placed = sb("placed", [P, TILES, EXPERTS])
        pos = sb("pos", [P, TILES])
        pos_i = sb("pos_i", [P, TILES], I32)
        past = sb("past", [P, SLOTS, EXPERTS])
        owner = sb("owner", [P, SLOTS])
        owner_i = sb("owner_i", [P, SLOTS], I32)
        xs = sb("xs", [P, UNROLL, D])
        xsT = sb("xsT", [P, UNROLL, P])
        h = sb("h", [P, 2, FF])
        hT = sb("hT", [P, 2, FC, P])
        ys = sb("ys", [P, UNROLL, D])
        yg = sb("yg", [P, TILES, D])

        psT = ps("psT", [P, 2, 4, P])
        psR = ps("psR", [P, 512])
        psU = ps("psU", [P, 2, FF])
        psH = ps("psH", [P, 2, FC, P])
        psY = ps("psY", [P, 512])
        ps_logits = psR[:, 0:TILES * EXPERTS].rearrange("p (t e) -> p t e", t=TILES)
        ys_banks = [psR[:, 0:P], psY[:, 0:P]]
        ps_rank = psR[:, 256:256 + (TILES + 1) * EXPERTS].rearrange("p (t e) -> p t e", e=EXPERTS)

        weights_in = sem("weights_in")
        chain = sem("chain")
        var_ready, std_ready = sem("var_ready"), sem("std_ready")
        xn_ready, xnT_psum, xnT_ready = sem("xn_ready"), sem("xnT_psum"), sem("xnT_ready")
        logits_ready, shifted_ready, exps_ready = sem("logits_ready"), sem("shifted_ready"), sem("exps_ready")
        onehot_ready, rank_ready = sem("onehot_ready"), sem("rank_ready")
        pos_ready, owner_ready = sem("pos_ready"), sem("owner_ready")
        scattered = soft_dma_sem("scattered")
        def sems(n):
            return [sem(f"{n}{j}") for j in range(UNROLL)]

        xs_in, xsT_psum, xsT_ready, up_ready = sems("xs_in"), sems("xsT_psum"), sems("xsT_ready"), sems("up_ready")
        h_ready, hT_psum, hT_ready = sems("h_ready"), sems("hT_psum"), sems("hT_ready")
        down_ready, ys_ready = sems("down_ready"), sems("ys_ready")
        ys_out = [soft_dma_sem(f"ys_out{j}") for j in range(UNROLL)]
        gathered, x_updated = soft_dma_sem("gathered"), sem("x_updated")

        xs_rows = xs_dram.rearrange("(s p) d -> p s d", p=P)
        ys_rows = ys_dram.rearrange("(s p) d -> p s d", p=P)

        def rounds(engine, body):
            body(0, True)
            with engine.Fori(1, ROUNDS) as i:
                body(i, False)

        with nc.Block() as block:

            @block.sync
            def _(sp):
                sp.dma_start(switch_w[:, :], w["switch_w"]).then_inc(weights_in, 16)
                sp.dma_start(switch_b[:, :], w["switch_b"].unsqueeze(0).partition_broadcast(P)).then_inc(weights_in, 16)
                sp.dma_start(w1[:, :, :], w["w1"].rearrange("e d f -> d e f")).then_inc(weights_in, 16)
                sp.dma_start(w2[:, :, :, :], w["w2"].rearrange("e (k p) d -> p e k d", p=P)).then_inc(weights_in, 16)
                sp.dma_start(b1[:, :, :], w["b1"].unsqueeze(0)).then_inc(weights_in, 16)
                sp.dma_start(b2[:, :, :], w["b2"].unsqueeze(0)).then_inc(weights_in, 16)
                sp.wait_ge(scattered, 16 * TILES)

                def body(i, first):
                    for j in range(UNROLL):
                        if not first:
                            sp.wait_ge(xsT_psum[j], i)
                        sp.dma_start(xs[:, j, :], xs_rows[:, bass.ds(i * UNROLL + j, 1), :].rearrange("p a d -> p (a d)")).then_inc(xs_in[j], 16)

                rounds(sp, body)

            @block.gpsimd
            def _(pool):
                pool.wait_ge(pos_ready, 1)
                for t in range(TILES):
                    pool.indirect_dma_start(
                        xs_dram[:, :], bass.IndirectOffsetOnAxis(ap=pos_i[:, t:t + 1], axis=0),
                        xn[:, t, :], None).then_inc(scattered, 16)
                with pool.Fori(0, ROUNDS) as i:
                    for j in range(UNROLL):
                        pool.wait_ge(ys_ready[j], i + 1)
                        pool.dma_start(ys_rows[:, bass.ds(i * UNROLL + j, 1), :].rearrange("p a d -> p (a d)"), ys[:, j, :]).then_inc(ys_out[j], 16)
                for j in range(UNROLL):
                    pool.wait_ge(ys_out[j], 16 * ROUNDS)
                for t in range(TILES):
                    pool.indirect_dma_start(
                        yg[:, t, :], None, ys_dram[:, :],
                        bass.IndirectOffsetOnAxis(ap=pos_i[:, t:t + 1], axis=0)).then_inc(gathered, 16)

            @block.scalar
            def _(act):
                act.wait_ge(var_ready, 1)
                nc.scalar.activation(newton[:, 0, :], mv[:, :, 1], ACT.Sqrt, bias=c["eps5"][:, 0:1]).then_inc(std_ready, 1)
                for g in range(4):
                    act.wait_ge(xnT_psum, g + 1)
                    nc.scalar.copy(xnT[:, 4 * g:4 * g + 4, :], psT[:, g % 2, :, :]).then_inc(xnT_ready, 1)
                act.wait_ge(shifted_ready, 1)
                nc.scalar.activation(exps[:, :, :], shifted[:, :, :], ACT.Exp).then_inc(exps_ready, 1)

                def body(i, first):
                    for j in range(UNROLL):
                        act.wait_ge(up_ready[j], i + 1)
                        if not (first and j < 2):
                            act.wait_ge(*two_back(hT_psum, i, j))
                        nc.scalar.activation(h[:, j % 2, :], psU[:, j % 2, :], ACT.Gelu_apprx_tanh).then_inc(h_ready[j], 1)

                rounds(act, body)

            @block.vector
            def _(dve):
                done = chain_on(dve, chain)
                done(dve.memset(logits[:, :, :], 0.0))
                normalise_tokens(dve, done, x, (stats, mv, rstd, newton), 1e-5, std_ready, var_ready)
                for t in range(TILES):
                    dve.tensor_scalar(xn[:, t, :], x[:, t, :], mv[:, t, 0:1], newton[:, 4, t:t + 1],
                                      ALU.subtract, ALU.mult).then_inc(xn_ready, 1)
                dve.wait_ge(logits_ready, 1)
                dve.wait_ge(weights_in, 96)
                done(dve.tensor_tensor(logits[:, :, :], ps_logits,
                                       switch_b[:, :].unsqueeze(1).broadcast_to((P, TILES, EXPERTS)), ALU.add))
                done(dve.tensor_reduce(top[:, :], logits[:, :, :], AX.X, ALU.max))
                dve.tensor_tensor(shifted[:, :, :], logits[:, :, :],
                                  top[:, :].unsqueeze(2).broadcast_to((P, TILES, EXPERTS)), ALU.subtract).then_inc(shifted_ready, 1)
                dve.wait_ge(exps_ready, 1)
                done(dve.tensor_reduce(total[:, :], exps[:, :, :], AX.X, ALU.add))
                done(dve.reciprocal(gate[:, :], total[:, :]))
                rev = c["countdown8"][:, :].unsqueeze(1).broadcast_to((P, TILES, EXPERTS))
                done(dve.scalar_tensor_tensor(marks[:, :, :], exps[:, :, :], 1.0, rev, ALU.is_equal, ALU.mult))
                done(dve.tensor_reduce(first[:, :], marks[:, :, :], AX.X, ALU.max))
                firsts = first[:, :].unsqueeze(2).broadcast_to((P, TILES, EXPERTS))
                done(dve.tensor_tensor(onehot[:, :, :], rev, firsts, ALU.is_equal))
                dve.tensor_copy(onehot_b[:, :, :], onehot[:, :, :]).then_inc(onehot_ready, 1)
                dve.wait_ge(rank_ready, 1)
                done(dve.tensor_tensor(over[:, :, :], ps_rank[:, TILES, :].unsqueeze(2).broadcast_to((P, EXPERTS, TILES)),
                                       c["tile_starts"][:, :].unsqueeze(1).broadcast_to((P, EXPERTS, TILES)), ALU.is_gt))
                done(dve.tensor_reduce(n_slots[:, :], over[:, :, :], AX.X, ALU.add))
                done(dve.tensor_tensor(before[:, :, :], n_slots[:, :].unsqueeze(1).broadcast_to((P, EXPERTS, EXPERTS)),
                                       c["earlier8"][:, :, :], ALU.mult))
                done(dve.tensor_reduce(base[:, :], before[:, :, :], AX.X, ALU.add))
                done(dve.tensor_tensor(ends[:, :], base[:, :], n_slots[:, :], ALU.add))
                done(dve.scalar_tensor_tensor(place[:, :, :], base[:, :].unsqueeze(1).broadcast_to((P, TILES, EXPERTS)),
                                              float(P), ps_rank[:, 0:TILES, :], ALU.mult, ALU.add))
                done(dve.tensor_tensor(placed[:, :, :], place[:, :, :], onehot[:, :, :], ALU.mult))
                done(dve.tensor_reduce(pos[:, :], placed[:, :, :], AX.X, ALU.add))
                dve.tensor_copy(pos_i[:, :], pos[:, :]).then_inc(pos_ready, 1)
                done(dve.tensor_tensor(past[:, :, :], ends[:, :].unsqueeze(1).broadcast_to((P, SLOTS, EXPERTS)),
                                       c["slot_ids"][:, :].unsqueeze(2).broadcast_to((P, SLOTS, EXPERTS)), ALU.is_le))
                done(dve.tensor_reduce(owner[:, :], past[:, :, :], AX.X, ALU.add))
                dve.tensor_scalar(owner_i[:, :], owner[:, :], float(EXPERTS - 1), None, ALU.min).then_inc(owner_ready, 1)

                done(dve.tensor_scalar(half_gate[:, :], gate[:, :], 0.5, None, ALU.mult))

                def to_xsT(i, j, first):
                    dve.wait_ge(xsT_psum[j], i + 1)
                    if not first:
                        dve.wait_ge(up_ready[j], i)
                    dve.tensor_copy(xsT[:, j, :], psT[:, j % 2, 0, :]).then_inc(xsT_ready[j], 1)

                def to_hT(i, j, first):
                    dve.wait_ge(hT_psum[j], i + 1)
                    if not (first and j < 2):
                        dve.wait_ge(*two_back(down_ready, i, j))
                    dve.tensor_copy(hT[:, j % 2, :, :], psH[:, j % 2, :, :]).then_inc(hT_ready[j], 1)

                def to_ys(i, j, first):
                    dve.wait_ge(down_ready[j], i + 1)
                    if not first:
                        dve.wait_ge(ys_out[j], i * 16)
                    dve.tensor_copy(ys[:, j, :], ys_banks[j % 2]).then_inc(ys_ready[j], 1)

                def body(i, first):
                    for step, j in ROUND_ORDER:
                        if step == "turn":
                            to_xsT(i, j, first)
                        elif step == "turn_h":
                            to_hT(i, j, first)
                        elif step == "down":
                            to_ys(i, j, first)

                rounds(dve, body)
                dve.wait_ge(gathered, 16 * TILES)
                for t in range(TILES):
                    last = dve.scalar_tensor_tensor(x[:, t, :], yg[:, t, :], half_gate[:, t:t + 1], x[:, t, :],
                                                    ALU.mult, ALU.add)
                last.then_inc(x_updated, 1)

            @block.tensor
            def _(pe):
                for g in range(4):
                    for k in range(4):
                        t = 4 * g + k
                        pe.wait_ge(xn_ready, t + 1)
                        if g >= 2 and k == 0:
                            pe.wait_ge(xnT_ready, g - 1)
                        last = pe.transpose(psT[:, g % 2, k, :], xn[:, t, :], c["ident"][:, :])
                    last.then_inc(xnT_psum, 1)
                pe.wait_ge(weights_in, 96)
                pe.wait_ge(xnT_ready, 4)
                for t in range(TILES):
                    last = pe.matmul(ps_logits[:, t, :], xnT[:, t, :], switch_w[:, :], start=True, stop=True)
                last.then_inc(logits_ready, 1)
                pe.wait_ge(onehot_ready, 1)
                pe.matmul(ps_rank[:, 0:TILES, :], c["earlier_b"][:, :], onehot_b[:, :, :], start=True, stop=False,
                          skip_group_check=True)
                for t in range(TILES):
                    n = TILES - t
                    last = pe.matmul(ps_rank[:, t + 1:TILES + 1, :], c["ones_b"][:, :],
                                     onehot_b[:, t:t + 1, :].broadcast_to((P, n, EXPERTS)),
                                     start=False, stop=(t == TILES - 1), skip_group_check=True)
                last.then_inc(rank_ready, 1)
                pe.wait_ge(owner_ready, 1)

                def turn(i, j, first):
                    pe.wait_ge(xs_in[j], i * 16 + 16)
                    if not (first and j < 2):
                        pe.wait_ge(*two_back(xsT_ready, i, j))
                    pe.transpose(psT[:, j % 2, 0, :], xs[:, j, :], c["ident"][:, :]).then_inc(xsT_psum[j], 1)

                def up(i, j, expert, first):
                    pe.wait_ge(xsT_ready[j], i + 1)
                    if not (first and j < 2):
                        pe.wait_ge(*two_back(h_ready, i, j))
                    pe.matmul(psU[:, j % 2, :], c["ones"][0:1, :],
                              b1[:, bass.ds(expert, 1), :].rearrange("p a f -> p (a f)"), start=True, stop=False)
                    pe.matmul(psU[:, j % 2, :], xsT[:, j, :],
                              w1[:, bass.ds(expert, 1), :].rearrange("p a f -> p (a f)"),
                              start=False, stop=True).then_inc(up_ready[j], 1)

                def turn_h(i, j, first):
                    pe.wait_ge(h_ready[j], i + 1)
                    if not (first and j < 2):
                        pe.wait_ge(*two_back(hT_ready, i, j))
                    for k in range(FC):
                        last = pe.transpose(psH[:, j % 2, k, :], h[:, j % 2, k * P:(k + 1) * P], c["ident"][:, :])
                    last.then_inc(hT_psum[j], 1)

                def down(i, j, expert, first):
                    pe.wait_ge(hT_ready[j], i + 1)
                    if not (first and j < 2):
                        pe.wait_ge(*two_back(ys_ready, i, j))
                    pe.matmul(ys_banks[j % 2], c["ones"][0:1, :],
                              b2[:, bass.ds(expert, 1), :].rearrange("p a d -> p (a d)"), start=True, stop=False)
                    for k in range(FC):
                        last = pe.matmul(ys_banks[j % 2], hT[:, j % 2, k, :],
                                         w2[:, bass.ds(expert, 1), k, :].rearrange("p a d -> p (a d)"),
                                         start=False, stop=(k == FC - 1))
                    last.then_inc(down_ready[j], 1)

                def body(i, first):
                    experts = [pe.value_load(owner_i[0:1, bass.ds(i * UNROLL + j, 1)], min_val=0, max_val=EXPERTS - 1)
                               for j in range(UNROLL)]
                    for step, j in ROUND_ORDER:
                        if step == "turn":
                            turn(i, j, first)
                        elif step == "up":
                            up(i, j, experts[j], first)
                        elif step == "turn_h":
                            turn_h(i, j, first)
                        else:
                            down(i, j, experts[j], first)

                rounds(pe, body)

        clear_semaphores(nc, own_sems)


def relative_prepare(nc, kept, name, x, xn, consts, w, dram):
    c = consts
    inv = 1.0 / float(np.sqrt(np.float32(DH * 3)))
    with ExitStack() as ctx:
        own_sems = []

        def sb(n, shape, dt=F32):
            return ctx.enter_context(nc.sbuf_tensor(f"{name}_{n}", shape, dt))

        def ps(n, shape, dt=F32):
            return ctx.enter_context(nc.psum_tensor(f"{name}_{n}", shape, dt))

        def sem(n):
            own_sems.append(ctx.enter_context(nc.semaphore(f"{name}_{n}")))
            return own_sems[-1]

        def soft_dma_sem(n):
            return kept.enter_context(nc.semaphore(f"{name}_{n}"))

        wq, wk, wv = sb("wq", [P, D]), sb("wk", [P, D]), sb("wv", [P, D])
        bq, bk, bv = sb("bq", [P, 1]), sb("bk", [P, 1]), sb("bv", [P, D])
        rel = sb("rel", [2 * BUCKETS, D])
        relT = sb("relT", [P, 2 * BUCKETS])
        pos, pos_s = sb("pos", [P, 2 * BUCKETS]), sb("pos_s", [P, 2 * BUCKETS])
        own_head = sb("own_head", [P, HEADS])
        far_mask = sb("far_mask", [P, 2, NB])
        block_hot = sb("block_hot", [P, NB])
        hot_rows = sb("hot_rows", [P, S], BF16)
        tab_w = sb("tab_w", [P, 2, HEADS, NP_])
        far_w = sb("far_w", [P, 4, HEADS, NB])
        xnT = sb("xnT", [P, TILES, P])
        stats, mv = sb("stats", [P, TILES, 6]), sb("mv", [P, TILES, 2])
        rstd, newton = sb("rstd", [P, TILES]), sb("newton", [P, 5, TILES])
        whole = sb("whole", [P, 2, 4, S])
        far_l, far_r = sb("far_l", [P, 2, S]), sb("far_r", [P, 2, S])
        rest, rest2 = sb("rest", [P, 4, S]), sb("rest2", [P, 4, S])
        parts = sb("parts", [P, 2, 4, 3, S], BF16)
        rows = sb("rows", [P, 4, S])
        v_pad = sb("v_pad", [P, TILES, HEADS, 32])
        edge = sb("edge", [P, 64])

        psT = ps("psT", [P, 2, 4, P])
        ps_qk = ps("ps_qk", [P, 2, S])
        ps_far = ps("ps_far", [P, 2, S])
        ps_tab = ps("ps_tab", [P, 2, S])

        weights_in, chain = sem("weights_in"), sem("chain")
        rel_ready, relT_psum, relT_ready, pos_psum, shapes_ready = (
            sem("rel_ready"), sem("relT_psum"), sem("relT_ready"), sem("pos_psum"), sem("shapes_ready"))
        var_ready, std_ready = sem("var_ready"), sem("std_ready")
        xn_ready, xT_psum, xT_ready = sem("xn_ready"), sem("xT_psum"), sem("xT_ready")
        qk_psum, qk_ready, far_psum, far_ready = sem("qk_psum"), sem("qk_ready"), sem("far_psum"), sem("far_ready")
        hi_ready, rest_ready, mid_ready, lo_ready = sem("hi_ready"), sem("rest_ready"), sem("mid_ready"), sem("lo_ready")
        tab_psum, rows_ready = sem("tab_psum"), sem("rows_ready")
        rows_out = [soft_dma_sem(f"rows_out{k}") for k in range(4)]
        v_psum, v_ready = sem("v_psum"), sem("v_ready")
        parts_out = [sem(f"parts_out{k}") for k in range(2)]
        v_out, hot_out, edge_out = soft_dma_sem("v_out"), sem("hot_out"), sem("edge_out")

        n_rows = 2 * len(CHUNKS)

        with nc.Block() as block:

            @block.sync
            def _(sp):
                loads = [
                    (wq[:, :], w["Wq"]), (wk[:, :], w["Wk"]), (wv[:, :], w["Wv"]),
                    (bq[:, :], w["bq"].unsqueeze(1)), (bk[:, :], w["bk"].unsqueeze(1)),
                    (bv[:, :], w["bv"].unsqueeze(0).partition_broadcast(P)),
                    (rel[:, :], w["rel_embeddings"]), (own_head[:, :], w["own_head"]),
                    (far_mask[:, :, :], w["far_mask"]), (block_hot[:, :], w["block_hot"]),
                ]
                assert len(loads) == PREP_LOADS
                for dst, src in loads:
                    sp.dma_start(dst, src).then_inc(weights_in, 16)
                sp.wait_ge(shapes_ready, 1)
                for b in range(B):
                    for e in (0, 64 + S):
                        for h0, n in CHUNKS:
                            sp.dma_start(dram["tab_k"][b, h0 * NP_:(h0 + n) * NP_, e:e + 64], edge[0:n * NP_, :])\
                                .then_inc(edge_out, 16)
                    for dst, r in ((dram["k"], 6), (dram["k"], 7), (dram["k"], 8), (dram["q"], 9), (dram["q"], 10), (dram["q"], 11)):
                        sp.dma_start(dst[b, :, r, :], hot_rows[:, :]).then_inc(hot_out, 16)
                sp.wait_ge(edge_out, 16 * 2 * len(CHUNKS) * B)
                sp.wait_ge(hot_out, 16 * 6 * B)
                for b in range(B):
                    u = b % 2
                    sp.wait_ge(hi_ready, 4 * b + 4)
                    sp.wait_ge(mid_ready, 4 * b + 4)
                    sp.wait_ge(lo_ready, 4 * b + 4)
                    for dst, r, n, src in (("q", 0, 0, 0), ("q", 1, 0, 0), ("q", 2, 0, 0), ("q", 3, 0, 1), ("q", 4, 0, 1), ("q", 5, 0, 2),
                                           ("k", 0, 1, 0), ("k", 1, 1, 1), ("k", 2, 1, 2), ("k", 3, 1, 0), ("k", 4, 1, 1), ("k", 5, 1, 0),
                                           ("q", 6, 2, 0), ("q", 7, 2, 1), ("q", 8, 2, 2), ("k", 9, 3, 0), ("k", 10, 3, 1), ("k", 11, 3, 2)):
                        sp.dma_start(dram[dst][b, :, r, :], parts[:, u, n, src, :]).then_inc(parts_out[u], 16)
                for u in range(2):
                    sp.wait_ge(parts_out[u], 16 * 18 * (B // 2))

            @block.gpsimd
            def _(pool):
                for b in range(B):
                    for k in range(n_rows):
                        side, (h0, n) = k // len(CHUNKS), CHUNKS[k % len(CHUNKS)]
                        m = n_rows * b + k
                        pool.wait_ge(rows_ready, m + 1)
                        dst = dram["tab_k"][b, h0 * NP_:(h0 + n) * NP_, 64:64 + S] if side else \
                            dram["tab_q"][b, h0 * NP_:(h0 + n) * NP_, :]
                        pool.dma_start(dst, rows[0:n * NP_, m % 4, :]).then_inc(rows_out[m % 4], 16)
                    pool.wait_ge(v_ready, b + 1)
                    pool.dma_start(dram["v"][b].rearrange("g p (t k) -> p t g k", t=T4),
                                   v_pad[:, T4 * b:T4 * b + T4, :, :].rearrange("p t (g j) k -> p t g (j k)", g=GROUPS)).then_inc(v_out, 16)
                for k in range(4):
                    pool.wait_ge(rows_out[k], 16 * (n_rows * B // 4))
                pool.wait_ge(v_out, 16 * B)

            @block.scalar
            def _(act):
                act.wait_ge(var_ready, 1)
                nc.scalar.activation(newton[:, 0, :], mv[:, :, 1], ACT.Sqrt, bias=c["eps5"][:, 0:1]).then_inc(std_ready, 1)
                for g in range(4):
                    act.wait_ge(xT_psum, g + 1)
                    nc.scalar.copy(xnT[:, 4 * g:4 * g + 4, :], psT[:, g % 2, :, :]).then_inc(xT_ready, 1)
                for b in range(B):
                    u = b % 2
                    for n in range(4):
                        if n < 2:
                            act.wait_ge(qk_ready, 2 * b + n + 1)
                        else:
                            act.wait_ge(far_ready, 2 * b + n - 1)
                        if b >= 2:
                            act.wait_ge(parts_out[u], 16 * 18 * (b // 2))
                        nc.scalar.copy(parts[:, u, n, 0, :], whole[:, u, n, :]).then_inc(hi_ready, 1)
                    for n in range(4):
                        act.wait_ge(rest_ready, 4 * b + n + 1)
                        nc.scalar.copy(parts[:, u, n, 1, :], rest[:, n, :]).then_inc(mid_ready, 1)
                    for k in range(n_rows):
                        m = n_rows * b + k
                        n = CHUNKS[k % len(CHUNKS)][1]
                        act.wait_ge(tab_psum, m + 1)
                        if m >= 4:
                            act.wait_ge(rows_out[m % 4], 16 * (m // 4))
                        nc.scalar.copy(rows[0:n * NP_, m % 4, :], ps_tab[0:n * NP_, m % 2, :]).then_inc(rows_ready, 1)

            @block.vector
            def _(dve):
                done = chain_on(dve, chain)
                dve.memset(edge[:, :], 0.0)
                dve.memset(v_pad[:, :, :, DH + 1:], 0.0)
                dve.memset(v_pad[:, :, :, DH:DH + 1], 1.0)
                dve.wait_ge(weights_in, 16 * PREP_LOADS)
                done(dve.tensor_copy(hot_rows[:, :].rearrange("p (n k) -> p n k", n=NB),
                                     block_hot[:, :].unsqueeze(2).broadcast_to((P, NB, 64))))
                dve.wait_ge(relT_psum, 1)
                dve.tensor_copy(relT[:, :], psT[:, 0, 0, 0:2 * BUCKETS]).then_inc(relT_ready, 1)
                dve.wait_ge(pos_psum, 1)
                done(dve.tensor_scalar(pos[:, :], psT[:, 1, 0, 0:2 * BUCKETS], bk[:, 0:1], None, ALU.add))
                done(dve.tensor_scalar(pos_s[:, :], pos[:, :], inv, None, ALU.mult))
                for side, src in enumerate((pos, pos_s)):
                    for p0, n0, n in STRETCHES:
                        wide = (P, HEADS, n)
                        dve.tensor_tensor(tab_w[:, side, :, n0:n0 + n], src[:, p0:p0 + n].unsqueeze(1).broadcast_to(wide),
                                          own_head[:, :].unsqueeze(2).broadcast_to(wide), ALU.mult)
                    for far, row in enumerate((LEFT_ROWS[side], RIGHT_ROWS[side])):
                        last = dve.tensor_scalar(far_w[:, 2 * side + far, :, :], own_head[:, :].unsqueeze(2).broadcast_to((P, HEADS, NB)),
                                                 src[:, row:row + 1], None, ALU.mult)
                last.then_inc(shapes_ready, 1)
                normalise_tokens(dve, done, x, (stats, mv, rstd, newton), 1e-5, std_ready, var_ready)
                for t in range(TILES):
                    dve.tensor_scalar(xn[:, t, :], x[:, t, :], mv[:, t, 0:1], newton[:, 4, t:t + 1],
                                      ALU.subtract, ALU.mult).then_inc(xn_ready, 1)
                for b in range(B):
                    u = b % 2
                    dve.wait_ge(qk_psum, b + 1)
                    if b >= 2:
                        dve.wait_ge(hi_ready, 4 * (b - 1))
                        dve.wait_ge(tab_psum, n_rows * (b - 1))
                    dve.tensor_scalar(whole[:, u, 0, :], ps_qk[:, 0, :], bq[:, 0:1], inv, ALU.add, ALU.mult).then_inc(qk_ready, 1)
                    dve.tensor_scalar(whole[:, u, 1, :], ps_qk[:, 1, :], bk[:, 0:1], None, ALU.add).then_inc(qk_ready, 1)
                    for n in range(2):
                        dve.wait_ge(far_psum, 2 * b + n + 1)
                        for far, dst in enumerate((far_l, far_r)):
                            last = dve.tensor_tensor(dst[:, n, :].rearrange("p (i k) -> p i k", i=NB),
                                                     ps_far[:, far, :].rearrange("p (i k) -> p i k", i=NB),
                                                     far_mask[:, far if n == 0 else 1 - far, :].unsqueeze(2).broadcast_to((P, NB, 64)), ALU.mult)
                        done(last)
                        dve.tensor_tensor(whole[:, u, 2 + n, :], far_l[:, n, :], far_r[:, n, :], ALU.add).then_inc(far_ready, 1)
                    dve.wait_ge(v_psum, b + 1)
                    dve.tensor_tensor(v_pad[:, T4 * b:T4 * b + T4, :, 0:DH],
                                      psT[:, 0, :, :].rearrange("p t (h d) -> p t h d", h=HEADS),
                                      bv[:, :].rearrange("p (h d) -> p h d", h=HEADS).unsqueeze(1).broadcast_to((P, T4, HEADS, DH)),
                                      ALU.add).then_inc(v_ready, 1)
                    for n in range(4):
                        dve.wait_ge(hi_ready, 4 * b + n + 1)
                        if b:
                            dve.wait_ge(mid_ready, 4 * (b - 1) + n + 1)
                        dve.tensor_tensor(rest[:, n, :], whole[:, u, n, :], parts[:, u, n, 0, :], ALU.subtract).then_inc(rest_ready, 1)
                    for n in range(4):
                        dve.wait_ge(mid_ready, 4 * b + n + 1)
                        dve.wait_ge(rest_ready, 4 * b + n + 1)
                        dve.tensor_tensor(parts[:, u, n, 2, :], rest[:, n, :], parts[:, u, n, 1, :], ALU.subtract).then_inc(lo_ready, 1)

            @block.tensor
            def _(pe):
                pe.wait_ge(weights_in, 16 * PREP_LOADS)
                pe.transpose(psT[:, 0, 0, 0:2 * BUCKETS], rel[:, :], c["ident"][0:2 * BUCKETS, 0:2 * BUCKETS]).then_inc(relT_psum, 1)
                pe.wait_ge(relT_ready, 1)
                pe.matmul(psT[:, 1, 0, 0:2 * BUCKETS], wk[:, :], relT[:, :], start=True, stop=True).then_inc(pos_psum, 1)
                pe.wait_ge(shapes_ready, 1)
                for g in range(4):
                    for k in range(4):
                        t = 4 * g + k
                        pe.wait_ge(xn_ready, t + 1)
                        if g >= 2 and k == 0:
                            pe.wait_ge(xT_ready, g - 1)
                        last = pe.transpose(psT[:, g % 2, k, :], xn[:, t, :], c["ident"][:, :])
                    last.then_inc(xT_psum, 1)
                pe.wait_ge(xT_ready, 4)
                for b in range(B):
                    u = b % 2
                    tokens = xnT[:, T4 * b:T4 * b + T4, :].rearrange("p t q -> p (t q)")
                    if b:
                        pe.wait_ge(qk_ready, 2 * b)
                    pe.matmul(ps_qk[:, 0, :], wq[:, :], tokens, start=True, stop=True)
                    pe.matmul(ps_qk[:, 1, :], wk[:, :], tokens, start=True, stop=True).then_inc(qk_psum, 1)
                    if b:
                        pe.wait_ge(v_ready, b)
                    for t in range(T4):
                        last = pe.matmul(psT[:, 0, t, :], xnT[:, T4 * b + t, :], wv[:, :], start=True, stop=True)
                    last.then_inc(v_psum, 1)
                    for n in range(2):
                        pe.wait_ge(qk_ready, 2 * b + n + 1)
                        if 2 * b + n:
                            pe.wait_ge(far_ready, 2 * b + n)
                        for far in range(2):
                            last = pe.matmul(ps_far[:, far, :], far_w[:, 2 * n + far, :, :].rearrange("p h j -> p (h j)"),
                                             whole[:, u, n, :], start=True, stop=True)
                        last.then_inc(far_psum, 1)
                    for k in range(n_rows):
                        side, (h0, n) = k // len(CHUNKS), CHUNKS[k % len(CHUNKS)]
                        m = n_rows * b + k
                        if m >= 2:
                            pe.wait_ge(rows_ready, m - 1)
                        pe.matmul(ps_tab[0:n * NP_, m % 2, :], tab_w[:, side, h0:h0 + n, :].rearrange("p h r -> p (h r)"),
                                  whole[:, u, side, :], start=True, stop=True).then_inc(tab_psum, 1)

        clear_semaphores(nc, own_sems)


def relative_attend(nc, kept, name, heads_out, consts, dram):
    with ExitStack() as ctx:
        own_sems = []

        def sb(n, shape, dt=F32):
            return ctx.enter_context(nc.sbuf_tensor(f"{name}_{n}", shape, dt))

        def ps(n, shape, dt=F32):
            return ctx.enter_context(nc.psum_tensor(f"{name}_{n}", shape, dt))

        def sem(n):
            own_sems.append(ctx.enter_context(nc.semaphore(f"{name}_{n}")))
            return own_sems[-1]

        def soft_dma_sem(n):
            return kept.enter_context(nc.semaphore(f"{name}_{n}"))

        HALF = 32
        K = 8 * ROWS
        UNITS = T4 * GROUP
        PROBS = 4
        PITCH = 6 * P
        ident = consts["ident"]
        rows_q, rows_k = sb("rows_q", [P, NP_ * 64]), sb("rows_k", [P, NP_ * WIN])
        near = sb("near", [P, HALF * WIN])
        qs, ks = sb("qs", [K, 2, GROUP, S], BF16), sb("ks", [K, 2, GROUP, S], BF16)
        v = sb("v", [P, 2, T4, GROUP, 32])
        bias = sb("bias", [P, GROUP, T4 * PITCH])
        neg, neg_top = sb("neg", [P, 4, S]), sb("neg_top", [P, 4])
        prob = sb("prob", [P, PROBS, S])
        probT = sb("probT", [P, 2, GROUP, T4, P])
        headT = sb("headT", [P, 2, P])
        rate = sb("rate", [P, 2, GROUP])

        ps_s = ps("ps_s", [P, 4, S])
        ps_t = ps("ps_t", [P, 2, T4, P])
        ps_c = ps("ps_c", [P, 2, 4, P])

        cleared, units_begun = sem("cleared"), sem("units_begun")
        rows_in, rows_free, near_steps, near_out = sem("rows_in"), sem("rows_free"), sem("near_steps"), soft_dma_sem("near_out")
        qk_in = [sem(f"qk_in{k}") for k in range(2)]
        v_in = [sem(f"v_in{k}") for k in range(2)]
        bias_in = [sem(f"bias_in{t}") for t in range(T4)]
        scores_psum, neg_ready, prob_ready, turned_psum = (
            sem("scores_psum"), sem("neg_ready"), sem("prob_ready"), sem("turned_psum"))
        copied = sem("copied_even"), sem("copied_odd")
        weighed, headT_ready, heads_turned, rates_ready, heads_ready = (
            sem("weighed"), sem("headT_ready"), sem("heads_turned"), sem("rates_ready"), sem("heads_ready"))

        def is_first(n):
            return isinstance(n, int) and n == 0

        def turn_of_parity(n, k):
            return n // 2 if isinstance(n, int) else (n - k) // 2

        def behind(n, u, lag):
            if u - lag >= UNITS:
                return None
            if u >= lag:
                return n, u - lag
            return None if is_first(n) else (n - 1, u - lag + UNITS)

        def pairs(engine, body, lag):
            body(0, 0, range(UNITS))
            body(1, 1, range(UNITS))
            with engine.Fori(1, B * GROUPS // 2) as m:
                body(m * 2, 0, range(UNITS))
                body(m * 2 + 1, 1, range(UNITS))
            body(LAST, 1, range(UNITS, UNITS + lag))

        LAST = B * GROUPS - 1

        with nc.Block() as block:

            @block.sync
            def _(sp):
                def load_rows(b):
                    for g in range(NB):
                        dst = bass.AP(rows_q[:, :].tensor, g * NP_ * 64, [(NB * NP_ * 64, HEADS), (64, NP_), (1, 64)])
                        src = bass.AP(dram["tab_q"].tensor, b * (HEADS * NP_ * S) + g * 64, [(NP_ * S, HEADS), (S, NP_), (1, 64)])
                        sp.dma_start(dst, src).then_inc(rows_in, 16)
                        dst = bass.AP(rows_k[:, :].tensor, g * NP_ * WIN, [(NB * NP_ * WIN, HEADS), (WIN, NP_), (1, WIN)])
                        src = bass.AP(dram["tab_k"].tensor, b * (HEADS * NP_ * QUOTA) + g * 64,
                                      [(NP_ * QUOTA, HEADS), (QUOTA, NP_), (1, WIN)])
                        sp.dma_start(dst, src).then_inc(rows_in, 16)

                def load_operands(n, b, g, fresh):
                    k = g % 2
                    head = b * HEADS + g * GROUP
                    if not fresh:
                        sp.wait_ge(scores_psum, n * UNITS - UNITS)
                    for side, dst in (("q", qs), ("k", ks)):
                        src = bass.AP(dram[side].tensor, head * (K * S), [(S, K), (K * S, GROUP), (1, S)])
                        sp.dma_start(dst[:, k, :, :], src).then_inc(qk_in[k], 16)
                    if not fresh:
                        sp.wait_ge(weighed, n * T4 - T4)
                    src = bass.AP(dram["v"].tensor, n * (P * T4 * P), [(T4 * P, P), (1, T4 * P)])
                    sp.dma_start(v[:, k, :, :, :].rearrange("p t j k -> p (t j k)"), src).then_inc(v_in[k], 16)

                def load_near(n, b, g, first):
                    head = b * HEADS + g * GROUP
                    for t in range(T4):
                        if not first:
                            sp.wait_ge(neg_ready, n * UNITS + (GROUP * (t + 1) - UNITS))
                        elif t == 0:
                            sp.wait_ge(cleared, 1)
                        if g == 0 and t == 0:
                            sp.wait_ge(near_out, b * 32 + 32)
                        for s in range(2):
                            src = bass.AP(dram["near"].tensor, head * (NB * 64 * WIN) + (2 * t + s) * (64 * WIN),
                                          [(WIN, 64), (NB * 64 * WIN, GROUP), (1, WIN)])
                            at = t * PITCH + 64 * s
                            sp.dma_start(bias[64 * s:64 * s + 64, :, at:at + WIN], src).then_inc(bias_in[t], 16)

                def batch(b, first):
                    for g in range(GROUPS):
                        n = b * GROUPS + g
                        load_operands(n, b, g, first and g < 2)
                        load_near(n, b, g, first and g == 0)

                load_rows(0)
                sp.wait_ge(rows_free, 1)
                load_rows(1)
                batch(0, True)
                with sp.Fori(1, B - 1) as b:
                    sp.wait_ge(rows_free, b + 1)
                    load_rows(b + 1)
                    batch(b, False)
                batch(B - 1, False)

            @block.gpsimd
            def _(pool):
                def view(buffer, offset, *dims):
                    t = buffer[:, :].tensor
                    return bass.AP(t, offset, [(t.shape[1], P), *dims])

                def lay_out(b, first):
                    pool.wait_ge(rows_in, b * (32 * NB) + 32 * NB)
                    for half in range(2):
                        q0 = HALF * half
                        if not (first and half == 0):
                            pool.wait_ge(near_out, b * 32 + 16 * half)

                        def far(rows, c0, c1):
                            rq, rk = (ROW_OF[r] for r in rows)
                            return pool.tensor_tensor(
                                view(near, c0, (WIN, HALF), (1, c1 - c0)), view(rows_q, rq * 64 + q0, (1, HALF), (0, c1 - c0)),
                                view(rows_k, rk * WIN + c0, (0, HALF), (1, c1 - c0)), ALU.add)

                        far(LEFT_ROWS, 0, q0 + HALF + 64 - LEFT)
                        far(RIGHT_ROWS, q0 + 64 - RIGHT, WIN).then_inc(near_steps, 1)
                        pool.wait_ge(near_steps, b * 4 + (2 * half + 1))
                        for d0, d1, pq, pk in RUNS:
                            at, width = q0 + 64 - d1, d1 - d0 + 1
                            last = pool.tensor_tensor(
                                view(near, at, (WIN + 1, HALF), (1, width)), view(rows_q, ROW_OF[pq] * 64 + q0, (1, HALF), (0, width)),
                                view(rows_k, ROW_OF[pk] * WIN + at, (1, HALF), (1, width)), ALU.add)
                        last.then_inc(near_steps, 1)
                        pool.wait_ge(near_steps, b * 4 + (2 * half + 2))
                        dst = bass.AP(dram["near"].tensor, b * (P * 64 * WIN) + q0 * WIN, [(64 * WIN, P), (1, HALF * WIN)])
                        pool.dma_start(dst, near[:, :]).then_inc(near_out, 16)
                    pool.engine_nop().then_inc(rows_free, 1)

                lay_out(0, True)
                with pool.Fori(1, B) as b:
                    lay_out(b, False)
                pool.wait_ge(near_out, 32 * B)

            @block.scalar
            def _(act):
                def copy_turned(n, u):
                    t, j = u // GROUP, u % GROUP
                    if j % 2 == 0:
                        return
                    act.wait_ge(turned_psum, n * UNITS + (u + 1))
                    nc.scalar.copy(probT[:, t % 2, j, :, :], ps_t[:, u % 2, :, :]).then_inc(copied[1], 1)

                def exp(n, u):
                    act.wait_ge(neg_ready, n * UNITS + (u + 1))
                    nc.scalar.activation(prob[:, u % PROBS, :], neg[:, u % 4, :], ACT.Exp, bias=neg_top[:, u % 4:u % 4 + 1],
                                         scale=-1.0).then_inc(prob_ready, 1)

                def copy_heads(n, t):
                    act.wait_ge(weighed, n * T4 + (t + 1))
                    if not (is_first(n) and t < 2):
                        act.wait_ge(heads_turned, n * T4 + (t - 1))
                    nc.scalar.copy(headT[:, t % 2, :], ps_c[:, t % 2, 0, :]).then_inc(headT_ready, 1)

                def body(n, parity, steps):
                    for u in steps:
                        if at := behind(n, u, COPY_LAG):
                            copy_turned(*at)
                        if at := behind(n, u, 0):
                            exp(*at)
                        if (at := behind(n, u, HEADS_LAG)) and at[1] % GROUP == 0:
                            copy_heads(at[0], at[1] // GROUP)

                pairs(act, body, HEADS_LAG)

            @block.vector
            def _(dve):
                dve.memset(bias[:, :, :], 0.0).then_inc(cleared, 1)
                dve.wait_ge(cleared, 1)

                def copy_turned(n, u):
                    t, j = u // GROUP, u % GROUP
                    if j % 2:
                        return
                    dve.wait_ge(turned_psum, n * UNITS + (u + 1))
                    dve.tensor_copy(probT[:, t % 2, j, :, :], ps_t[:, u % 2, :, :]).then_inc(copied[0], 1)

                def add_terms(n, u):
                    t, j = u // GROUP, u % GROUP
                    dve.wait_ge(scores_psum, n * UNITS + (u + 1))
                    if j == 0:
                        dve.wait_ge(bias_in[t], n * 32 + 32)
                    dve.sem_inc(units_begun, 1)
                    at = t * (PITCH - P) + 64
                    dve.tensor_tensor_reduce(out=neg[:, u % 4, :], in0=ps_s[:, u % 4, :], in1=bias[:, j, at:at + S], scale=-1.0,
                                             scalar=HUGE, op0=ALU.add, op1=ALU.min,
                                             accum_out=neg_top[:, u % 4:u % 4 + 1]).then_inc(neg_ready, 1)

                def by_head(t):
                    return ps_c[:, t % 2, 1, :].rearrange("p (j k) -> p j k", j=GROUP)

                def invert_sums(n, t):
                    dve.wait_ge(heads_turned, n * T4 + (t + 1))
                    dve.reciprocal(rate[:, t % 2, :], by_head(t)[:, :, DH]).then_inc(rates_ready, 1)

                def normalise_heads(n, t):
                    dve.wait_ge(rates_ready, n * T4 + (t + 1))
                    dve.tensor_tensor(heads_out[:, t, bass.ds(n, 1), :].rearrange("p a (j d) -> p (a j) d", j=GROUP),
                                      by_head(t)[:, :, 0:DH], rate[:, t % 2, :].unsqueeze(2).broadcast_to((P, GROUP, DH)),
                                      ALU.mult).then_inc(heads_ready, 1)

                def body(n, parity, steps):
                    for u in steps:
                        if at := behind(n, u, COPY_LAG):
                            copy_turned(*at)
                        if at := behind(n, u, 0):
                            add_terms(*at)
                        if (at := behind(n, u, RATE_LAG)) and at[1] % GROUP == 0:
                            invert_sums(at[0], at[1] // GROUP)
                        if (at := behind(n, u, RATE_LAG + 1)) and at[1] % GROUP == 0:
                            normalise_heads(at[0], at[1] // GROUP)

                pairs(dve, body, RATE_LAG + 1)

            @block.tensor
            def _(pe):
                def score(n, k, u):
                    t, j = u // GROUP, u % GROUP
                    if u == 0:
                        pe.wait_ge(qk_in[k], turn_of_parity(n, k) * 32 + 32)
                    pe.matmul(ps_s[:, u % 4, :], qs[:, k, j, t * P:(t + 1) * P], ks[:, k, j, :], start=True, stop=True)\
                        .then_inc(scores_psum, 1)

                def turn(n, u):
                    pe.wait_ge(prob_ready, n * UNITS + (u + 1))
                    if not (is_first(n) and u < 2):
                        pe.wait_ge(copied[u % 2], n * (UNITS // 2) + u // 2)
                    for i in range(T4):
                        last = pe.transpose(ps_t[:, u % 2, i, :], prob[:, u % PROBS, i * P:(i + 1) * P], ident[:, :])
                    last.then_inc(turned_psum, 1)

                def weigh(n, k, t, i):
                    if i == 0:
                        pe.wait_ge(copied[0], n * (UNITS // 2) + (t + 1) * (GROUP // 2))
                        pe.wait_ge(copied[1], n * (UNITS // 2) + (t + 1) * (GROUP // 2))
                        if t == 0:
                            pe.wait_ge(v_in[k], turn_of_parity(n, k) * 16 + 16)
                        if not (is_first(n) and t < 2):
                            pe.wait_ge(heads_ready, n * T4 + (t - 1))
                    for j in range(GROUP):
                        last = pe.matmul(ps_c[32 * j:32 * j + 32, t % 2, 0, :], v[:, k, i, j, :],
                                         probT[:, t % 2, j, i, :], start=(i == 0), stop=(i == T4 - 1),
                                         tile_position=(0, 32 * j))
                    if i == T4 - 1:
                        last.then_inc(weighed, 1)

                def turn_heads(n, t):
                    pe.wait_ge(headT_ready, n * T4 + (t + 1))
                    pe.transpose(ps_c[:, t % 2, 1, :], headT[:, t % 2, :], ident[:, :]).then_inc(heads_turned, 1)

                def body(n, k, steps):
                    for u in steps:
                        if at := behind(n, u, 0):
                            score(n, k, u)
                        if at := behind(n, u, WEIGH_LAG):
                            weigh(at[0], k if u >= WEIGH_LAG else 1 - k, at[1] // T4, at[1] % T4)
                        if at := behind(n, u, TURN_LAG):
                            turn(*at)
                        if (at := behind(n, u, BACK_LAG)) and at[1] % GROUP == 0:
                            turn_heads(at[0], at[1] // GROUP)

                pairs(pe, body, BACK_LAG)

        clear_semaphores(nc, own_sems)


def relative_finish(nc, name, x, xn, heads, consts, w):
    c = consts
    with ExitStack() as ctx:
        own_sems = []

        def sb(n, shape, dt=F32):
            return ctx.enter_context(nc.sbuf_tensor(f"{name}_{n}", shape, dt))

        def ps(n, shape, dt=F32):
            return ctx.enter_context(nc.psum_tensor(f"{name}_{n}", shape, dt))

        def sem(n):
            own_sems.append(ctx.enter_context(nc.semaphore(f"{name}_{n}")))
            return own_sems[-1]

        wo, bo = sb("wo", [P, D]), sb("bo", [P, D])
        ln_scale, ln_bias = sb("ln_scale", [P, D]), sb("ln_bias", [P, D])
        headsT = sb("headsT", [P, TILES, P])
        y, scaled = sb("y", [P, TILES, D]), sb("scaled", [P, TILES, D])
        stats, mv = sb("stats", [P, TILES, 6]), sb("mv", [P, TILES, 2])
        rstd, newton = sb("rstd", [P, TILES]), sb("newton", [P, 5, TILES])
        psT, ps_y = ps("psT", [P, 2, 4, P]), ps("ps_y", [P, 4, 4, P])
        weights_in, chain = sem("weights_in"), sem("chain")
        turned, headsT_ready, y_psum = sem("turned"), sem("headsT_ready"), sem("y_psum")
        var_ready, std_ready = sem("var_ready"), sem("std_ready")

        with nc.Block() as block:

            @block.sync
            def _(sp):
                for dst, src in ((wo, w["Wo"]), (bo, w["bo"].unsqueeze(0).partition_broadcast(P)),
                                 (ln_scale, w["ln_scale"].unsqueeze(0).partition_broadcast(P)),
                                 (ln_bias, w["ln_bias"].unsqueeze(0).partition_broadcast(P))):
                    sp.dma_start(dst[:, :], src).then_inc(weights_in, 16)

            @block.scalar
            def _(act):
                for b in range(B):
                    act.wait_ge(turned, b + 1)
                    nc.scalar.copy(headsT[:, T4 * b:T4 * b + T4, :], psT[:, b % 2, :, :]).then_inc(headsT_ready, 1)
                act.wait_ge(var_ready, 1)
                nc.scalar.activation(newton[:, 0, :], mv[:, :, 1], ACT.Sqrt, bias=c["eps7"][:, 0:1]).then_inc(std_ready, 1)

            @block.tensor
            def _(pe):
                pe.wait_ge(weights_in, 64)
                for b in range(B):
                    if b >= 2:
                        pe.wait_ge(headsT_ready, b - 1)
                    for t in range(T4):
                        last = pe.transpose(psT[:, b % 2, t, :], heads[:, t, b * GROUPS:(b + 1) * GROUPS, :].rearrange("p g k -> p (g k)"), c["ident"][:, :])
                    last.then_inc(turned, 1)
                for b in range(B):
                    pe.wait_ge(headsT_ready, b + 1)
                    for t in range(T4):
                        last = pe.matmul(ps_y[:, b, t, :], headsT[:, T4 * b + t, :], wo[:, :], start=True, stop=True)
                    last.then_inc(y_psum, 1)

            @block.vector
            def _(dve):
                done = chain_on(dve, chain)
                dve.wait_ge(weights_in, 64)
                for b in range(B):
                    dve.wait_ge(y_psum, b + 1)
                    rows = slice(T4 * b, T4 * b + T4)
                    done(dve.tensor_tensor(scaled[:, rows, :], ps_y[:, b, :, :],
                                           bo[:, :].unsqueeze(1).broadcast_to((P, T4, D)), ALU.add))
                    done(dve.tensor_tensor(y[:, rows, :], scaled[:, rows, :], xn[:, rows, :], ALU.add))
                normalise_tokens(dve, done, y, (stats, mv, rstd, newton), 1e-7, std_ready, var_ready)
                for t in range(TILES):
                    last = dve.tensor_scalar(scaled[:, t, :], y[:, t, :], mv[:, t, 0:1], newton[:, 4, t:t + 1],
                                             ALU.subtract, ALU.mult)
                done(last)
                full = (P, TILES, D)
                done(dve.tensor_tensor(y[:, :, :], scaled[:, :, :], ln_scale[:, :].unsqueeze(1).broadcast_to(full), ALU.mult))
                done(dve.tensor_tensor(scaled[:, :, :], y[:, :, :], ln_bias[:, :].unsqueeze(1).broadcast_to(full), ALU.add))
                done(dve.tensor_tensor(x[:, :, :], scaled[:, :, :], x[:, :, :], ALU.add))

        clear_semaphores(nc, own_sems)


def relative_phase(nc, kept, name, x, consts, w, dram):
    with ExitStack() as ctx:
        xn = ctx.enter_context(nc.sbuf_tensor(f"{name}_xn", [P, TILES, D], F32))
        heads = ctx.enter_context(nc.sbuf_tensor(f"{name}_heads", [P, T4, B * GROUPS, GROUP * DH], F32))
        relative_prepare(nc, kept, f"{name}p", x, xn, consts, w, dram)
        relative_attend(nc, kept, f"{name}m", heads, consts, dram)
        relative_finish(nc, f"{name}f", x, xn, heads, consts, w)


def spline_phase(nc, name, x, consts, w):
    c = consts
    with ExitStack() as ctx:
        own_sems = []

        def sb(n, shape, dt=F32):
            return ctx.enter_context(nc.sbuf_tensor(f"{name}_{n}", shape, dt))

        def ps(n, shape, dt=F32):
            return ctx.enter_context(nc.psum_tensor(f"{name}_{n}", shape, dt))

        def sem(n):
            own_sems.append(ctx.enter_context(nc.semaphore(f"{name}_{n}")))
            return own_sems[-1]

        raw = sb("raw", [SIGS, D])
        above = sb("above", [SIGS, D])
        below = sb("below", [SIGS, D])
        ternary = sb("ternary", [SIGS, D])
        change = sb("change", [SIGS, D])
        sigs = sb("sigs", [SIGS, D])
        score_w = sb("score_w", [P, SCORES])
        cluster_sum = sb("cluster_sum", [P, CLUSTERS])
        cluster_neg = sb("cluster_neg", [P, CLUSTERS])
        cluster_pos = sb("cluster_pos", [P, CLUSTERS])
        table = sb("table", [SIGS, PARAMS])
        cw1, cb1, cw2 = sb("cw1", [P, COMP]), sb("cb1", [COMP, 1]), sb("cw2", [COMP, 2])
        cb2 = sb("cb2", [P, 2])
        knots, temp, divisor = sb("knots", [P, KNOTS]), sb("temp", [P, 1]), sb("divisor", [P, 1])
        rate, neg_rate = sb("rate", [P, 1]), sb("neg_rate", [P, 1])
        gamma, beta, out_scale = sb("gamma", [P, D]), sb("beta", [P, D]), sb("out_scale", [P, 1])
        xn = sb("xn", [P, TILES, D])
        xnT = sb("xnT", [P, TILES, P])
        stats, mv = sb("stats", [P, TILES, 6]), sb("mv", [P, TILES, 2])
        rstd, newton = sb("rstd", [P, TILES]), sb("newton", [P, 5, TILES])
        picks = sb("picks", [P, 2, TILES, 8])
        e = sb("e", [P, 2, TILES, 8])
        at = sb("at", [P, TILES * 8])
        reach = sb("reach", [P, TILES * 8, KNOTS - 2])
        low, frac = sb("low", [P, TILES * 8]), sb("frac", [P, TILES * 8])
        seg = sb("seg", [P, TILES * 8, KNOTS - 1])
        picked = sb("picked", [P, TILES * 8, KNOTS - 1])
        v_low, v_high = sb("v_low", [P, TILES * 8]), sb("v_high", [P, TILES * 8])
        rise = sb("rise", [P, TILES * 8])
        gates = sb("gates", [P, TILES, 8])
        best, marks, first = sb("best", [P, TILES]), sb("marks", [P, TILES, 8]), sb("first", [P, TILES])
        chosen = sb("chosen", [P, 2, TILES, 8])
        masked = sb("masked", [P, TILES, CLUSTERS, PER])
        tile_hot = sb("tile_hot", [P, TILES, SIGS])
        tile_hotT = sb("tile_hotT", [SIGS, TILES, P])
        hT = sb("hT", [COMP, TILES, P])
        comp_in, comp = sb("comp_in", [P, TILES, 2]), sb("comp", [P, TILES, 2])
        par = sb("par", [P, TILES, PARAMS])
        term0, term1 = sb("term0", [P, TILES, GRID]), sb("term1", [P, TILES, GRID])
        mag = sb("mag", [P, TILES])
        y, scaled = sb("y", [P, TILES, D]), sb("scaled", [P, TILES, D])

        banks = ps("banks", [P, 8, 512])
        psT = banks[:, 0:2, :].rearrange("p b (k q) -> p b k q", k=4)
        ps_scores = banks[:, 2:6, 0:4 * SCORES].rearrange("p b (k s) -> p b k s", k=4)
        ps_h = banks[:, 6:8, :]
        ps_comp = banks[:, 0, 0:2 * TILES].rearrange("p (t o) -> p t o", o=2)
        ps_sigs = banks[:, 1, 0:SIGS]
        ps_par = banks[:, 2:8, 0:2 * PARAMS].rearrange("p b (k n) -> p b k n", k=2)

        weights_in, sigs_ready, sigsT_psum = sem("weights_in"), sem("sigs_ready"), sem("sigsT_psum")
        score_w_ready = sem("score_w_ready")
        chain = sem("chain")
        var_ready, std_ready = sem("var_ready"), sem("std_ready")
        xn_ready, xnT_psum, xnT_ready = sem("xn_ready"), sem("xnT_psum"), sem("xnT_ready")
        picks_ready = sem("picks_ready")
        scores_ready, e_ready = sem("scores_ready"), sem("e_ready")
        h_psum, h_ready, comp_psum = sem("h_psum"), sem("h_ready"), sem("comp_psum")
        comp_in_ready, comp_ready = sem("comp_in_ready"), sem("comp_ready")
        hot_ready, hotT_psum, hotT_ready = sem("hot_ready"), sem("hotT_psum"), sem("hotT_ready")
        par_psum, par_ready = sem("par_psum"), sem("par_ready")
        var2_ready, std2_ready = sem("var2_ready"), sem("std2_ready")

        with nc.Block() as block:

            @block.sync
            def _(sp):
                loads = [
                    (raw[:, :], w["signatures_raw"]),
                    (cw1[:, :], w["compress_w1"]),
                    (cb1[:, :], w["compress_b1"].unsqueeze(1)),
                    (cw2[:, :], w["compress_w2"]),
                    (cb2[:, :], w["compress_b2"].unsqueeze(0).partition_broadcast(P)),
                    (knots[:, :], w["knot_values"].unsqueeze(0).partition_broadcast(P)),
                    (temp[:, :], w["temperature"].unsqueeze(0).partition_broadcast(P)),
                    (gamma[:, :], w["norm_gamma"].unsqueeze(0).partition_broadcast(P)),
                    (beta[:, :], w["norm_beta"].unsqueeze(0).partition_broadcast(P)),
                    (out_scale[:, :], w["output_scale"].unsqueeze(0).partition_broadcast(P)),
                    (table[:, W1_AT:B1_AT], w["spline_w1"].rearrange("s i g -> s (i g)")),
                    (table[:, B1_AT:W2_AT], w["spline_b1"]),
                    (table[:, W2_AT:B2_AT], w["spline_w2"].rearrange("s g o -> s (g o)")),
                    (table[:, B2_AT:DIR_AT], w["spline_b2"]),
                    (table[:, DIR_AT:PARAMS], w["directions"]),
                ]
                assert len(loads) == SPLINE_LOADS
                for dst, src in loads:
                    sp.dma_start(dst, src).then_inc(weights_in, 16)

            @block.scalar
            def _(act):
                act.wait_ge(var_ready, 1)
                nc.scalar.activation(newton[:, 0, :], mv[:, :, 1], ACT.Sqrt, bias=c["eps5"][:, 0:1]).then_inc(std_ready, 1)
                for g in range(4):
                    act.wait_ge(xnT_psum, g + 1)
                    nc.scalar.copy(xnT[:, 4 * g:4 * g + 4, :], psT[:, g % 2, :, :]).then_inc(xnT_ready, 1)
                for n in range(2):
                    act.wait_ge(picks_ready, n + 1)
                    nc.scalar.activation(e[:, n, :, :], picks[:, n, :, :], ACT.Exp, scale=neg_rate[:, 0:1]).then_inc(e_ready, 1)
                act.wait_ge(weights_in, 16 * SPLINE_LOADS)
                for g in range(4):
                    act.wait_ge(h_psum, g + 1)
                    nc.scalar.activation(hT[:, 4 * g:4 * g + 4, :].rearrange("p k q -> p (k q)"), ps_h[0:COMP, g % 2, :],
                                         ACT.Gelu, bias=cb1[:, 0:1]).then_inc(h_ready, 1)
                act.wait_ge(comp_in_ready, 1)
                nc.scalar.activation(comp[:, :, :], comp_in[:, :, :], ACT.Tanh).then_inc(comp_ready, 1)
                for g in range(8):
                    act.wait_ge(par_psum, g + 1)
                    nc.scalar.copy(par[:, 2 * g:2 * g + 2, :], ps_par[:, g % 6, :, :]).then_inc(par_ready, 1)
                act.wait_ge(var2_ready, 1)
                nc.scalar.activation(newton[:, 0, :], mv[:, :, 1], ACT.Sqrt, bias=c["eps5"][:, 0:1]).then_inc(std2_ready, 1)

            @block.vector
            def _(dve):
                done = chain_on(dve, chain)
                dve.wait_ge(weights_in, 16 * SPLINE_LOADS)
                done(dve.tensor_scalar(above[:, :], raw[:, :], 0.3, None, ALU.is_gt))
                done(dve.tensor_scalar(below[:, :], raw[:, :], -0.3, -1.0, ALU.is_lt, ALU.mult))
                done(dve.tensor_tensor(ternary[:, :], above[:, :], below[:, :], ALU.add))
                done(dve.tensor_tensor(change[:, :], ternary[:, :], raw[:, :], ALU.subtract))
                dve.tensor_tensor(sigs[:, :], raw[:, :], change[:, :], ALU.add).then_inc(sigs_ready, 1)
                done(dve.tensor_scalar(divisor[:, :], temp[:, :], 1e-6, None, ALU.add))
                done(dve.reciprocal(rate[:, :], divisor[:, :]))
                done(dve.tensor_scalar(neg_rate[:, :], rate[:, :], -1.0, None, ALU.mult))
                dve.wait_ge(sigsT_psum, 1)
                done(dve.tensor_copy(score_w[:, CLUSTERS:], ps_sigs))
                done(dve.tensor_reduce(cluster_sum[:, :], score_w[:, CLUSTERS:].rearrange("p (c j) -> p c j", c=CLUSTERS),
                                       AX.X, ALU.add))
                done(dve.tensor_scalar(cluster_pos[:, :], cluster_sum[:, :], 0.0, None, ALU.is_gt))
                done(dve.tensor_scalar(cluster_neg[:, :], cluster_sum[:, :], 0.0, None, ALU.is_lt))
                dve.tensor_tensor(score_w[:, 0:CLUSTERS], cluster_pos[:, :], cluster_neg[:, :], ALU.subtract)\
                    .then_inc(score_w_ready, 1)
                normalise_tokens(dve, done, x, (stats, mv, rstd, newton), 1e-5, std_ready, var_ready)
                for t in range(TILES):
                    dve.tensor_scalar(xn[:, t, :], x[:, t, :], mv[:, t, 0:1], newton[:, 4, t:t + 1],
                                      ALU.subtract, ALU.mult).then_inc(xn_ready, 1)

                def calibrate(n):
                    flat = (P, TILES * 8)
                    ev = e[:, n, :, :].rearrange("p t k -> p (t k)")
                    done(dve.tensor_scalar(at[:, :], ev, 1.0, None, ALU.add))
                    done(dve.reciprocal(low[:, :], at[:, :]))
                    done(dve.tensor_scalar(at[:, :], low[:, :], float(KNOTS - 1), None, ALU.mult))
                    done(dve.tensor_tensor(reach[:, :, :], at[:, :].unsqueeze(2).broadcast_to((*flat, KNOTS - 2)),
                                           c["segment_ids"][:, 1:KNOTS - 1].unsqueeze(1).broadcast_to((*flat, KNOTS - 2)),
                                           ALU.is_ge))
                    done(dve.tensor_reduce(low[:, :], reach[:, :, :], AX.X, ALU.add))
                    done(dve.tensor_tensor(frac[:, :], at[:, :], low[:, :], ALU.subtract))
                    done(dve.tensor_tensor(seg[:, :, :], low[:, :].unsqueeze(2).broadcast_to((*flat, KNOTS - 1)),
                                           c["segment_ids"][:, 0:KNOTS - 1].unsqueeze(1).broadcast_to((*flat, KNOTS - 1)),
                                           ALU.is_equal))
                    for value, k in ((v_low, 0), (v_high, 1)):
                        done(dve.tensor_tensor(picked[:, :, :], seg[:, :, :],
                                               knots[:, k:k + KNOTS - 1].unsqueeze(1).broadcast_to((*flat, KNOTS - 1)),
                                               ALU.mult))
                        done(dve.tensor_reduce(value[:, :], picked[:, :, :], AX.X, ALU.add))
                    done(dve.tensor_tensor(rise[:, :], v_high[:, :], v_low[:, :], ALU.subtract))
                    done(dve.tensor_tensor(rise[:, :], frac[:, :], rise[:, :], ALU.mult))
                    done(dve.tensor_tensor(gates[:, :, :].rearrange("p t k -> p (t k)"), v_low[:, :], rise[:, :], ALU.add))

                def choose(n):
                    wide = (P, TILES, 8)
                    rev = c["countdown8"][:, :].unsqueeze(1).broadcast_to(wide)
                    done(dve.tensor_reduce(best[:, :], gates[:, :, :], AX.X, ALU.max))
                    done(dve.tensor_tensor(marks[:, :, :], gates[:, :, :], best[:, :].unsqueeze(2).broadcast_to(wide),
                                           ALU.is_equal))
                    done(dve.tensor_tensor(marks[:, :, :], marks[:, :, :], rev, ALU.mult))
                    done(dve.tensor_reduce(first[:, :], marks[:, :, :], AX.X, ALU.max))
                    done(dve.tensor_tensor(chosen[:, n, :, :], rev, first[:, :].unsqueeze(2).broadcast_to(wide),
                                           ALU.is_equal))

                dve.wait_ge(scores_ready, 4)
                for g in range(4):
                    last = dve.tensor_copy(picks[:, 0, 4 * g:4 * g + 4, :], ps_scores[:, g, :, 0:CLUSTERS])
                last.then_inc(picks_ready, 1)
                dve.wait_ge(e_ready, 1)
                calibrate(0)
                choose(0)
                for g in range(4):
                    for k in range(4):
                        t = 4 * g + k
                        last = dve.tensor_tensor(masked[:, t, :, :],
                                                 ps_scores[:, g, k, CLUSTERS:].rearrange("p (c j) -> p c j", c=CLUSTERS),
                                                 chosen[:, 0, t, :].unsqueeze(2).broadcast_to((P, CLUSTERS, PER)), ALU.mult)
                done(last)
                dve.tensor_reduce(picks[:, 1, :, :], masked[:, :, :, :].rearrange("p t c j -> p t j c"), AX.X, ALU.add)\
                    .then_inc(picks_ready, 1)
                dve.wait_ge(e_ready, 2)
                calibrate(1)
                choose(1)
                for half in range(2):
                    ts = slice(8 * half, 8 * half + 8)
                    dve.tensor_tensor(tile_hot[:, ts, :].rearrange("p t (c j) -> p t c j", c=CLUSTERS),
                                      chosen[:, 0, ts, :].unsqueeze(3).broadcast_to((P, 8, CLUSTERS, PER)),
                                      chosen[:, 1, ts, :].unsqueeze(2).broadcast_to((P, 8, CLUSTERS, PER)),
                                      ALU.mult).then_inc(hot_ready, 1)
                for g in range(4):
                    dve.wait_ge(hotT_psum, g + 1)
                    dve.tensor_copy(tile_hotT[:, 4 * g:4 * g + 4, :], psT[0:SIGS, g % 2, :, :]).then_inc(hotT_ready, 1)
                dve.wait_ge(comp_psum, 1)
                dve.tensor_tensor(comp_in[:, :, :], ps_comp, cb2[:, :].unsqueeze(1).broadcast_to((P, TILES, 2)), ALU.add)\
                    .then_inc(comp_in_ready, 1)
                dve.wait_ge(comp_ready, 1)
                dve.wait_ge(par_ready, 8)
                grid = (P, TILES, GRID)
                done(dve.tensor_tensor(term0[:, :, :], par[:, :, 0:GRID], comp[:, :, 0:1].broadcast_to(grid), ALU.mult))
                done(dve.tensor_tensor(term1[:, :, :], par[:, :, GRID:B1_AT], comp[:, :, 1:2].broadcast_to(grid), ALU.mult))
                done(dve.tensor_tensor(term0[:, :, :], term0[:, :, :], term1[:, :, :], ALU.add))
                done(dve.tensor_tensor(term0[:, :, :], term0[:, :, :], par[:, :, B1_AT:W2_AT], ALU.add))
                done(dve.scalar_tensor_tensor(term1[:, :, :], term0[:, :, :], 0.0, par[:, :, W2_AT:B2_AT], ALU.max, ALU.mult))
                done(dve.tensor_reduce(mag[:, :], term1[:, :, :], AX.X, ALU.add))
                done(dve.tensor_tensor(mag[:, :].unsqueeze(2), mag[:, :].unsqueeze(2), par[:, :, B2_AT:DIR_AT], ALU.add))
                for t in range(TILES):
                    last = dve.tensor_scalar(scaled[:, t, :], par[:, t, DIR_AT:], mag[:, t:t + 1], out_scale[:, 0:1],
                                             ALU.mult, ALU.mult)
                done(last)
                done(dve.tensor_tensor(y[:, :, :], scaled[:, :, :], xn[:, :, :], ALU.add))
                normalise_tokens(dve, done, y, (stats, mv, rstd, newton), 1e-5, std2_ready, var2_ready)
                for t in range(TILES):
                    last = dve.tensor_scalar(scaled[:, t, :], y[:, t, :], mv[:, t, 0:1], newton[:, 4, t:t + 1],
                                             ALU.subtract, ALU.mult)
                done(last)
                full = (P, TILES, D)
                done(dve.tensor_tensor(y[:, :, :], scaled[:, :, :], gamma[:, :].unsqueeze(1).broadcast_to(full), ALU.mult))
                done(dve.tensor_tensor(scaled[:, :, :], y[:, :, :], beta[:, :].unsqueeze(1).broadcast_to(full), ALU.add))
                done(dve.scalar_tensor_tensor(x[:, :, :], scaled[:, :, :], 0.5, x[:, :, :], ALU.mult, ALU.add))

            @block.tensor
            def _(pe):
                pe.wait_ge(sigs_ready, 1)
                pe.transpose(ps_sigs, sigs[:, :], c["ident"][0:SIGS, 0:SIGS]).then_inc(sigsT_psum, 1)
                pe.wait_ge(score_w_ready, 1)
                for g in range(4):
                    for k in range(4):
                        t = 4 * g + k
                        pe.wait_ge(xn_ready, t + 1)
                        if g >= 2 and k == 0:
                            pe.wait_ge(xnT_ready, g - 1)
                        last = pe.transpose(psT[:, g % 2, k, :], xn[:, t, :], c["ident"][:, :])
                    last.then_inc(xnT_psum, 1)
                for g in range(4):
                    pe.wait_ge(xnT_ready, g + 1)
                    for k in range(4):
                        last = pe.matmul(ps_scores[:, g, k, :], xnT[:, 4 * g + k, :], score_w[:, :], start=True, stop=True)
                    last.then_inc(scores_ready, 1)
                for g in range(4):
                    if g >= 2:
                        pe.wait_ge(h_ready, g - 1)
                    pe.matmul(ps_h[0:COMP, g % 2, :], cw1[:, :], xnT[:, 4 * g:4 * g + 4, :].rearrange("p k q -> p (k q)"),
                              start=True, stop=True).then_inc(h_psum, 1)
                for g in range(4):
                    for k in range(4):
                        t = 4 * g + k
                        if k == 0:
                            pe.wait_ge(hot_ready, t // 8 + 1)
                            if g >= 2:
                                pe.wait_ge(hotT_ready, g - 1)
                        last = pe.transpose(psT[0:SIGS, g % 2, k, :], tile_hot[:, t, :], c["ident"][:, :])
                    last.then_inc(hotT_psum, 1)
                pe.wait_ge(h_ready, 4)
                pe.wait_ge(hotT_ready, 3)
                for t in range(TILES):
                    last = pe.matmul(ps_comp[:, t, :], hT[:, t, :], cw2[:, :], start=True, stop=True)
                last.then_inc(comp_psum, 1)
                for g in range(8):
                    pe.wait_ge(hotT_ready, g // 2 + 1)
                    if g >= 6:
                        pe.wait_ge(par_ready, g - 5)
                    for k in range(2):
                        last = pe.matmul(ps_par[:, g % 6, k, :], tile_hotT[:, 2 * g + k, :], table[:, :], start=True, stop=True)
                    last.then_inc(par_psum, 1)

        clear_semaphores(nc, own_sems)


def causal_phase(nc, name, x, consts, w):
    c = consts
    scale = float(D) ** -0.5
    with ExitStack() as ctx:
        own_sems = []

        def sb(n, shape, dt=F32):
            return ctx.enter_context(nc.sbuf_tensor(f"{name}_{n}", shape, dt))

        def ps(n, shape, dt=F32):
            return ctx.enter_context(nc.psum_tensor(f"{name}_{n}", shape, dt))

        def sem(n):
            own_sems.append(ctx.enter_context(nc.semaphore(f"{name}_{n}")))
            return own_sems[-1]

        T = S // P
        w_kqv, b_kqv = sb("w_kqv", [P, 3, D]), sb("b_kqv", [P, 3, D])
        w_p, b_p = sb("w_p", [P, D]), sb("b_p", [P, D])
        cos, sin = sb("cos", [P, T, D // 2]), sb("sin", [P, T, D // 2])
        xn = sb("xn", [P, TILES, D])
        xnT = sb("xnT", [P, TILES, P])
        stats, mv = sb("stats", [P, TILES, 6]), sb("mv", [P, TILES, 2])
        rstd, newton = sb("rstd", [P, TILES]), sb("newton", [P, 5, TILES])
        kqv = sb("kqv", [P, TILES, 3, D])
        half_a, half_b = sb("half_a", [P, 2, T, 2, D // 2]), sb("half_b", [P, 2, T, 2, D // 2])
        half_c, half_d = sb("half_c", [P, 2, T, 2, D // 2]), sb("half_d", [P, 2, T, 2, D // 2])
        turned = sb("turned", [P, TILES, 2, D])
        kT, qT = sb("kT", [P, TILES, P]), sb("qT", [P, TILES, P])
        size = sb("size", [P, 2, S])
        tail = sb("tail", [P, 2, S])
        soft = sb("soft", [P, 2, S])
        over = sb("over", [P, 2, S])
        weiT = sb("weiT", [P, T, S])
        outT = sb("outT", [P, 2, S])

        ps_kqv = ps("ps_kqv", [P, 2, 512])
        psT = ps("psT", [P, 2, 4, P])
        ps_wei = ps("ps_wei", [P, 2, S])
        ps_out = ps("ps_out", [P, S])
        ps_y = ps("ps_y", [P, T, D])

        weights_in, chain = sem("weights_in"), sem("chain")
        var_ready, std_ready = sem("var_ready"), sem("std_ready")
        xn_ready, xT_psum, xT_ready = sem("xn_ready"), sem("xT_psum"), sem("xT_ready")
        kqv_psum, kqv_ready = sem("kqv_psum"), sem("kqv_ready")
        parts_ready, turned_ready = sem("parts_ready"), sem("turned_ready")
        kq_psum, kq_ready = sem("kq_psum"), sem("kq_ready")
        wei_psum, size_ready, tail_ready, soft_ready = sem("wei_psum"), sem("size_ready"), sem("tail_ready"), sem("soft_ready")
        over_ready, wei_ready, wei_masked = sem("over_ready"), sem("wei_ready"), sem("wei_masked")
        out_psum, out_ready, y_psum, y_added = sem("out_psum"), sem("out_ready"), sem("y_psum"), sem("y_added")

        with nc.Block() as block:

            @block.sync
            def _(sp):
                loads = [(w_kqv[:, n, :], w[k]) for n, k in enumerate(("Wk", "Wq", "Wv"))]
                loads += [(b_kqv[:, n, :], w[k].unsqueeze(0).partition_broadcast(P)) for n, k in enumerate(("bk", "bq", "bv"))]
                loads += [(w_p[:, :], w["Wp"]), (b_p[:, :], w["bp"].unsqueeze(0).partition_broadcast(P)),
                          (cos[:, :, :], w["cos"].rearrange("(t p) f -> p t f", p=P)),
                          (sin[:, :, :], w["sin"].rearrange("(t p) f -> p t f", p=P))]
                assert len(loads) == CAUSAL_LOADS
                for dst, src in loads:
                    sp.dma_start(dst, src).then_inc(weights_in, 16)

            @block.scalar
            def _(act):
                act.wait_ge(var_ready, 1)
                nc.scalar.activation(newton[:, 0, :], mv[:, :, 1], ACT.Sqrt, bias=c["eps5"][:, 0:1]).then_inc(std_ready, 1)
                for g in range(4):
                    act.wait_ge(xT_psum, g + 1)
                    nc.scalar.copy(xnT[:, 4 * g:4 * g + 4, :], psT[:, g % 2, :, :]).then_inc(xT_ready, 1)
                for b in range(B):
                    for n, dst in enumerate((kT, qT)):
                        act.wait_ge(kq_psum, 2 * b + n + 1)
                        nc.scalar.copy(dst[:, T * b:T * b + T, :], psT[:, n, :, :]).then_inc(kq_ready, 1)
                for b in range(B):
                    for j in range(T):
                        k, u = T * b + j, j % 2
                        cols = slice(P * j, S)
                        act.wait_ge(wei_psum, k + 1)
                        if k >= 2:
                            act.wait_ge(wei_ready, k - 1)
                        nc.scalar.activation(size[:, u, cols], ps_wei[:, u, cols], ACT.Abs, scale=scale).then_inc(size_ready, 1)
                        act.wait_ge(size_ready, k + 1)
                        nc.scalar.activation(tail[:, u, cols], size[:, u, cols], ACT.Exp, scale=-1.0).then_inc(tail_ready, 1)
                        act.wait_ge(tail_ready, k + 1)
                        nc.scalar.activation(soft[:, u, cols], tail[:, u, cols], ACT.Ln, bias=1.0).then_inc(soft_ready, 1)
                    act.wait_ge(out_psum, b + 1)
                    if b >= 2:
                        act.wait_ge(y_psum, b - 1)
                    nc.scalar.copy(outT[:, b % 2, :], ps_out[:, :]).then_inc(out_ready, 1)

            @block.gpsimd
            def _(pool):
                for b in range(B):
                    pool.wait_ge(kqv_ready, T * b + T)
                    if b >= 2:
                        pool.wait_ge(turned_ready, b - 1)
                    pair = kqv[:, T * b:T * b + T, 0:2, :].rearrange("p t n (f two) -> p t n f two", two=2)
                    wide = (P, T, 2, D // 2)
                    cs, sn = cos[:, :, :].unsqueeze(2).broadcast_to(wide), sin[:, :, :].unsqueeze(2).broadcast_to(wide)
                    pool.tensor_tensor(half_c[:, b % 2, :, :, :], pair[:, :, :, :, 0], sn, ALU.mult)
                    pool.tensor_tensor(half_d[:, b % 2, :, :, :], pair[:, :, :, :, 1], cs, ALU.mult).then_inc(parts_ready, 1)
                for b in range(B):
                    for j in range(T):
                        pool.wait_ge(wei_ready, T * b + j + 1)
                        block_ = weiT[:, j, P * j:P * j + P]
                        pool.affine_select(block_, block_, compare_op=ALU.is_ge, fill=0.0, base=0,
                                           pattern=[[1, P]], channel_multiplier=-1).then_inc(wei_masked, 1)

            @block.vector
            def _(dve):
                done = chain_on(dve, chain)

                def add_y(b):
                    dve.wait_ge(y_psum, b + 1)
                    xb = x[:, T * b:T * b + T, :]
                    dve.tensor_tensor(xb, ps_y[:, :, :], xb, ALU.add).then_inc(y_added, 1)
                    dve.wait_ge(y_added, b + 1)
                    done(dve.tensor_tensor(xb, xb, b_p[:, :].unsqueeze(1).broadcast_to((P, T, D)), ALU.add))

                normalise_tokens(dve, done, x, (stats, mv, rstd, newton), 1e-5, std_ready, var_ready)
                for t in range(TILES):
                    dve.tensor_scalar(xn[:, t, :], x[:, t, :], mv[:, t, 0:1], newton[:, 4, t:t + 1],
                                      ALU.subtract, ALU.mult).then_inc(xn_ready, 1)
                dve.wait_ge(weights_in, 16 * CAUSAL_LOADS)
                for b in range(B):
                    for t in range(T * b, T * b + T):
                        dve.wait_ge(kqv_psum, t + 1)
                        dve.tensor_tensor(kqv[:, t, :, :], ps_kqv[:, t % 2, 0:3 * D].rearrange("p (n d) -> p n d", n=3),
                                          b_kqv[:, :, :], ALU.add).then_inc(kqv_ready, 1)
                    dve.wait_ge(kqv_ready, T * b + T)
                    pair = kqv[:, T * b:T * b + T, 0:2, :].rearrange("p t n (f two) -> p t n f two", two=2)
                    out = turned[:, T * b:T * b + T, :, :].rearrange("p t n (f two) -> p t n f two", two=2)
                    wide = (P, T, 2, D // 2)
                    cs, sn = cos[:, :, :].unsqueeze(2).broadcast_to(wide), sin[:, :, :].unsqueeze(2).broadcast_to(wide)
                    dve.tensor_tensor(half_a[:, b % 2, :, :, :], pair[:, :, :, :, 0], cs, ALU.mult)
                    done(dve.tensor_tensor(half_b[:, b % 2, :, :, :], pair[:, :, :, :, 1], sn, ALU.mult))
                    dve.tensor_tensor(out[:, :, :, :, 0], half_a[:, b % 2, :, :, :], half_b[:, b % 2, :, :, :], ALU.add)
                    dve.wait_ge(parts_ready, b + 1)
                    dve.tensor_tensor(out[:, :, :, :, 1], half_d[:, b % 2, :, :, :], half_c[:, b % 2, :, :, :], ALU.subtract)\
                        .then_inc(turned_ready, 1)
                for b in range(B):
                    for j in range(T):
                        k, u = T * b + j, j % 2
                        cols = slice(P * j, S)
                        dve.wait_ge(size_ready, k + 1)
                        dve.tensor_scalar(over[:, u, cols], ps_wei[:, u, cols], scale, 0.0, ALU.mult, ALU.max).then_inc(over_ready, 1)
                        dve.wait_ge(over_ready, k + 1)
                        dve.wait_ge(soft_ready, k + 1)
                        if b:
                            dve.wait_ge(out_psum, b)
                        dve.tensor_tensor(weiT[:, j, cols], over[:, u, cols], soft[:, u, cols], ALU.add).then_inc(wei_ready, 1)
                    if b:
                        add_y(b - 1)
                add_y(B - 1)

            @block.tensor
            def _(pe):
                for g in range(4):
                    for k in range(4):
                        t = 4 * g + k
                        pe.wait_ge(xn_ready, t + 1)
                        if g >= 2 and k == 0:
                            pe.wait_ge(xT_ready, g - 1)
                        last = pe.transpose(psT[:, g % 2, k, :], xn[:, t, :], c["ident"][:, :])
                    last.then_inc(xT_psum, 1)
                pe.wait_ge(weights_in, 16 * CAUSAL_LOADS)

                def turn(b):
                    pe.wait_ge(turned_ready, b + 1)
                    for n in range(2):
                        pe.wait_ge(*((xT_ready, 4) if b == 0 else (kq_ready, 2 * b - 1 + n)))
                        for k in range(T):
                            last = pe.transpose(psT[:, n, k, :], turned[:, T * b + k, n, :], c["ident"][:, :])
                        last.then_inc(kq_psum, 1)

                for t in range(TILES):
                    pe.wait_ge(xT_ready, t // 4 + 1)
                    if t >= 2:
                        pe.wait_ge(kqv_ready, t - 1)
                    pe.matmul(ps_kqv[:, t % 2, 0:3 * D], xnT[:, t, :], w_kqv[:, :, :].rearrange("p n d -> p (n d)"),
                              start=True, stop=True).then_inc(kqv_psum, 1)
                    if t % T == T - 1 and t // T:
                        turn(t // T - 1)
                turn(B - 1)

                def project(b):
                    pe.wait_ge(out_ready, b + 1)
                    if b:
                        pe.wait_ge(y_added, b)
                    for k in range(T):
                        last = pe.matmul(ps_y[:, k, :], outT[:, b % 2, k * P:(k + 1) * P], w_p[:, :], start=True, stop=True)
                    last.then_inc(y_psum, 1)

                for b in range(B):
                    for j in range(T):
                        k = T * b + j
                        pe.wait_ge(kq_ready, 2 * b + 2)
                        if k >= 2:
                            pe.wait_ge(over_ready, k - 1)
                        pe.matmul(ps_wei[:, j % 2, P * j:S], qT[:, k, :],
                                  kT[:, k:T * b + T, :].rearrange("p t q -> p (t q)"), start=True, stop=True).then_inc(wei_psum, 1)
                    if b:
                        project(b - 1)
                    for j in range(T):
                        pe.wait_ge(wei_masked, T * b + j + 1)
                        if b and j == 0:
                            pe.wait_ge(out_ready, b)
                        last = pe.matmul(ps_out[:, P * j:S], kqv[:, T * b + j, 2, :], weiT[:, j, P * j:S],
                                         start=(j == 0), stop=(j == T - 1), skip_group_check=True)
                    last.then_inc(out_psum, 1)
                project(B - 1)

        clear_semaphores(nc, own_sems)


def network(nc, inputs, out, tables):
    def weights(prefix, *more):
        names = {n[len(prefix):]: a for n, a in inputs.items() if n.startswith(prefix)}
        return {**names, **{n: tables[n] for n in more}}

    sorted_tokens = nc.dram_tensor("sorted_tokens", (SLOTS * P, D), F32).ap()
    sorted_results = nc.dram_tensor("sorted_results", (SLOTS * P, D), F32).ap()
    with ExitStack() as ctx:
        x = ctx.enter_context(nc.sbuf_tensor("x_tokens", [P, TILES, D], F32))
        c = constants_phase(nc, ctx, x, inputs["L0_attn_hidden_states"], sorted_tokens)
        ffn_phase(nc, ctx, "l0f0", x, c, weights("L0_ffn_"), (sorted_tokens, sorted_results))
        relative_phase(nc, ctx, "l0a", x, c, weights("L0_attn_", "own_head", "far_mask", "block_hot"), attention_dram(nc))
        ffn_phase(nc, ctx, "l0f1", x, c, weights("L0_ffn_"), (sorted_tokens, sorted_results))
        spline_phase(nc, "l1f0", x, c, weights("L1_ffn_"))
        causal_phase(nc, "l1a", x, c, weights("L1_attn_", "cos", "sin"))
        spline_phase(nc, "l1f1", x, c, weights("L1_ffn_"))
        x_out = ctx.enter_context(nc.semaphore("x_out"))
        with nc.Block() as block:

            @block.sync
            def _(sp):
                sp.dma_start(out.rearrange("b (t p) d -> p (b t) d", p=P), x[:, :, :]).then_inc(x_out, 16)
                sp.wait_ge(x_out, 16)


def kernel(**inputs):
    import concourse.bacc as _bacc
    from concourse.bass_utils import run_bass_kernel_spmd as _run

    nc = _bacc.Bacc("TRN2", target_bir_lowering=False, num_devices=1)
    arrays, handles = {}, {}
    for name, a in {**inputs, **host_tables()}.items():
        if name == "L0_attn_attention_mask":
            continue
        arrays[f"in_{name}"] = np.ascontiguousarray(a)
        handles[name] = nc.dram_tensor(f"in_{name}", a.shape, F32, kind="ExternalInput").ap()
    out = nc.dram_tensor("out", (B, S, D), F32, kind="ExternalOutput").ap()
    tables = {name: handles.pop(name) for name in host_tables()}
    network(nc, handles, out, tables)
    r = _run(nc, [arrays], core_ids=[0])
    return r.results[0]["out"]
```

```python
from contextlib import ExitStack

import numpy as np

import concourse.bass as bass
from concourse import mybir

F32 = mybir.dt.float32
BF16 = mybir.dt.bfloat16
I32 = mybir.dt.int32
ALU = mybir.AluOpType
ACT = mybir.ActivationFunctionType
AX = mybir.AxisListType

P = 128
B, S, D = 4, 512, 128
TILES = B * S // P
EXPERTS, FF = 8, 512
FC = FF // P
UNROLL = 6
SLOTS = -(-(TILES + EXPERTS - 1) // UNROLL) * UNROLL
ROUNDS = SLOTS // UNROLL
STORE_LAG = 3
MINE_LAG, UP_LAG, DOWN_LAG = 1, 1, 3
FFN_LOADS = 3 + EXPERTS
SLAB_W1, SLAB_W2 = 0, FF
SLAB_B2 = SLAB_W2 + FC * D
SLAB_B1 = SLAB_B2 + D
SLAB = SLAB_B1 + FC

SIGS, CLUSTERS = 64, 8
PER = SIGS // CLUSTERS
KNOTS, GRID, COMP = 8, 16, 32
SCORES = CLUSTERS + SIGS
W1_AT, B1_AT, W2_AT, B2_AT, DIR_AT = 0, 2 * GRID, 3 * GRID, 4 * GRID, 4 * GRID + 1
PARAMS = DIR_AT + D
SPLINE_LOADS = 15
CAUSAL_LOADS = 10

HEADS, DH = 16, 8
BUCKETS, MAX_REL = 32, 64
NB = S // 64
WIN = 192
GROUP = 4
GROUPS = HEADS // GROUP
T4 = S // P
QUOTA = S + 2 * 64
ROWS = 12


def bucket(d):
    mid = BUCKETS // 2
    size = mid - 1 if -mid < d < mid else abs(d)
    if size <= mid:
        return size
    f = np.float32
    far = np.ceil(np.log(f(size) / f(mid)) / np.log(f((MAX_REL - 1) / mid)) * f(mid - 1)) + f(mid)
    return int(far) * (1 if d > 0 else -1)


def clipped(v):
    return min(max(v, 0), 2 * BUCKETS - 1)


def bucket_runs():
    pair = {d: (clipped(bucket(d) + BUCKETS), clipped(BUCKETS - bucket(-d))) for d in range(1 - S, S)}
    right = max(d for d in pair if all(pair[k] == pair[1 - S] for k in range(1 - S, d + 1)))
    left = min(d for d in pair if all(pair[k] == pair[S - 1] for k in range(d, S)))
    assert left <= 64 and right >= -64
    runs = []
    for d in range(right + 1, left):
        if runs and runs[-1][2:] == pair[d]:
            runs[-1] = (runs[-1][0], d, *pair[d])
        else:
            runs.append((d, d, *pair[d]))
    return runs, left, right, pair[S - 1], pair[1 - S]


RUNS, LEFT, RIGHT, LEFT_ROWS, RIGHT_ROWS = bucket_runs()
USED = sorted({r for run in RUNS for r in run[2:]} | set(LEFT_ROWS) | set(RIGHT_ROWS))
CUT = next(n for n in range(1, len(USED)) if USED[n] != USED[n - 1] + 1)
STRETCHES = [(USED[0], 0, CUT), (USED[CUT], CUT, len(USED) - CUT)]
NP_ = len(USED)
ROW_OF = {p: n for n, p in enumerate(USED)}
PER_CHUNK = P // NP_
CHUNKS = [(h, min(PER_CHUNK, HEADS - h)) for h in range(0, HEADS, PER_CHUNK)]

PREP_LOADS = 10
PART_STORES = 8
ROW_BUFFERS = 8
EDGE_ROWS = next(a for a in range(1, HEADS * NP_) if HEADS * NP_ % a == 0 and HEADS * NP_ // a <= P)
HUGE = 3.0e38
TURN_LAG, COPY_LAG, WEIGH_LAG = 3, 4, 8
HEADS_LAG, BACK_LAG, RATE_LAG = 12, 13, 14


def host_tables():
    p = np.arange(P)
    i = np.arange(NB)
    mine = (p % NB)[:, None]
    angle = np.outer(np.arange(S, dtype=np.float32), np.arange(D // 2, dtype=np.float32))[::-1].astype(np.float64)
    return {
        "own_head": (p[:, None] // DH == np.arange(HEADS)).astype(np.float32),
        "far_mask": np.stack([mine < i - 1, mine > i + 1], 1).astype(np.float32),
        "block_hot": (mine == i).astype(np.float32),
        "cos": np.cos(angle).astype(np.float32),
        "sin": np.sin(angle).astype(np.float32),
    }


def attention_dram(nc):
    def dram(n, shape, dt=F32):
        return nc.dram_tensor(n, shape, dt).ap()

    return {
        "q": dram("stacked_q", (B, P, ROWS, S), BF16),
        "k": dram("stacked_k", (B, P, ROWS, S), BF16),
        "tab_q": dram("position_q", (B, HEADS * NP_, S)),
        "tab_k": dram("position_k", (B, HEADS * NP_, QUOTA)),
        "v": dram("values", (B, GROUPS, P, T4 * P)),
        "near": dram("near_terms", (B, P, 64, WIN)),
    }


def clear_semaphores(nc, sems):
    numbers = sorted(s.num for s in sems)
    starts = [n for n in numbers if n - 1 not in numbers]
    ends = [n + 1 for n in numbers if n + 1 not in numbers]
    with nc.Block() as block:

        @block.sync
        def _(sp):
            for first, end in zip(starts, ends):
                sp.sem_clear(range(first, end))


def constants_phase(nc, ctx, x, x_dram, xs_dram):
    def sb(n, shape, dt=F32):
        return ctx.enter_context(nc.sbuf_tensor(f"c_{n}", shape, dt))

    c = {
        "ident": sb("ident", [P, P]),
        "ones": sb("ones", [P, P]),
        "ones_b": sb("ones_b", [P, P], BF16),
        "earlier_b": sb("earlier_b", [P, P], BF16),
        "eps5": sb("eps5", [P, 1]),
        "eps7": sb("eps7", [P, 1]),
        "countdown8": sb("countdown8", [P, EXPERTS]),
        "tile_starts": sb("tile_starts", [P, TILES]),
        "earlier8": sb("earlier8", [P, EXPERTS, EXPERTS]),
        "slot_ids": sb("slot_ids", [P, SLOTS]),
        "segment_ids": sb("segment_ids", [P, KNOTS]),
    }
    x_in = ctx.enter_context(nc.semaphore("x_in"))
    filled = ctx.enter_context(nc.semaphore("filled"))
    zero_ready = ctx.enter_context(nc.semaphore("zero_ready"))
    slots_cleared = ctx.enter_context(nc.semaphore("slots_cleared"))
    shaped = ctx.enter_context(nc.semaphore("shaped"))
    with nc.sbuf_tensor("c_zeros", [P, SLOTS, D], F32) as zeros, nc.Block() as block:

        @block.sync
        def _(sp):
            sp.dma_start(x[:, :, :], x_dram.rearrange("b (t p) d -> p (b t) d", p=P)).then_inc(x_in, 16)
            sp.wait_ge(zero_ready, 1)
            sp.dma_start(xs_dram.rearrange("(s p) d -> p s d", p=P), zeros[:, :, :]).then_inc(slots_cleared, 16)
            sp.wait_ge(x_in, 16)
            sp.wait_ge(slots_cleared, 16)

        @block.vector
        def _(dve):
            dve.memset(zeros[:, :, :], 0.0).then_inc(zero_ready, 1)
            dve.memset(c["ident"][:, :], 1.0).then_inc(filled, 1)
            dve.memset(c["ones"][:, :], 1.0).then_inc(filled, 1)
            dve.memset(c["ones_b"][:, :], 1.0).then_inc(filled, 1)
            dve.memset(c["earlier_b"][:, :], 1.0).then_inc(filled, 1)
            dve.memset(c["earlier8"][:, :, :], 1.0).then_inc(filled, 1)
            dve.memset(c["eps5"][:, :], 1e-5).then_inc(filled, 1)
            dve.memset(c["eps7"][:, :], 1e-7).then_inc(filled, 1)

        @block.gpsimd
        def _(pool):
            pool.iota(c["countdown8"][:, :], [[-1, EXPERTS]], base=EXPERTS, channel_multiplier=0,
                      allow_small_or_imprecise_dtypes=True)
            pool.iota(c["tile_starts"][:, :], [[P, TILES]], base=0, channel_multiplier=0,
                      allow_small_or_imprecise_dtypes=True)
            pool.iota(c["segment_ids"][:, :], [[1, KNOTS]], base=0, channel_multiplier=0,
                      allow_small_or_imprecise_dtypes=True)
            pool.iota(c["slot_ids"][:, :], [[1, SLOTS]], base=0, channel_multiplier=0,
                      allow_small_or_imprecise_dtypes=True).then_inc(shaped, 1)
            pool.wait_ge(filled, 7)
            pool.affine_select(c["ident"][:, :], c["ident"][:, :], compare_op=ALU.is_equal, fill=0.0,
                               base=0, pattern=[[-1, P]], channel_multiplier=1)
            pool.affine_select(c["earlier_b"][:, :], c["earlier_b"][:, :], compare_op=ALU.is_gt, fill=0.0,
                               base=0, pattern=[[1, P]], channel_multiplier=-1)
            pool.affine_select(c["earlier8"][:, :, :], c["earlier8"][:, :, :], compare_op=ALU.is_gt, fill=0.0,
                               base=0, pattern=[[1, EXPERTS], [-1, EXPERTS]], channel_multiplier=0).then_inc(shaped, 1)
            pool.wait_ge(shaped, 2)
    return c


def normalise_tokens(dve, done, x, scratch, eps, std_ready, var_ready):
    stats, mv, rstd, newton = scratch
    for t in range(TILES):
        last = dve.bn_stats(stats[:, t, :], x[:, t, :])
    done(last)
    for t in range(TILES):
        last = dve.bn_aggr(mv[:, t, :], stats[:, t, :])
    last.then_inc(var_ready, 1)
    dve.wait_ge(std_ready, 1)
    done(dve.reciprocal(rstd[:, :], newton[:, 0, :]))
    done(dve.tensor_tensor(newton[:, 1, :], rstd[:, :], rstd[:, :], ALU.mult))
    done(dve.scalar_tensor_tensor(newton[:, 2, :], mv[:, :, 1], eps, newton[:, 1, :], ALU.add, ALU.mult))
    done(dve.tensor_scalar(newton[:, 3, :], newton[:, 2, :], -0.5, 1.5, ALU.mult, ALU.add))
    done(dve.tensor_tensor(newton[:, 4, :], rstd[:, :], newton[:, 3, :], ALU.mult))


def chain_on(engine, sem):
    count = [0]

    def done(instruction):
        count[0] += 1
        instruction.then_inc(sem, 1)
        engine.wait_ge(sem, count[0])

    return done


def ffn_phase(nc, kept, name, x, consts, w, scratch_dram):
    c = consts
    xs_dram, ys_dram = scratch_dram
    with ExitStack() as ctx:
        own_sems = []

        def sb(n, shape, dt=F32):
            return ctx.enter_context(nc.sbuf_tensor(f"{name}_{n}", shape, dt))

        def ps(n, shape, dt=F32):
            return ctx.enter_context(nc.psum_tensor(f"{name}_{n}", shape, dt))

        def sem(n):
            own_sems.append(ctx.enter_context(nc.semaphore(f"{name}_{n}")))
            return own_sems[-1]

        def soft_dma_sem(n):
            return kept.enter_context(nc.semaphore(f"{name}_{n}"))

        experts = sb("experts", [P, EXPERTS, SLAB])
        mine = sb("mine", [P, UNROLL, SLAB])
        b1 = sb("b1", [EXPERTS * FC, P])
        switch_w = sb("switch_w", [P, EXPERTS])
        switch_b = sb("switch_b", [P, EXPERTS])
        xn = sb("xn", [P, TILES, D])
        xnT = sb("xnT", [P, TILES, P])
        stats = sb("stats", [P, TILES, 6])
        mv = sb("mv", [P, TILES, 2])
        rstd = sb("rstd", [P, TILES])
        newton = sb("newton", [P, 5, TILES])
        logits = sb("logits", [P, TILES, EXPERTS])
        top = sb("top", [P, TILES])
        shifted = sb("shifted", [P, TILES, EXPERTS])
        exps = sb("exps", [P, TILES, EXPERTS])
        total = sb("total", [P, TILES])
        gate = sb("gate", [P, TILES])
        half_gate = sb("half_gate", [P, TILES])
        marks = sb("marks", [P, TILES, EXPERTS])
        first = sb("first", [P, TILES])
        onehot = sb("onehot", [P, TILES, EXPERTS])
        onehot_b = sb("onehot_b", [P, TILES, EXPERTS], BF16)
        over = sb("over", [P, EXPERTS, TILES])
        n_slots = sb("n_slots", [P, EXPERTS])
        before = sb("before", [P, EXPERTS, EXPERTS])
        base = sb("base", [P, EXPERTS])
        ends = sb("ends", [P, EXPERTS])
        place = sb("place", [P, TILES, EXPERTS])
        placed = sb("placed", [P, TILES, EXPERTS])
        pos = sb("pos", [P, TILES])
        pos_i = sb("pos_i", [P, TILES], I32)
        past = sb("past", [P, SLOTS, EXPERTS])
        owner = sb("owner", [P, SLOTS])
        owner_i = sb("owner_i", [P, SLOTS], I32)
        xs = sb("xs", [P, UNROLL, D])
        xsT = sb("xsT", [P, UNROLL, P])
        h = sb("h", [P, UNROLL, FC, P])
        ys = sb("ys", [P, UNROLL, D])
        yg = sb("yg", [P, TILES, D])

        psT = ps("psT", [P, 2, 4, P])
        psR = ps("psR", [P, 512])
        psU = ps("psU", [P, 2, FC, P])
        psY = ps("psY", [P, 512])
        ps_logits = psR[:, 0:TILES * EXPERTS].rearrange("p (t e) -> p t e", t=TILES)
        ys_banks = [psR[:, 0:P], psY[:, 0:P]]
        ps_rank = psR[:, 256:256 + (TILES + 1) * EXPERTS].rearrange("p (t e) -> p t e", e=EXPERTS)

        switch_in, weights_in = sem("switch_in"), sem("weights_in")
        chain = sem("chain")
        var_ready, std_ready = sem("var_ready"), sem("std_ready")
        xn_ready, xnT_psum, xnT_ready = sem("xn_ready"), sem("xnT_psum"), sem("xnT_ready")
        logits_ready, shifted_ready, exps_ready = sem("logits_ready"), sem("shifted_ready"), sem("exps_ready")
        onehot_ready, rank_ready = sem("onehot_ready"), sem("rank_ready")
        pos_ready, owner_ready = sem("pos_ready"), sem("owner_ready")
        scattered = soft_dma_sem("scattered")
        def sems(n):
            return [sem(f"{n}{j}") for j in range(UNROLL)]

        b1_psum, b1_ready = sem("b1_psum"), sem("b1_ready")
        xs_in = sems("xs_in")
        mine_in = [soft_dma_sem(f"mine_in{j}") if j % 2 else sem(f"mine_in{j}") for j in range(UNROLL)]
        xsT_psum, xsT_ready, up_ready, h_ready = sems("xsT_psum"), sems("xsT_ready"), sems("up_ready"), sems("h_ready")
        down_ready, ys_ready = sems("down_ready"), sems("ys_ready")
        ys_out = sems("ys_out")
        gathered, x_updated = [soft_dma_sem(f"gathered{g}") for g in range(TILES // 4)], sem("x_updated")

        xs_rows = xs_dram.rearrange("(s p) d -> p s d", p=P)
        ys_rows = ys_dram.rearrange("(s p) d -> p s d", p=P)

        def is_first(i):
            return isinstance(i, int) and i == 0

        def behind(i, j, lag):
            if j - lag >= UNROLL:
                return None
            if j >= lag:
                return i, j - lag
            return None if is_first(i) else (i - 1, j - lag + UNROLL)

        def rounds(engine, body, lag):
            body(0, range(UNROLL))
            with engine.Fori(1, ROUNDS) as i:
                body(i, range(UNROLL))
            body(ROUNDS - 1, range(UNROLL, UNROLL + lag))

        def load_mine(engine, i, j):
            expert = engine.value_load(owner_i[0:1, bass.ds(i * UNROLL + j, 1)], min_val=0, max_val=EXPERTS - 1)
            if not is_first(i):
                engine.wait_ge(ys_ready[j], i)
            engine.dma_start(mine[:, j, :], experts[:, bass.ds(expert, 1), :].rearrange("p a k -> p (a k)"))\
                .then_inc(mine_in[j], 16)

        with nc.Block() as block:

            @block.sync
            def _(sp):
                sp.dma_start(switch_w[:, :], w["switch_w"]).then_inc(switch_in, 16)
                sp.dma_start(switch_b[:, :], w["switch_b"].unsqueeze(0).partition_broadcast(P)).then_inc(switch_in, 16)
                loads = [
                    (b1[:, :], w["b1"].rearrange("e (k p) -> (e k) p", p=P)),
                    (experts[:, :, SLAB_W1:SLAB_W2], w["w1"].rearrange("e d f -> d e f")),
                    (experts[:, :, SLAB_B2:SLAB_B1], w["b2"].unsqueeze(0).partition_broadcast(P)),
                ]
                for dst, src in loads:
                    sp.dma_start(dst, src).then_inc(weights_in, 16)
                for e in range(EXPERTS):
                    sp.dma_start(experts[:, e, SLAB_W2:SLAB_B2].rearrange("p (k d) -> p k d", k=FC),
                                 w["w2"][e].rearrange("(k p) d -> p k d", p=P)).then_inc(weights_in, 16)
                sp.wait_ge(weights_in, FFN_LOADS * 16)
                sp.wait_ge(b1_ready, 1)
                sp.wait_ge(owner_ready, 1)
                sp.wait_ge(scattered, 16 * TILES)

                def load_tokens(i, j):
                    if not is_first(i):
                        sp.wait_ge(xsT_psum[j], i)
                    sp.dma_start(xs[:, j, :], xs_rows[:, bass.ds(i * UNROLL + j, 1), :].rearrange("p a d -> p (a d)"))\
                        .then_inc(xs_in[j], 16)

                def body(i, steps):
                    for j in steps:
                        if at := behind(i, j, 0):
                            load_tokens(*at)
                        if (at := behind(i, j, MINE_LAG)) and at[1] % 2 == 0:
                            load_mine(sp, *at)

                rounds(sp, body, MINE_LAG)

            @block.gpsimd
            def _(pool):
                pool.wait_ge(pos_ready, 1)
                for t in range(TILES):
                    pool.indirect_dma_start(
                        xs_dram[:, :], bass.IndirectOffsetOnAxis(ap=pos_i[:, t:t + 1], axis=0),
                        xn[:, t, :], None).then_inc(scattered, 16)
                pool.wait_ge(weights_in, FFN_LOADS * 16)
                pool.wait_ge(b1_ready, 1)
                pool.wait_ge(owner_ready, 1)

                def body(i, steps):
                    for j in steps:
                        if j % 2:
                            load_mine(pool, i, j)

                rounds(pool, body, 0)
                for j in range(UNROLL):
                    pool.wait_ge(ys_out[j], 16 * ROUNDS)
                for t in range(TILES):
                    pool.indirect_dma_start(
                        yg[:, t, :], None, ys_dram[:, :],
                        bass.IndirectOffsetOnAxis(ap=pos_i[:, t:t + 1], axis=0)).then_inc(gathered[t // 4], 16)

            @block.scalar
            def _(act):
                act.wait_ge(var_ready, 1)
                nc.scalar.activation(newton[:, 0, :], mv[:, :, 1], ACT.Sqrt, bias=c["eps5"][:, 0:1]).then_inc(std_ready, 1)
                for g in range(4):
                    act.wait_ge(xnT_psum, g + 1)
                    nc.scalar.copy(xnT[:, 4 * g:4 * g + 4, :], psT[:, g % 2, :, :]).then_inc(xnT_ready, 1)
                act.wait_ge(shifted_ready, 1)
                nc.scalar.activation(exps[:, :, :], shifted[:, :, :], ACT.Exp).then_inc(exps_ready, 1)

                def activate(i, j):
                    act.wait_ge(up_ready[j], i + 1)
                    for k in range(FC):
                        last = nc.scalar.activation(h[:, j, k, :], psU[:, j % 2, k, :], ACT.Gelu_apprx_tanh,
                                                    bias=mine[:, j, SLAB_B1 + k:SLAB_B1 + k + 1])
                    last.then_inc(h_ready[j], 1)

                def store(i, j):
                    act.wait_ge(ys_ready[j], i + 1)
                    act.dma_start(ys_rows[:, bass.ds(i * UNROLL + j, 1), :].rearrange("p a d -> p (a d)"), ys[:, j, :])\
                        .then_inc(ys_out[j], 16)

                def body(i, steps):
                    for j in steps:
                        if at := behind(i, j, 0):
                            activate(*at)
                        if at := behind(i, j, STORE_LAG):
                            store(*at)

                rounds(act, body, STORE_LAG)

            @block.vector
            def _(dve):
                done = chain_on(dve, chain)
                normalise_tokens(dve, done, x, (stats, mv, rstd, newton), 1e-5, std_ready, var_ready)
                for t in range(TILES):
                    dve.tensor_scalar(xn[:, t, :], x[:, t, :], mv[:, t, 0:1], newton[:, 4, t:t + 1],
                                      ALU.subtract, ALU.mult).then_inc(xn_ready, 1)
                dve.wait_ge(logits_ready, 1)
                dve.wait_ge(switch_in, 32)
                done(dve.tensor_tensor(logits[:, :, :], ps_logits,
                                       switch_b[:, :].unsqueeze(1).broadcast_to((P, TILES, EXPERTS)), ALU.add))
                done(dve.tensor_reduce(top[:, :], logits[:, :, :], AX.X, ALU.max))
                dve.tensor_tensor(shifted[:, :, :], logits[:, :, :],
                                  top[:, :].unsqueeze(2).broadcast_to((P, TILES, EXPERTS)), ALU.subtract).then_inc(shifted_ready, 1)
                dve.wait_ge(exps_ready, 1)
                done(dve.tensor_reduce(total[:, :], exps[:, :, :], AX.X, ALU.add))
                done(dve.reciprocal(gate[:, :], total[:, :]))
                rev = c["countdown8"][:, :].unsqueeze(1).broadcast_to((P, TILES, EXPERTS))
                done(dve.scalar_tensor_tensor(marks[:, :, :], exps[:, :, :], 1.0, rev, ALU.is_equal, ALU.mult))
                done(dve.tensor_reduce(first[:, :], marks[:, :, :], AX.X, ALU.max))
                firsts = first[:, :].unsqueeze(2).broadcast_to((P, TILES, EXPERTS))
                done(dve.tensor_tensor(onehot[:, :, :], rev, firsts, ALU.is_equal))
                dve.tensor_copy(onehot_b[:, :, :], onehot[:, :, :]).then_inc(onehot_ready, 1)
                dve.wait_ge(rank_ready, 1)
                done(dve.tensor_tensor(over[:, :, :], ps_rank[:, TILES, :].unsqueeze(2).broadcast_to((P, EXPERTS, TILES)),
                                       c["tile_starts"][:, :].unsqueeze(1).broadcast_to((P, EXPERTS, TILES)), ALU.is_gt))
                done(dve.tensor_reduce(n_slots[:, :], over[:, :, :], AX.X, ALU.add))
                done(dve.tensor_tensor(before[:, :, :], n_slots[:, :].unsqueeze(1).broadcast_to((P, EXPERTS, EXPERTS)),
                                       c["earlier8"][:, :, :], ALU.mult))
                done(dve.tensor_reduce(base[:, :], before[:, :, :], AX.X, ALU.add))
                done(dve.tensor_tensor(ends[:, :], base[:, :], n_slots[:, :], ALU.add))
                done(dve.scalar_tensor_tensor(place[:, :, :], base[:, :].unsqueeze(1).broadcast_to((P, TILES, EXPERTS)),
                                              float(P), ps_rank[:, 0:TILES, :], ALU.mult, ALU.add))
                done(dve.tensor_tensor(placed[:, :, :], place[:, :, :], onehot[:, :, :], ALU.mult))
                done(dve.tensor_reduce(pos[:, :], placed[:, :, :], AX.X, ALU.add))
                dve.tensor_copy(pos_i[:, :], pos[:, :]).then_inc(pos_ready, 1)
                done(dve.tensor_tensor(past[:, :, :], ends[:, :].unsqueeze(1).broadcast_to((P, SLOTS, EXPERTS)),
                                       c["slot_ids"][:, :].unsqueeze(2).broadcast_to((P, SLOTS, EXPERTS)), ALU.is_le))
                done(dve.tensor_reduce(owner[:, :], past[:, :, :], AX.X, ALU.add))
                dve.tensor_scalar(owner_i[:, :], owner[:, :], float(EXPERTS - 1), None, ALU.min).then_inc(owner_ready, 1)

                dve.wait_ge(b1_psum, 1)
                dve.tensor_copy(experts[:, :, SLAB_B1:SLAB], psU[:, 0, 0, 0:EXPERTS * FC].rearrange("p (e k) -> p e k", e=EXPERTS))\
                    .then_inc(b1_ready, 1)
                done(dve.tensor_scalar(half_gate[:, :], gate[:, :], 0.5, None, ALU.mult))

                def to_xsT(i, j):
                    dve.wait_ge(xsT_psum[j], i + 1)
                    dve.tensor_copy(xsT[:, j, :], psT[:, j % 2, 0, :]).then_inc(xsT_ready[j], 1)

                def to_ys(i, j):
                    dve.wait_ge(down_ready[j], i + 1)
                    if not is_first(i):
                        dve.wait_ge(ys_out[j], i * 16)
                    dve.tensor_tensor(ys[:, j, :], ys_banks[j % 2], mine[:, j, SLAB_B2:SLAB_B1], ALU.add).then_inc(ys_ready[j], 1)

                def body(i, steps):
                    for j in steps:
                        if at := behind(i, j, 0):
                            to_xsT(*at)
                        if at := behind(i, j, DOWN_LAG):
                            to_ys(*at)

                rounds(dve, body, DOWN_LAG)
                for t in range(TILES):
                    if t % 4 == 0:
                        dve.wait_ge(gathered[t // 4], 16 * 4)
                    last = dve.scalar_tensor_tensor(x[:, t, :], yg[:, t, :], half_gate[:, t:t + 1], x[:, t, :],
                                                    ALU.mult, ALU.add)
                last.then_inc(x_updated, 1)

            @block.tensor
            def _(pe):
                for g in range(4):
                    for k in range(4):
                        t = 4 * g + k
                        pe.wait_ge(xn_ready, t + 1)
                        if g >= 2 and k == 0:
                            pe.wait_ge(xnT_ready, g - 1)
                        last = pe.transpose(psT[:, g % 2, k, :], xn[:, t, :], c["ident"][:, :])
                    last.then_inc(xnT_psum, 1)
                pe.wait_ge(switch_in, 32)
                pe.wait_ge(xnT_ready, 4)
                for t in range(TILES):
                    last = pe.matmul(ps_logits[:, t, :], xnT[:, t, :], switch_w[:, :], start=True, stop=True)
                last.then_inc(logits_ready, 1)
                pe.wait_ge(onehot_ready, 1)
                pe.matmul(ps_rank[:, 0:TILES, :], c["earlier_b"][:, :], onehot_b[:, :, :], start=True, stop=False,
                          skip_group_check=True)
                for t in range(TILES):
                    n = TILES - t
                    last = pe.matmul(ps_rank[:, t + 1:TILES + 1, :], c["ones_b"][:, :],
                                     onehot_b[:, t:t + 1, :].broadcast_to((P, n, EXPERTS)),
                                     start=False, stop=(t == TILES - 1), skip_group_check=True)
                last.then_inc(rank_ready, 1)
                pe.wait_ge(weights_in, FFN_LOADS * 16)
                pe.transpose(psU[:, 0, 0, 0:EXPERTS * FC], b1[:, :], c["ident"][0:EXPERTS * FC, 0:EXPERTS * FC]).then_inc(b1_psum, 1)
                pe.wait_ge(b1_ready, 1)

                def turn(i, j):
                    pe.wait_ge(xs_in[j], i * 16 + 16)
                    pe.transpose(psT[:, j % 2, 0, :], xs[:, j, :], c["ident"][:, :]).then_inc(xsT_psum[j], 1)

                def up(i, j):
                    pe.wait_ge(xsT_ready[j], i + 1)
                    pe.wait_ge(mine_in[j], i * 16 + 16)
                    for k in range(FC):
                        last = pe.matmul(psU[:, j % 2, k, :], mine[:, j, SLAB_W1 + k * P:SLAB_W1 + (k + 1) * P], xsT[:, j, :],
                                         start=True, stop=True)
                    last.then_inc(up_ready[j], 1)

                def down(i, j):
                    pe.wait_ge(h_ready[j], i + 1)
                    if not (is_first(i) and j < 2):
                        pe.wait_ge(ys_ready[(j - 2) % UNROLL], i + (1 if j >= 2 else 0))
                    for k in range(FC):
                        last = pe.matmul(ys_banks[j % 2], h[:, j, k, :], mine[:, j, SLAB_W2 + k * D:SLAB_W2 + (k + 1) * D],
                                         start=(k == 0), stop=(k == FC - 1))
                    last.then_inc(down_ready[j], 1)

                def body(i, steps):
                    for j in steps:
                        if at := behind(i, j, DOWN_LAG):
                            down(*at)
                        if at := behind(i, j, UP_LAG):
                            up(*at)
                        if at := behind(i, j, 0):
                            turn(*at)

                rounds(pe, body, DOWN_LAG)

        clear_semaphores(nc, own_sems)


def near_layout(nc, kept, ctx, name, dram):
    PART = 16
    PARTS = 64 // PART

    def sb(n, shape):
        return ctx.enter_context(nc.sbuf_tensor(f"{name}_{n}", shape, F32))

    rows_q, rows_k, near = sb("rows_q", [P, NP_ * 64]), sb("rows_k", [P, NP_ * WIN]), sb("near", [P, 2 * PART * WIN])
    rows_in, rows_free, near_steps = (ctx.enter_context(nc.semaphore(f"{name}_{n}"))
                                      for n in ("rows_in", "rows_free", "near_steps"))
    near_out = [kept.enter_context(nc.semaphore(f"{name}_near_out{k}")) for k in range(2)]

    def load_rows(sp, b):
        for g in range(NB):
            dst = bass.AP(rows_q[:, :].tensor, g * NP_ * 64, [(NB * NP_ * 64, HEADS), (64, NP_), (1, 64)])
            src = bass.AP(dram["tab_q"].tensor, b * (HEADS * NP_ * S) + g * 64, [(NP_ * S, HEADS), (S, NP_), (1, 64)])
            sp.dma_start(dst, src).then_inc(rows_in, 16)
            dst = bass.AP(rows_k[:, :].tensor, g * NP_ * WIN, [(NB * NP_ * WIN, HEADS), (WIN, NP_), (1, WIN)])
            src = bass.AP(dram["tab_k"].tensor, b * (HEADS * NP_ * QUOTA) + g * 64,
                          [(NP_ * QUOTA, HEADS), (QUOTA, NP_), (1, WIN)])
            sp.dma_start(dst, src).then_inc(rows_in, 16)

    NEAR_STORES = 16 * PARTS // 2

    def view(what, offset, *dims):
        t = what[:, :].tensor
        return bass.AP(t, offset, [(t.shape[1], P), *dims])

    def lay_out(pool, b, first):
        pool.wait_ge(rows_in, b * (32 * NB) + 32 * NB)
        for part in range(PARTS):
            q0 = PART * part
            buffer = (part % 2) * PART * WIN
            if not (first and part < 2):
                pool.wait_ge(near_out[part % 2], b * NEAR_STORES + 16 * (part // 2))

            def far(rows, c0, c1):
                rq, rk = (ROW_OF[r] for r in rows)
                return pool.tensor_tensor(
                    view(near, buffer + c0, (WIN, PART), (1, c1 - c0)), view(rows_q, rq * 64 + q0, (1, PART), (0, c1 - c0)),
                    view(rows_k, rk * WIN + c0, (0, PART), (1, c1 - c0)), ALU.add)

            far(LEFT_ROWS, 0, q0 + PART + 64 - LEFT)
            far(RIGHT_ROWS, q0 + 64 - RIGHT, WIN).then_inc(near_steps, 1)
            pool.wait_ge(near_steps, b * (2 * PARTS) + (2 * part + 1))
            for d0, d1, pq, pk in RUNS:
                at, width = q0 + 64 - d1, d1 - d0 + 1
                last = pool.tensor_tensor(
                    view(near, buffer + at, (WIN + 1, PART), (1, width)), view(rows_q, ROW_OF[pq] * 64 + q0, (1, PART), (0, width)),
                    view(rows_k, ROW_OF[pk] * WIN + at, (1, PART), (1, width)), ALU.add)
            last.then_inc(near_steps, 1)
            pool.wait_ge(near_steps, b * (2 * PARTS) + (2 * part + 2))
            dst = bass.AP(dram["near"].tensor, b * (P * 64 * WIN) + q0 * WIN, [(64 * WIN, P), (1, PART * WIN)])
            pool.dma_start(dst, near[:, buffer:buffer + PART * WIN]).then_inc(near_out[part % 2], 16)
        pool.engine_nop().then_inc(rows_free, 1)

    return load_rows, lay_out, rows_free, near_out, [rows_in, rows_free, near_steps]


def relative_prepare(nc, name, x, xn, consts, w, dram, layout):
    c = consts
    inv = 1.0 / float(np.sqrt(np.float32(DH * 3)))
    with ExitStack() as ctx:
        own_sems = []

        def sb(n, shape, dt=F32):
            return ctx.enter_context(nc.sbuf_tensor(f"{name}_{n}", shape, dt))

        def ps(n, shape, dt=F32):
            return ctx.enter_context(nc.psum_tensor(f"{name}_{n}", shape, dt))

        def sem(n):
            own_sems.append(ctx.enter_context(nc.semaphore(f"{name}_{n}")))
            return own_sems[-1]

        wq, wk, wv = sb("wq", [P, D]), sb("wk", [P, D]), sb("wv", [P, D])
        bq, bk, bv = sb("bq", [P, 1]), sb("bk", [P, 1]), sb("bv", [P, D])
        rel = sb("rel", [2 * BUCKETS, D])
        relT = sb("relT", [P, 2 * BUCKETS])
        pos, pos_s = sb("pos", [P, 2 * BUCKETS]), sb("pos_s", [P, 2 * BUCKETS])
        own_head = sb("own_head", [P, HEADS])
        far_mask = sb("far_mask", [P, 2, NB])
        block_hot = sb("block_hot", [P, NB])
        hot_rows = sb("hot_rows", [P, S], BF16)
        tab_w = sb("tab_w", [P, 2, HEADS, NP_])
        far_w = sb("far_w", [P, 4, HEADS, NB])
        xnT = sb("xnT", [P, TILES, P])
        stats, mv = sb("stats", [P, TILES, 6]), sb("mv", [P, TILES, 2])
        rstd, newton = sb("rstd", [P, TILES]), sb("newton", [P, 5, TILES])
        whole = sb("whole", [P, 2, 4, S])
        far_l, far_r = sb("far_l", [P, 2, S]), sb("far_r", [P, 2, S])
        rest = sb("rest", [P, 4, S])
        parts = sb("parts", [P, 2, 4, 3, S], BF16)
        rows = sb("rows", [P, ROW_BUFFERS, S])
        v_pad = sb("v_pad", [P, 2 * T4, HEADS, 32])
        edge = sb("edge", [P, 64])

        psT = ps("psT", [P, 2, 4, P])
        ps_qk = ps("ps_qk", [P, 2, S])
        ps_far = ps("ps_far", [P, 2, S])
        ps_tab = ps("ps_tab", [P, 2, S])

        weights_in, chain = sem("weights_in"), sem("chain")
        rel_ready, relT_psum, relT_ready, pos_psum, shapes_ready = (
            sem("rel_ready"), sem("relT_psum"), sem("relT_ready"), sem("pos_psum"), sem("shapes_ready"))
        var_ready, std_ready = sem("var_ready"), sem("std_ready")
        xn_ready, xT_psum, xT_ready = sem("xn_ready"), sem("xT_psum"), sem("xT_ready")
        qk_psum, qk_ready, far_psum, far_ready = sem("qk_psum"), sem("qk_ready"), sem("far_psum"), sem("far_ready")
        hi_ready, rest_ready, mid_ready, lo_ready = sem("hi_ready"), sem("rest_ready"), sem("mid_ready"), sem("lo_ready")
        tab_psum, rows_ready = sem("tab_psum"), sem("rows_ready")
        rows_out = [sem(f"rows_out{k}") for k in range(ROW_BUFFERS)]
        v_psum, v_ready = sem("v_psum"), sem("v_ready")
        parts_out = [sem(f"parts_out{k}") for k in range(2)]
        v_out = [sem(f"v_out{k}") for k in range(2)]
        hot_out, edge_out = sem("hot_out"), sem("edge_out")

        load_rows, lay_out = layout[:2]
        n_rows = 2 * len(CHUNKS)

        with nc.Block() as block:

            @block.sync
            def _(sp):
                loads = [
                    (wq[:, :], w["Wq"]), (wk[:, :], w["Wk"]), (wv[:, :], w["Wv"]),
                    (bq[:, :], w["bq"].unsqueeze(1)), (bk[:, :], w["bk"].unsqueeze(1)),
                    (bv[:, :], w["bv"].unsqueeze(0).partition_broadcast(P)),
                    (rel[:, :], w["rel_embeddings"]), (own_head[:, :], w["own_head"]),
                    (far_mask[:, :, :], w["far_mask"]), (block_hot[:, :], w["block_hot"]),
                ]
                assert len(loads) == PREP_LOADS
                for dst, src in loads:
                    sp.dma_start(dst, src).then_inc(weights_in, 16)
                sp.wait_ge(shapes_ready, 1)
                for b in range(B):
                    for e in (0, 64 + S):
                        sp.dma_start(dram["tab_k"][b, :, e:e + 64].rearrange("(p a) k -> p a k", a=EDGE_ROWS),
                                     edge[0:HEADS * NP_ // EDGE_ROWS, :].unsqueeze(1).broadcast_to(
                                         (HEADS * NP_ // EDGE_ROWS, EDGE_ROWS, 64))).then_inc(edge_out, 16)
                    for dst, r in ((dram["k"], 6), (dram["q"], 9)):
                        sp.dma_start(dst[b, :, r:r + 3, :], hot_rows[:, :].unsqueeze(1).broadcast_to((P, 3, S))).then_inc(hot_out, 16)
                sp.wait_ge(edge_out, 16 * 2 * B)
                sp.wait_ge(hot_out, 16 * 2 * B)
                for b in range(B):
                    u = b % 2
                    for k in range(n_rows):
                        side, (h0, n) = k // len(CHUNKS), CHUNKS[k % len(CHUNKS)]
                        m = n_rows * b + k
                        sp.wait_ge(rows_ready, m + 1)
                        dst = dram["tab_k"][b, h0 * NP_:(h0 + n) * NP_, 64:64 + S] if side else \
                            dram["tab_q"][b, h0 * NP_:(h0 + n) * NP_, :]
                        sp.dma_start(dst, rows[0:n * NP_, m % ROW_BUFFERS, :]).then_inc(rows_out[m % ROW_BUFFERS], 16)
                    if b == 0:
                        for k in range(ROW_BUFFERS):
                            sp.wait_ge(rows_out[k], 16 * len(range(k, n_rows, ROW_BUFFERS)))
                        load_rows(sp, 0)
                    sp.wait_ge(v_ready, b + 1)
                    sp.dma_start(dram["v"][b].rearrange("g p (t k) -> p t g k", t=T4),
                                 v_pad[:, T4 * u:T4 * u + T4, :, :].rearrange("p t (g j) k -> p t g (j k)", g=GROUPS)).then_inc(v_out[u], 16)
                    sp.wait_ge(hi_ready, 4 * b + 4)
                    sp.wait_ge(mid_ready, 4 * b + 4)
                    sp.wait_ge(lo_ready, 4 * b + 4)
                    for dst, r, n, first, rows_n in (("q", 0, 0, 0, 3), ("q", 3, 0, 1, 2), ("q", 5, 0, 2, 1), ("q", 6, 2, None, 3),
                                                     ("k", 0, 1, None, 3), ("k", 3, 1, None, 2), ("k", 5, 1, 0, 1), ("k", 9, 3, None, 3)):
                        src = parts[:, u, n, 0:rows_n, :] if first is None else \
                            parts[:, u, n, first:first + 1, :].broadcast_to((P, rows_n, S))
                        sp.dma_start(dram[dst][b, :, r:r + rows_n, :], src).then_inc(parts_out[u], 16)
                for u in range(2):
                    sp.wait_ge(parts_out[u], 16 * PART_STORES * (B // 2))
                for k in range(ROW_BUFFERS):
                    sp.wait_ge(rows_out[k], 16 * len(range(k, n_rows * B, ROW_BUFFERS)))
                for u in range(2):
                    sp.wait_ge(v_out[u], 16 * (B // 2))

            @block.gpsimd
            def _(pool):
                lay_out(pool, 0, True)

            @block.scalar
            def _(act):
                act.wait_ge(var_ready, 1)
                nc.scalar.activation(newton[:, 0, :], mv[:, :, 1], ACT.Sqrt, bias=c["eps5"][:, 0:1]).then_inc(std_ready, 1)
                for g in range(4):
                    act.wait_ge(xT_psum, g + 1)
                    nc.scalar.copy(xnT[:, 4 * g:4 * g + 4, :], psT[:, g % 2, :, :]).then_inc(xT_ready, 1)

                def high(b, ns):
                    for n in ns:
                        if n < 2:
                            act.wait_ge(qk_ready, 2 * b + n + 1)
                        else:
                            act.wait_ge(far_ready, 2 * b + n - 1)
                        if b >= 2:
                            act.wait_ge(parts_out[b % 2], 16 * PART_STORES * (b // 2))
                        nc.scalar.copy(parts[:, b % 2, n, 0, :], whole[:, b % 2, n, :]).then_inc(hi_ready, 1)

                def middle(b):
                    for n in range(4):
                        act.wait_ge(rest_ready, 4 * b + n + 1)
                        nc.scalar.copy(parts[:, b % 2, n, 1, :], rest[:, n, :]).then_inc(mid_ready, 1)

                def copy_rows(b, ks):
                    for k in ks:
                        m = n_rows * b + k
                        n = CHUNKS[k % len(CHUNKS)][1]
                        act.wait_ge(tab_psum, m + 1)
                        if m >= ROW_BUFFERS:
                            act.wait_ge(rows_out[m % ROW_BUFFERS], 16 * (m // ROW_BUFFERS))
                        nc.scalar.copy(rows[0:n * NP_, m % ROW_BUFFERS, :], ps_tab[0:n * NP_, m % 2, :]).then_inc(rows_ready, 1)

                high(0, range(4))
                middle(0)
                for b in range(B):
                    copy_rows(b, range(len(CHUNKS)))
                    if b + 1 < B:
                        high(b + 1, (0, 1))
                        copy_rows(b, range(len(CHUNKS), len(CHUNKS) + 2))
                        high(b + 1, (2, 3))
                        copy_rows(b, range(len(CHUNKS) + 2, n_rows - 2))
                        middle(b + 1)
                        copy_rows(b, range(n_rows - 2, n_rows))
                    else:
                        copy_rows(b, range(len(CHUNKS), n_rows))

            @block.vector
            def _(dve):
                done = chain_on(dve, chain)
                dve.memset(edge[:, :], 0.0)
                dve.memset(v_pad[:, :, :, DH + 1:], 0.0)
                dve.memset(v_pad[:, :, :, DH:DH + 1], 1.0)
                dve.wait_ge(weights_in, 16 * PREP_LOADS)
                done(dve.tensor_copy(hot_rows[:, :].rearrange("p (n k) -> p n k", n=NB),
                                     block_hot[:, :].unsqueeze(2).broadcast_to((P, NB, 64))))
                dve.wait_ge(relT_psum, 1)
                dve.tensor_copy(relT[:, :], psT[:, 0, 0, 0:2 * BUCKETS]).then_inc(relT_ready, 1)
                dve.wait_ge(pos_psum, 1)
                done(dve.tensor_scalar(pos[:, :], psT[:, 1, 0, 0:2 * BUCKETS], bk[:, 0:1], None, ALU.add))
                done(dve.tensor_scalar(pos_s[:, :], pos[:, :], inv, None, ALU.mult))
                for side, src in enumerate((pos, pos_s)):
                    for p0, n0, n in STRETCHES:
                        wide = (P, HEADS, n)
                        dve.tensor_tensor(tab_w[:, side, :, n0:n0 + n], src[:, p0:p0 + n].unsqueeze(1).broadcast_to(wide),
                                          own_head[:, :].unsqueeze(2).broadcast_to(wide), ALU.mult)
                    for far, row in enumerate((LEFT_ROWS[side], RIGHT_ROWS[side])):
                        last = dve.tensor_scalar(far_w[:, 2 * side + far, :, :], own_head[:, :].unsqueeze(2).broadcast_to((P, HEADS, NB)),
                                                 src[:, row:row + 1], None, ALU.mult)
                last.then_inc(shapes_ready, 1)
                normalise_tokens(dve, done, x, (stats, mv, rstd, newton), 1e-5, std_ready, var_ready)
                for t in range(TILES):
                    dve.tensor_scalar(xn[:, t, :], x[:, t, :], mv[:, t, 0:1], newton[:, 4, t:t + 1],
                                      ALU.subtract, ALU.mult).then_inc(xn_ready, 1)
                for b in range(B):
                    u = b % 2
                    dve.wait_ge(qk_psum, b + 1)
                    if b >= 2:
                        dve.wait_ge(hi_ready, 4 * (b - 1))
                        dve.wait_ge(tab_psum, n_rows * (b - 1))
                    dve.tensor_scalar(whole[:, u, 0, :], ps_qk[:, 0, :], bq[:, 0:1], inv, ALU.add, ALU.mult).then_inc(qk_ready, 1)
                    dve.tensor_scalar(whole[:, u, 1, :], ps_qk[:, 1, :], bk[:, 0:1], None, ALU.add).then_inc(qk_ready, 1)
                    for n in range(2):
                        dve.wait_ge(far_psum, 2 * b + n + 1)
                        for far, dst in enumerate((far_l, far_r)):
                            last = dve.tensor_tensor(dst[:, n, :].rearrange("p (i k) -> p i k", i=NB),
                                                     ps_far[:, far, :].rearrange("p (i k) -> p i k", i=NB),
                                                     far_mask[:, far if n == 0 else 1 - far, :].unsqueeze(2).broadcast_to((P, NB, 64)), ALU.mult)
                        done(last)
                        dve.tensor_tensor(whole[:, u, 2 + n, :], far_l[:, n, :], far_r[:, n, :], ALU.add).then_inc(far_ready, 1)
                    dve.wait_ge(v_psum, b + 1)
                    if b >= 2:
                        dve.wait_ge(v_out[u], 16 * (b // 2))
                    dve.tensor_tensor(v_pad[:, T4 * u:T4 * u + T4, :, 0:DH],
                                      psT[:, 0, :, :].rearrange("p t (h d) -> p t h d", h=HEADS),
                                      bv[:, :].rearrange("p (h d) -> p h d", h=HEADS).unsqueeze(1).broadcast_to((P, T4, HEADS, DH)),
                                      ALU.add).then_inc(v_ready, 1)
                    for n in range(4):
                        dve.wait_ge(hi_ready, 4 * b + n + 1)
                        if b:
                            dve.wait_ge(mid_ready, 4 * (b - 1) + n + 1)
                        dve.tensor_tensor(rest[:, n, :], whole[:, u, n, :], parts[:, u, n, 0, :], ALU.subtract).then_inc(rest_ready, 1)
                    for n in range(4):
                        dve.wait_ge(mid_ready, 4 * b + n + 1)
                        dve.wait_ge(rest_ready, 4 * b + n + 1)
                        dve.tensor_tensor(parts[:, u, n, 2, :], rest[:, n, :], parts[:, u, n, 1, :], ALU.subtract).then_inc(lo_ready, 1)

            @block.tensor
            def _(pe):
                pe.wait_ge(weights_in, 16 * PREP_LOADS)
                pe.transpose(psT[:, 0, 0, 0:2 * BUCKETS], rel[:, :], c["ident"][0:2 * BUCKETS, 0:2 * BUCKETS]).then_inc(relT_psum, 1)
                pe.wait_ge(relT_ready, 1)
                pe.matmul(psT[:, 1, 0, 0:2 * BUCKETS], wk[:, :], relT[:, :], start=True, stop=True).then_inc(pos_psum, 1)
                pe.wait_ge(shapes_ready, 1)
                for g in range(4):
                    for k in range(4):
                        t = 4 * g + k
                        pe.wait_ge(xn_ready, t + 1)
                        if g >= 2 and k == 0:
                            pe.wait_ge(xT_ready, g - 1)
                        last = pe.transpose(psT[:, g % 2, k, :], xn[:, t, :], c["ident"][:, :])
                    last.then_inc(xT_psum, 1)
                pe.wait_ge(xT_ready, 4)

                def project(b):
                    tokens = xnT[:, T4 * b:T4 * b + T4, :].rearrange("p t q -> p (t q)")
                    if b:
                        pe.wait_ge(qk_ready, 2 * b)
                    pe.matmul(ps_qk[:, 0, :], wq[:, :], tokens, start=True, stop=True)
                    pe.matmul(ps_qk[:, 1, :], wk[:, :], tokens, start=True, stop=True).then_inc(qk_psum, 1)
                    if b:
                        pe.wait_ge(v_ready, b)
                    for t in range(T4):
                        last = pe.matmul(psT[:, 0, t, :], xnT[:, T4 * b + t, :], wv[:, :], start=True, stop=True)
                    last.then_inc(v_psum, 1)

                def far_products(b):
                    for n in range(2):
                        pe.wait_ge(qk_ready, 2 * b + n + 1)
                        if 2 * b + n:
                            pe.wait_ge(far_ready, 2 * b + n)
                        for far in range(2):
                            last = pe.matmul(ps_far[:, far, :], far_w[:, 2 * n + far, :, :].rearrange("p h j -> p (h j)"),
                                             whole[:, b % 2, n, :], start=True, stop=True)
                        last.then_inc(far_psum, 1)

                def row_products(b, ks):
                    for k in ks:
                        side, (h0, n) = k // len(CHUNKS), CHUNKS[k % len(CHUNKS)]
                        m = n_rows * b + k
                        if m >= 2:
                            pe.wait_ge(rows_ready, m - 1)
                        pe.matmul(ps_tab[0:n * NP_, m % 2, :], tab_w[:, side, h0:h0 + n, :].rearrange("p h r -> p (h r)"),
                                  whole[:, b % 2, side, :], start=True, stop=True).then_inc(tab_psum, 1)

                project(0)
                far_products(0)
                for b in range(B):
                    if b + 1 < B:
                        project(b + 1)
                    row_products(b, range(len(CHUNKS) - 2))
                    if b + 1 < B:
                        far_products(b + 1)
                    row_products(b, range(len(CHUNKS) - 2, n_rows))

        clear_semaphores(nc, own_sems)


def relative_attend(nc, name, heads_out, consts, dram, layout):
    with ExitStack() as ctx:
        own_sems = []

        def sb(n, shape, dt=F32):
            return ctx.enter_context(nc.sbuf_tensor(f"{name}_{n}", shape, dt))

        def ps(n, shape, dt=F32):
            return ctx.enter_context(nc.psum_tensor(f"{name}_{n}", shape, dt))

        def sem(n):
            own_sems.append(ctx.enter_context(nc.semaphore(f"{name}_{n}")))
            return own_sems[-1]

        load_rows, lay_out, rows_free, near_out, _ = layout
        K = 8 * ROWS
        UNITS = T4 * GROUP
        PROBS = 4
        PITCH = 6 * P
        ident = consts["ident"]
        qs, ks = sb("qs", [K, 2, GROUP, S], BF16), sb("ks", [K, 2, GROUP, S], BF16)
        v = sb("v", [P, 2, T4, GROUP, 32])
        bias = sb("bias", [P, GROUP, T4 * PITCH])
        neg, neg_top = sb("neg", [P, 4, S]), sb("neg_top", [P, 4])
        prob = sb("prob", [P, PROBS, S])
        probT = sb("probT", [P, 2, GROUP, T4, P])
        headT = sb("headT", [P, 2, P])
        rate = sb("rate", [P, 2, GROUP])

        ps_s = ps("ps_s", [P, 4, S])
        ps_t = ps("ps_t", [P, 2, T4, P])
        ps_c = ps("ps_c", [P, 2, 4, P])

        cleared, units_begun = sem("cleared"), sem("units_begun")
        qk_in = [sem(f"qk_in{k}") for k in range(2)]
        v_in = [sem(f"v_in{k}") for k in range(2)]
        bias_in = [sem(f"bias_in{t}") for t in range(T4)]
        scores_psum, neg_ready, prob_ready, turned_psum = (
            sem("scores_psum"), sem("neg_ready"), sem("prob_ready"), sem("turned_psum"))
        copied = sem("copied_even"), sem("copied_odd")
        weighed, headT_ready, heads_turned, rates_ready, heads_ready = (
            sem("weighed"), sem("headT_ready"), sem("heads_turned"), sem("rates_ready"), sem("heads_ready"))

        def is_first(n):
            return isinstance(n, int) and n == 0

        def turn_of_parity(n, k):
            return n // 2 if isinstance(n, int) else (n - k) // 2

        def behind(n, u, lag):
            if u - lag >= UNITS:
                return None
            if u >= lag:
                return n, u - lag
            return None if is_first(n) else (n - 1, u - lag + UNITS)

        def pairs(engine, body, lag):
            body(0, 0, range(UNITS))
            body(1, 1, range(UNITS))
            with engine.Fori(1, B * GROUPS // 2) as m:
                body(m * 2, 0, range(UNITS))
                body(m * 2 + 1, 1, range(UNITS))
            body(LAST, 1, range(UNITS, UNITS + lag))

        LAST = B * GROUPS - 1

        with nc.Block() as block:

            @block.sync
            def _(sp):
                def load_operands(n, b, g, fresh):
                    k = g % 2
                    head = b * HEADS + g * GROUP
                    if not fresh:
                        sp.wait_ge(scores_psum, n * UNITS - UNITS)
                    for side, dst in (("q", qs), ("k", ks)):
                        src = bass.AP(dram[side].tensor, head * (K * S), [(S, K), (K * S, GROUP), (1, S)])
                        sp.dma_start(dst[:, k, :, :], src).then_inc(qk_in[k], 16)
                    if not fresh:
                        sp.wait_ge(weighed, n * T4 - T4)
                    src = bass.AP(dram["v"].tensor, n * (P * T4 * P), [(T4 * P, P), (1, T4 * P)])
                    sp.dma_start(v[:, k, :, :, :].rearrange("p t j k -> p (t j k)"), src).then_inc(v_in[k], 16)

                def load_near(n, b, g, first):
                    head = b * HEADS + g * GROUP
                    for t in range(T4):
                        if not first:
                            sp.wait_ge(neg_ready, n * UNITS + (GROUP * (t + 1) - UNITS))
                        elif t == 0:
                            sp.wait_ge(cleared, 1)
                        if g == 0 and t == 0:
                            for k in range(2):
                                sp.wait_ge(near_out[k], b * 32 + 32)
                        for s in range(2):
                            src = bass.AP(dram["near"].tensor, head * (NB * 64 * WIN) + (2 * t + s) * (64 * WIN),
                                          [(WIN, 64), (NB * 64 * WIN, GROUP), (1, WIN)])
                            at = t * PITCH + 64 * s
                            sp.dma_start(bias[64 * s:64 * s + 64, :, at:at + WIN], src).then_inc(bias_in[t], 16)

                def batch(b, first):
                    for g in range(GROUPS):
                        n = b * GROUPS + g
                        load_operands(n, b, g, first and g < 2)
                        load_near(n, b, g, first and g == 0)

                sp.wait_ge(rows_free, 1)
                load_rows(sp, 1)
                batch(0, True)
                with sp.Fori(1, B - 1) as b:
                    sp.wait_ge(rows_free, b + 1)
                    load_rows(sp, b + 1)
                    batch(b, False)
                batch(B - 1, False)

            @block.gpsimd
            def _(pool):
                with pool.Fori(1, B) as b:
                    lay_out(pool, b, False)
                for k in range(2):
                    pool.wait_ge(near_out[k], 32 * B)

            @block.scalar
            def _(act):
                def copy_turned(n, u):
                    t, j = u // GROUP, u % GROUP
                    if j % 2 == 0:
                        return
                    act.wait_ge(turned_psum, n * UNITS + (u + 1))
                    nc.scalar.copy(probT[:, t % 2, j, :, :], ps_t[:, u % 2, :, :]).then_inc(copied[1], 1)

                def exp(n, u):
                    act.wait_ge(neg_ready, n * UNITS + (u + 1))
                    nc.scalar.activation(prob[:, u % PROBS, :], neg[:, u % 4, :], ACT.Exp, bias=neg_top[:, u % 4:u % 4 + 1],
                                         scale=-1.0).then_inc(prob_ready, 1)

                def copy_heads(n, t):
                    act.wait_ge(weighed, n * T4 + (t + 1))
                    if not (is_first(n) and t < 2):
                        act.wait_ge(heads_turned, n * T4 + (t - 1))
                    nc.scalar.copy(headT[:, t % 2, :], ps_c[:, t % 2, 0, :]).then_inc(headT_ready, 1)

                def body(n, parity, steps):
                    for u in steps:
                        if at := behind(n, u, COPY_LAG):
                            copy_turned(*at)
                        if at := behind(n, u, 0):
                            exp(*at)
                        if (at := behind(n, u, HEADS_LAG)) and at[1] % GROUP == 0:
                            copy_heads(at[0], at[1] // GROUP)

                pairs(act, body, HEADS_LAG)

            @block.vector
            def _(dve):
                dve.memset(bias[:, :, :], 0.0).then_inc(cleared, 1)
                dve.wait_ge(cleared, 1)

                def copy_turned(n, u):
                    t, j = u // GROUP, u % GROUP
                    if j % 2:
                        return
                    dve.wait_ge(turned_psum, n * UNITS + (u + 1))
                    dve.tensor_copy(probT[:, t % 2, j, :, :], ps_t[:, u % 2, :, :]).then_inc(copied[0], 1)

                def add_terms(n, u):
                    t, j = u // GROUP, u % GROUP
                    dve.wait_ge(scores_psum, n * UNITS + (u + 1))
                    if j == 0:
                        dve.wait_ge(bias_in[t], n * 32 + 32)
                    dve.sem_inc(units_begun, 1)
                    at = t * (PITCH - P) + 64
                    dve.tensor_tensor_reduce(out=neg[:, u % 4, :], in0=ps_s[:, u % 4, :], in1=bias[:, j, at:at + S], scale=-1.0,
                                             scalar=HUGE, op0=ALU.add, op1=ALU.min,
                                             accum_out=neg_top[:, u % 4:u % 4 + 1]).then_inc(neg_ready, 1)

                def by_head(t):
                    return ps_c[:, t % 2, 1, :].rearrange("p (j k) -> p j k", j=GROUP)

                def invert_sums(n, t):
                    dve.wait_ge(heads_turned, n * T4 + (t + 1))
                    dve.reciprocal(rate[:, t % 2, :], by_head(t)[:, :, DH]).then_inc(rates_ready, 1)

                def normalise_heads(n, t):
                    dve.wait_ge(rates_ready, n * T4 + (t + 1))
                    dve.tensor_tensor(heads_out[:, t, bass.ds(n, 1), :].rearrange("p a (j d) -> p (a j) d", j=GROUP),
                                      by_head(t)[:, :, 0:DH], rate[:, t % 2, :].unsqueeze(2).broadcast_to((P, GROUP, DH)),
                                      ALU.mult).then_inc(heads_ready, 1)

                def body(n, parity, steps):
                    for u in steps:
                        if at := behind(n, u, COPY_LAG):
                            copy_turned(*at)
                        if at := behind(n, u, 0):
                            add_terms(*at)
                        if (at := behind(n, u, RATE_LAG)) and at[1] % GROUP == 0:
                            invert_sums(at[0], at[1] // GROUP)
                        if (at := behind(n, u, RATE_LAG + 1)) and at[1] % GROUP == 0:
                            normalise_heads(at[0], at[1] // GROUP)

                pairs(dve, body, RATE_LAG + 1)

            @block.tensor
            def _(pe):
                def score(n, k, u):
                    t, j = u // GROUP, u % GROUP
                    if u == 0:
                        pe.wait_ge(qk_in[k], turn_of_parity(n, k) * 32 + 32)
                    pe.matmul(ps_s[:, u % 4, :], qs[:, k, j, t * P:(t + 1) * P], ks[:, k, j, :], start=True, stop=True)\
                        .then_inc(scores_psum, 1)

                def turn(n, u):
                    pe.wait_ge(prob_ready, n * UNITS + (u + 1))
                    if not (is_first(n) and u < 2):
                        pe.wait_ge(copied[u % 2], n * (UNITS // 2) + u // 2)
                    for i in range(T4):
                        last = pe.transpose(ps_t[:, u % 2, i, :], prob[:, u % PROBS, i * P:(i + 1) * P], ident[:, :])
                    last.then_inc(turned_psum, 1)

                def weigh(n, k, t, i):
                    if i == 0:
                        pe.wait_ge(copied[0], n * (UNITS // 2) + (t + 1) * (GROUP // 2))
                        pe.wait_ge(copied[1], n * (UNITS // 2) + (t + 1) * (GROUP // 2))
                        if t == 0:
                            pe.wait_ge(v_in[k], turn_of_parity(n, k) * 16 + 16)
                        if not (is_first(n) and t < 2):
                            pe.wait_ge(heads_ready, n * T4 + (t - 1))
                    for j in range(GROUP):
                        last = pe.matmul(ps_c[32 * j:32 * j + 32, t % 2, 0, :], v[:, k, i, j, :],
                                         probT[:, t % 2, j, i, :], start=(i == 0), stop=(i == T4 - 1),
                                         tile_position=(0, 32 * j))
                    if i == T4 - 1:
                        last.then_inc(weighed, 1)

                def turn_heads(n, t):
                    pe.wait_ge(headT_ready, n * T4 + (t + 1))
                    pe.transpose(ps_c[:, t % 2, 1, :], headT[:, t % 2, :], ident[:, :]).then_inc(heads_turned, 1)

                def body(n, k, steps):
                    for u in steps:
                        if at := behind(n, u, 0):
                            score(n, k, u)
                        if at := behind(n, u, WEIGH_LAG):
                            weigh(at[0], k if u >= WEIGH_LAG else 1 - k, at[1] // T4, at[1] % T4)
                        if at := behind(n, u, TURN_LAG):
                            turn(*at)
                        if (at := behind(n, u, BACK_LAG)) and at[1] % GROUP == 0:
                            turn_heads(at[0], at[1] // GROUP)

                pairs(pe, body, BACK_LAG)

        clear_semaphores(nc, own_sems)


def relative_finish(nc, name, x, xn, heads, consts, w):
    c = consts
    with ExitStack() as ctx:
        own_sems = []

        def sb(n, shape, dt=F32):
            return ctx.enter_context(nc.sbuf_tensor(f"{name}_{n}", shape, dt))

        def ps(n, shape, dt=F32):
            return ctx.enter_context(nc.psum_tensor(f"{name}_{n}", shape, dt))

        def sem(n):
            own_sems.append(ctx.enter_context(nc.semaphore(f"{name}_{n}")))
            return own_sems[-1]

        wo, bo = sb("wo", [P, D]), sb("bo", [P, D])
        ln_scale, ln_bias = sb("ln_scale", [P, D]), sb("ln_bias", [P, D])
        headsT = sb("headsT", [P, TILES, P])
        y, scaled = sb("y", [P, TILES, D]), sb("scaled", [P, TILES, D])
        xn_shifted, x_shifted = sb("xn_shifted", [P, TILES, D]), sb("x_shifted", [P, TILES, D])
        stats, mv = sb("stats", [P, TILES, 6]), sb("mv", [P, TILES, 2])
        rstd, newton = sb("rstd", [P, TILES]), sb("newton", [P, 5, TILES])
        psT, ps_y = ps("psT", [P, 2, 4, P]), ps("ps_y", [P, 4, 4, P])
        weights_in, chain = sem("weights_in"), sem("chain")
        turned, headsT_ready, y_psum = sem("turned"), sem("headsT_ready"), sem("y_psum")
        var_ready, std_ready = sem("var_ready"), sem("std_ready")
        xn_shifted_ready, x_shifted_ready = sem("xn_shifted_ready"), sem("x_shifted_ready")

        with nc.Block() as block:

            @block.sync
            def _(sp):
                for dst, src in ((wo, w["Wo"]), (bo, w["bo"].unsqueeze(0).partition_broadcast(P)),
                                 (ln_scale, w["ln_scale"].unsqueeze(0).partition_broadcast(P)),
                                 (ln_bias, w["ln_bias"].unsqueeze(0).partition_broadcast(P))):
                    sp.dma_start(dst[:, :], src).then_inc(weights_in, 16)

            @block.gpsimd
            def _(pool):
                pool.wait_ge(weights_in, 64)
                for b in range(B):
                    rows = slice(T4 * b, T4 * b + T4)
                    pool.tensor_tensor(xn_shifted[:, rows, :], xn[:, rows, :], bo[:, :].unsqueeze(1).broadcast_to((P, T4, D)),
                                       ALU.add).then_inc(xn_shifted_ready, 1)
                pool.tensor_tensor(x_shifted[:, :, :], x[:, :, :], ln_bias[:, :].unsqueeze(1).broadcast_to((P, TILES, D)), ALU.add)\
                    .then_inc(x_shifted_ready, 1)

            @block.scalar
            def _(act):
                for b in range(B):
                    act.wait_ge(turned, b + 1)
                    nc.scalar.copy(headsT[:, T4 * b:T4 * b + T4, :], psT[:, b % 2, :, :]).then_inc(headsT_ready, 1)
                act.wait_ge(var_ready, 1)
                nc.scalar.activation(newton[:, 0, :], mv[:, :, 1], ACT.Sqrt, bias=c["eps7"][:, 0:1]).then_inc(std_ready, 1)

            @block.tensor
            def _(pe):
                pe.wait_ge(weights_in, 64)
                for b in range(B):
                    if b >= 2:
                        pe.wait_ge(headsT_ready, b - 1)
                    for t in range(T4):
                        last = pe.transpose(psT[:, b % 2, t, :], heads[:, t, b * GROUPS:(b + 1) * GROUPS, :].rearrange("p g k -> p (g k)"), c["ident"][:, :])
                    last.then_inc(turned, 1)
                for b in range(B):
                    pe.wait_ge(headsT_ready, b + 1)
                    for t in range(T4):
                        last = pe.matmul(ps_y[:, b, t, :], headsT[:, T4 * b + t, :], wo[:, :], start=True, stop=True)
                    last.then_inc(y_psum, 1)

            @block.vector
            def _(dve):
                done = chain_on(dve, chain)
                dve.wait_ge(weights_in, 64)
                for b in range(B):
                    dve.wait_ge(y_psum, b + 1)
                    rows = slice(T4 * b, T4 * b + T4)
                    dve.wait_ge(xn_shifted_ready, b + 1)
                    last = dve.tensor_tensor(y[:, rows, :], ps_y[:, b, :, :], xn_shifted[:, rows, :], ALU.add)
                done(last)
                normalise_tokens(dve, done, y, (stats, mv, rstd, newton), 1e-7, std_ready, var_ready)
                for t in range(TILES):
                    last = dve.tensor_scalar(scaled[:, t, :], y[:, t, :], mv[:, t, 0:1], newton[:, 4, t:t + 1],
                                             ALU.subtract, ALU.mult)
                done(last)
                full = (P, TILES, D)
                done(dve.tensor_tensor(y[:, :, :], scaled[:, :, :], ln_scale[:, :].unsqueeze(1).broadcast_to(full), ALU.mult))
                dve.wait_ge(x_shifted_ready, 1)
                done(dve.tensor_tensor(x[:, :, :], y[:, :, :], x_shifted[:, :, :], ALU.add))

        clear_semaphores(nc, own_sems)


def relative_phase(nc, kept, name, x, consts, w, dram):
    with ExitStack() as ctx:
        xn = ctx.enter_context(nc.sbuf_tensor(f"{name}_xn", [P, TILES, D], F32))
        heads = ctx.enter_context(nc.sbuf_tensor(f"{name}_heads", [P, T4, B * GROUPS, GROUP * DH], F32))
        with ExitStack() as layout_ctx:
            layout = near_layout(nc, kept, layout_ctx, f"{name}n", dram)
            relative_prepare(nc, f"{name}p", x, xn, consts, w, dram, layout)
            relative_attend(nc, f"{name}m", heads, consts, dram, layout)
            clear_semaphores(nc, layout[-1])
        relative_finish(nc, f"{name}f", x, xn, heads, consts, w)


def spline_phase(nc, name, x, consts, w):
    c = consts
    with ExitStack() as ctx:
        own_sems = []

        def sb(n, shape, dt=F32):
            return ctx.enter_context(nc.sbuf_tensor(f"{name}_{n}", shape, dt))

        def ps(n, shape, dt=F32):
            return ctx.enter_context(nc.psum_tensor(f"{name}_{n}", shape, dt))

        def sem(n):
            own_sems.append(ctx.enter_context(nc.semaphore(f"{name}_{n}")))
            return own_sems[-1]

        raw = sb("raw", [SIGS, D])
        above = sb("above", [SIGS, D])
        below = sb("below", [SIGS, D])
        ternary = sb("ternary", [SIGS, D])
        change = sb("change", [SIGS, D])
        sigs = sb("sigs", [SIGS, D])
        score_w = sb("score_w", [P, SCORES])
        cluster_sum = sb("cluster_sum", [P, CLUSTERS])
        cluster_neg = sb("cluster_neg", [P, CLUSTERS])
        cluster_pos = sb("cluster_pos", [P, CLUSTERS])
        table = sb("table", [SIGS, PARAMS])
        cw1, cb1, cw2 = sb("cw1", [P, COMP]), sb("cb1", [COMP, 1]), sb("cw2", [COMP, 2])
        cb2 = sb("cb2", [P, 2])
        knots, temp, divisor = sb("knots", [P, KNOTS]), sb("temp", [P, 1]), sb("divisor", [P, 1])
        rate, neg_rate = sb("rate", [P, 1]), sb("neg_rate", [P, 1])
        gamma, beta, out_scale = sb("gamma", [P, D]), sb("beta", [P, D]), sb("out_scale", [P, 1])
        xn = sb("xn", [P, TILES, D])
        xnT = sb("xnT", [P, TILES, P])
        stats, mv = sb("stats", [P, TILES, 6]), sb("mv", [P, TILES, 2])
        rstd, newton = sb("rstd", [P, TILES]), sb("newton", [P, 5, TILES])
        picks = sb("picks", [P, 2, TILES, 8])
        e = sb("e", [P, 2, TILES, 8])
        at = sb("at", [P, TILES * 8])
        reach = sb("reach", [P, TILES * 8, KNOTS - 2])
        low, frac = sb("low", [P, TILES * 8]), sb("frac", [P, TILES * 8])
        seg = sb("seg", [P, TILES * 8, KNOTS - 1])
        picked = sb("picked", [P, TILES * 8, KNOTS - 1])
        v_low, v_high = sb("v_low", [P, TILES * 8]), sb("v_high", [P, TILES * 8])
        rise = sb("rise", [P, TILES * 8])
        gates = sb("gates", [P, TILES, 8])
        best, marks, first = sb("best", [P, TILES]), sb("marks", [P, TILES, 8]), sb("first", [P, TILES])
        chosen = sb("chosen", [P, 2, TILES, 8])
        masked = sb("masked", [P, TILES, CLUSTERS, PER])
        tile_hot = sb("tile_hot", [P, TILES, SIGS])
        tile_hotT = sb("tile_hotT", [SIGS, TILES, P])
        hT = sb("hT", [COMP, TILES, P])
        comp_in, comp = sb("comp_in", [P, TILES, 2]), sb("comp", [P, TILES, 2])
        par = sb("par", [P, TILES, PARAMS])
        term0, term1 = sb("term0", [P, TILES, GRID]), sb("term1", [P, TILES, GRID])
        mag = sb("mag", [P, TILES])
        y, scaled = sb("y", [P, TILES, D]), sb("scaled", [P, TILES, D])
        half_gamma, half_beta, mag_scaled = sb("half_gamma", [P, D]), sb("half_beta", [P, D]), sb("mag_scaled", [P, TILES])
        x_shifted = sb("x_shifted", [P, TILES, D])

        banks = ps("banks", [P, 8, 512])
        psT = banks[:, 0:2, :].rearrange("p b (k q) -> p b k q", k=4)
        ps_scores = banks[:, 2:6, 0:4 * SCORES].rearrange("p b (k s) -> p b k s", k=4)
        ps_h = banks[:, 6:8, :]
        ps_comp = banks[:, 0, 0:2 * TILES].rearrange("p (t o) -> p t o", o=2)
        ps_sigs = banks[:, 5, 0:SIGS]
        ps_par = banks[:, 2:8, 0:2 * PARAMS].rearrange("p b (k n) -> p b k n", k=2)

        weights_in, sigs_ready, sigsT_psum = sem("weights_in"), sem("sigs_ready"), sem("sigsT_psum")
        score_w_ready = sem("score_w_ready")
        chain = sem("chain")
        var_ready, std_ready = sem("var_ready"), sem("std_ready")
        xn_ready, xnT_psum, xnT_ready = sem("xn_ready"), sem("xnT_psum"), sem("xnT_ready")
        picks_ready = sem("picks_ready")
        scores_ready, e_ready = sem("scores_ready"), sem("e_ready")
        h_psum, h_ready, comp_psum = sem("h_psum"), sem("h_ready"), sem("comp_psum")
        comp_in_ready, comp_ready = sem("comp_in_ready"), sem("comp_ready")
        hot_ready, hotT_psum, hotT_ready = sem("hot_ready"), sem("hotT_psum"), sem("hotT_ready")
        par_psum, par_ready = sem("par_psum"), sem("par_ready")
        var2_ready, std2_ready = sem("var2_ready"), sem("std2_ready")
        half_ready, x_shifted_ready = sem("half_ready"), sem("x_shifted_ready")

        with nc.Block() as block:

            @block.sync
            def _(sp):
                loads = [
                    (raw[:, :], w["signatures_raw"]),
                    (cw1[:, :], w["compress_w1"]),
                    (cb1[:, :], w["compress_b1"].unsqueeze(1)),
                    (cw2[:, :], w["compress_w2"]),
                    (cb2[:, :], w["compress_b2"].unsqueeze(0).partition_broadcast(P)),
                    (knots[:, :], w["knot_values"].unsqueeze(0).partition_broadcast(P)),
                    (temp[:, :], w["temperature"].unsqueeze(0).partition_broadcast(P)),
                    (gamma[:, :], w["norm_gamma"].unsqueeze(0).partition_broadcast(P)),
                    (beta[:, :], w["norm_beta"].unsqueeze(0).partition_broadcast(P)),
                    (out_scale[:, :], w["output_scale"].unsqueeze(0).partition_broadcast(P)),
                    (table[:, W1_AT:B1_AT], w["spline_w1"].rearrange("s i g -> s (i g)")),
                    (table[:, B1_AT:W2_AT], w["spline_b1"]),
                    (table[:, W2_AT:B2_AT], w["spline_w2"].rearrange("s g o -> s (g o)")),
                    (table[:, B2_AT:DIR_AT], w["spline_b2"]),
                    (table[:, DIR_AT:PARAMS], w["directions"]),
                ]
                assert len(loads) == SPLINE_LOADS
                for dst, src in loads:
                    sp.dma_start(dst, src).then_inc(weights_in, 16)

            @block.gpsimd
            def _(pool):
                pool.wait_ge(half_ready, 1)
                pool.tensor_tensor(x_shifted[:, :, :], x[:, :, :], half_beta[:, :].unsqueeze(1).broadcast_to((P, TILES, D)), ALU.add)\
                    .then_inc(x_shifted_ready, 1)

            @block.scalar
            def _(act):
                act.wait_ge(var_ready, 1)
                nc.scalar.activation(newton[:, 0, :], mv[:, :, 1], ACT.Sqrt, bias=c["eps5"][:, 0:1]).then_inc(std_ready, 1)
                for g in range(4):
                    act.wait_ge(xnT_psum, g + 1)
                    nc.scalar.copy(xnT[:, 4 * g:4 * g + 4, :], psT[:, g % 2, :, :]).then_inc(xnT_ready, 1)
                for n in range(2):
                    act.wait_ge(picks_ready, n + 1)
                    nc.scalar.activation(e[:, n, :, :], picks[:, n, :, :], ACT.Exp, scale=neg_rate[:, 0:1]).then_inc(e_ready, 1)
                act.wait_ge(weights_in, 16 * SPLINE_LOADS)
                for g in range(4):
                    act.wait_ge(h_psum, g + 1)
                    nc.scalar.activation(hT[:, 4 * g:4 * g + 4, :].rearrange("p k q -> p (k q)"), ps_h[0:COMP, g % 2, :],
                                         ACT.Gelu, bias=cb1[:, 0:1]).then_inc(h_ready, 1)
                act.wait_ge(comp_in_ready, 1)
                nc.scalar.activation(comp[:, :, :], comp_in[:, :, :], ACT.Tanh).then_inc(comp_ready, 1)
                for g in range(8):
                    act.wait_ge(par_psum, g + 1)
                    nc.scalar.copy(par[:, 2 * g:2 * g + 2, :], ps_par[:, g % 6, :, :]).then_inc(par_ready, 1)
                act.wait_ge(var2_ready, 1)
                nc.scalar.activation(newton[:, 0, :], mv[:, :, 1], ACT.Sqrt, bias=c["eps5"][:, 0:1]).then_inc(std2_ready, 1)

            @block.vector
            def _(dve):
                done = chain_on(dve, chain)
                normalise_tokens(dve, done, x, (stats, mv, rstd, newton), 1e-5, std_ready, var_ready)
                for t in range(TILES):
                    dve.tensor_scalar(xn[:, t, :], x[:, t, :], mv[:, t, 0:1], newton[:, 4, t:t + 1],
                                      ALU.subtract, ALU.mult).then_inc(xn_ready, 1)
                dve.wait_ge(weights_in, 16 * SPLINE_LOADS)
                done(dve.tensor_scalar(above[:, :], raw[:, :], 0.3, None, ALU.is_gt))
                done(dve.tensor_scalar(below[:, :], raw[:, :], -0.3, -1.0, ALU.is_lt, ALU.mult))
                done(dve.tensor_tensor(ternary[:, :], above[:, :], below[:, :], ALU.add))
                done(dve.tensor_tensor(change[:, :], ternary[:, :], raw[:, :], ALU.subtract))
                dve.tensor_tensor(sigs[:, :], raw[:, :], change[:, :], ALU.add).then_inc(sigs_ready, 1)
                done(dve.tensor_scalar(divisor[:, :], temp[:, :], 1e-6, None, ALU.add))
                done(dve.reciprocal(rate[:, :], divisor[:, :]))
                done(dve.tensor_scalar(neg_rate[:, :], rate[:, :], -1.0, None, ALU.mult))
                dve.wait_ge(sigsT_psum, 1)
                done(dve.tensor_copy(score_w[:, CLUSTERS:], ps_sigs))
                done(dve.tensor_reduce(cluster_sum[:, :], score_w[:, CLUSTERS:].rearrange("p (c j) -> p c j", c=CLUSTERS),
                                       AX.X, ALU.add))
                done(dve.tensor_scalar(cluster_pos[:, :], cluster_sum[:, :], 0.0, None, ALU.is_gt))
                done(dve.tensor_scalar(cluster_neg[:, :], cluster_sum[:, :], 0.0, None, ALU.is_lt))
                dve.tensor_tensor(score_w[:, 0:CLUSTERS], cluster_pos[:, :], cluster_neg[:, :], ALU.subtract)\
                    .then_inc(score_w_ready, 1)

                def calibrate(n):
                    flat = (P, TILES * 8)
                    ev = e[:, n, :, :].rearrange("p t k -> p (t k)")
                    done(dve.tensor_scalar(at[:, :], ev, 1.0, None, ALU.add))
                    done(dve.reciprocal(low[:, :], at[:, :]))
                    done(dve.tensor_scalar(at[:, :], low[:, :], float(KNOTS - 1), None, ALU.mult))
                    done(dve.tensor_tensor(reach[:, :, :], at[:, :].unsqueeze(2).broadcast_to((*flat, KNOTS - 2)),
                                           c["segment_ids"][:, 1:KNOTS - 1].unsqueeze(1).broadcast_to((*flat, KNOTS - 2)),
                                           ALU.is_ge))
                    done(dve.tensor_reduce(low[:, :], reach[:, :, :], AX.X, ALU.add))
                    done(dve.tensor_tensor(frac[:, :], at[:, :], low[:, :], ALU.subtract))
                    done(dve.tensor_tensor(seg[:, :, :], low[:, :].unsqueeze(2).broadcast_to((*flat, KNOTS - 1)),
                                           c["segment_ids"][:, 0:KNOTS - 1].unsqueeze(1).broadcast_to((*flat, KNOTS - 1)),
                                           ALU.is_equal))
                    for value, k in ((v_low, 0), (v_high, 1)):
                        done(dve.tensor_tensor(picked[:, :, :], seg[:, :, :],
                                               knots[:, k:k + KNOTS - 1].unsqueeze(1).broadcast_to((*flat, KNOTS - 1)),
                                               ALU.mult))
                        done(dve.tensor_reduce(value[:, :], picked[:, :, :], AX.X, ALU.add))
                    done(dve.tensor_tensor(rise[:, :], v_high[:, :], v_low[:, :], ALU.subtract))
                    done(dve.tensor_tensor(rise[:, :], frac[:, :], rise[:, :], ALU.mult))
                    done(dve.tensor_tensor(gates[:, :, :].rearrange("p t k -> p (t k)"), v_low[:, :], rise[:, :], ALU.add))

                def choose(n):
                    wide = (P, TILES, 8)
                    rev = c["countdown8"][:, :].unsqueeze(1).broadcast_to(wide)
                    done(dve.tensor_reduce(best[:, :], gates[:, :, :], AX.X, ALU.max))
                    done(dve.tensor_tensor(marks[:, :, :], gates[:, :, :], best[:, :].unsqueeze(2).broadcast_to(wide),
                                           ALU.is_equal))
                    done(dve.tensor_tensor(marks[:, :, :], marks[:, :, :], rev, ALU.mult))
                    done(dve.tensor_reduce(first[:, :], marks[:, :, :], AX.X, ALU.max))
                    done(dve.tensor_tensor(chosen[:, n, :, :], rev, first[:, :].unsqueeze(2).broadcast_to(wide),
                                           ALU.is_equal))

                dve.tensor_scalar(half_gamma[:, :], gamma[:, :], 0.5, None, ALU.mult)
                dve.tensor_scalar(half_beta[:, :], beta[:, :], 0.5, None, ALU.mult).then_inc(half_ready, 1)
                dve.wait_ge(scores_ready, 4)
                for g in range(4):
                    last = dve.tensor_copy(picks[:, 0, 4 * g:4 * g + 4, :], ps_scores[:, g, :, 0:CLUSTERS])
                last.then_inc(picks_ready, 1)
                dve.wait_ge(e_ready, 1)
                calibrate(0)
                choose(0)
                for g in range(4):
                    for k in range(4):
                        t = 4 * g + k
                        last = dve.tensor_tensor(masked[:, t, :, :],
                                                 ps_scores[:, g, k, CLUSTERS:].rearrange("p (c j) -> p c j", c=CLUSTERS),
                                                 chosen[:, 0, t, :].unsqueeze(2).broadcast_to((P, CLUSTERS, PER)), ALU.mult)
                done(last)
                dve.tensor_reduce(picks[:, 1, :, :], masked[:, :, :, :].rearrange("p t c j -> p t j c"), AX.X, ALU.add)\
                    .then_inc(picks_ready, 1)
                dve.wait_ge(e_ready, 2)
                calibrate(1)
                choose(1)
                for half in range(2):
                    ts = slice(8 * half, 8 * half + 8)
                    dve.tensor_tensor(tile_hot[:, ts, :].rearrange("p t (c j) -> p t c j", c=CLUSTERS),
                                      chosen[:, 0, ts, :].unsqueeze(3).broadcast_to((P, 8, CLUSTERS, PER)),
                                      chosen[:, 1, ts, :].unsqueeze(2).broadcast_to((P, 8, CLUSTERS, PER)),
                                      ALU.mult).then_inc(hot_ready, 1)
                for g in range(4):
                    dve.wait_ge(hotT_psum, g + 1)
                    dve.tensor_copy(tile_hotT[:, 4 * g:4 * g + 4, :], psT[0:SIGS, g % 2, :, :]).then_inc(hotT_ready, 1)
                dve.wait_ge(comp_psum, 1)
                dve.tensor_tensor(comp_in[:, :, :], ps_comp, cb2[:, :].unsqueeze(1).broadcast_to((P, TILES, 2)), ALU.add)\
                    .then_inc(comp_in_ready, 1)
                dve.wait_ge(comp_ready, 1)
                dve.wait_ge(par_ready, 8)
                grid = (P, TILES, GRID)
                done(dve.tensor_tensor(term0[:, :, :], par[:, :, 0:GRID], comp[:, :, 0:1].broadcast_to(grid), ALU.mult))
                done(dve.tensor_tensor(term1[:, :, :], par[:, :, GRID:B1_AT], comp[:, :, 1:2].broadcast_to(grid), ALU.mult))
                done(dve.tensor_tensor(term0[:, :, :], term0[:, :, :], term1[:, :, :], ALU.add))
                done(dve.tensor_tensor(term0[:, :, :], term0[:, :, :], par[:, :, B1_AT:W2_AT], ALU.add))
                done(dve.scalar_tensor_tensor(term1[:, :, :], term0[:, :, :], 0.0, par[:, :, W2_AT:B2_AT], ALU.max, ALU.mult))
                done(dve.tensor_reduce(mag[:, :], term1[:, :, :], AX.X, ALU.add))
                done(dve.tensor_tensor(mag[:, :].unsqueeze(2), mag[:, :].unsqueeze(2), par[:, :, B2_AT:DIR_AT], ALU.add))
                done(dve.tensor_scalar(mag_scaled[:, :], mag[:, :], out_scale[:, 0:1], None, ALU.mult))
                for t in range(TILES):
                    last = dve.scalar_tensor_tensor(y[:, t, :], par[:, t, DIR_AT:], mag_scaled[:, t:t + 1], xn[:, t, :],
                                                    ALU.mult, ALU.add)
                done(last)
                normalise_tokens(dve, done, y, (stats, mv, rstd, newton), 1e-5, std2_ready, var2_ready)
                for t in range(TILES):
                    last = dve.tensor_scalar(scaled[:, t, :], y[:, t, :], mv[:, t, 0:1], newton[:, 4, t:t + 1],
                                             ALU.subtract, ALU.mult)
                done(last)
                full = (P, TILES, D)
                dve.wait_ge(half_ready, 1)
                done(dve.tensor_tensor(y[:, :, :], scaled[:, :, :], half_gamma[:, :].unsqueeze(1).broadcast_to(full), ALU.mult))
                dve.wait_ge(x_shifted_ready, 1)
                done(dve.tensor_tensor(x[:, :, :], y[:, :, :], x_shifted[:, :, :], ALU.add))

            @block.tensor
            def _(pe):
                for g in range(4):
                    for k in range(4):
                        t = 4 * g + k
                        pe.wait_ge(xn_ready, t + 1)
                        if g >= 2 and k == 0:
                            pe.wait_ge(xnT_ready, g - 1)
                        last = pe.transpose(psT[:, g % 2, k, :], xn[:, t, :], c["ident"][:, :])
                    last.then_inc(xnT_psum, 1)
                pe.wait_ge(sigs_ready, 1)
                pe.transpose(ps_sigs, sigs[:, :], c["ident"][0:SIGS, 0:SIGS]).then_inc(sigsT_psum, 1)
                pe.wait_ge(score_w_ready, 1)
                for g in range(4):
                    pe.wait_ge(xnT_ready, g + 1)
                    for k in range(4):
                        last = pe.matmul(ps_scores[:, g, k, :], xnT[:, 4 * g + k, :], score_w[:, :], start=True, stop=True)
                    last.then_inc(scores_ready, 1)
                for g in range(4):
                    if g >= 2:
                        pe.wait_ge(h_ready, g - 1)
                    pe.matmul(ps_h[0:COMP, g % 2, :], cw1[:, :], xnT[:, 4 * g:4 * g + 4, :].rearrange("p k q -> p (k q)"),
                              start=True, stop=True).then_inc(h_psum, 1)
                for g in range(4):
                    for k in range(4):
                        t = 4 * g + k
                        if k == 0:
                            pe.wait_ge(hot_ready, t // 8 + 1)
                            if g >= 2:
                                pe.wait_ge(hotT_ready, g - 1)
                        last = pe.transpose(psT[0:SIGS, g % 2, k, :], tile_hot[:, t, :], c["ident"][:, :])
                    last.then_inc(hotT_psum, 1)
                pe.wait_ge(h_ready, 4)
                pe.wait_ge(hotT_ready, 3)
                for t in range(TILES):
                    last = pe.matmul(ps_comp[:, t, :], hT[:, t, :], cw2[:, :], start=True, stop=True)
                last.then_inc(comp_psum, 1)
                for g in range(8):
                    pe.wait_ge(hotT_ready, g // 2 + 1)
                    if g >= 6:
                        pe.wait_ge(par_ready, g - 5)
                    for k in range(2):
                        last = pe.matmul(ps_par[:, g % 6, k, :], tile_hotT[:, 2 * g + k, :], table[:, :], start=True, stop=True)
                    last.then_inc(par_psum, 1)

        clear_semaphores(nc, own_sems)


def causal_phase(nc, name, x, consts, w):
    c = consts
    scale = float(D) ** -0.5
    with ExitStack() as ctx:
        own_sems = []

        def sb(n, shape, dt=F32):
            return ctx.enter_context(nc.sbuf_tensor(f"{name}_{n}", shape, dt))

        def ps(n, shape, dt=F32):
            return ctx.enter_context(nc.psum_tensor(f"{name}_{n}", shape, dt))

        def sem(n):
            own_sems.append(ctx.enter_context(nc.semaphore(f"{name}_{n}")))
            return own_sems[-1]

        T = S // P
        w_kqv, b_kqv = sb("w_kqv", [P, 3, D]), sb("b_kqv", [P, 3, D])
        w_p, b_p = sb("w_p", [P, D]), sb("b_p", [P, D])
        cos, sin = sb("cos", [P, T, D // 2]), sb("sin", [P, T, D // 2])
        xn = sb("xn", [P, TILES, D])
        xnT = sb("xnT", [P, TILES, P])
        stats, mv = sb("stats", [P, TILES, 6]), sb("mv", [P, TILES, 2])
        rstd, newton = sb("rstd", [P, TILES]), sb("newton", [P, 5, TILES])
        kqv = sb("kqv", [P, TILES, 3, D])
        half_a, half_b = sb("half_a", [P, 2, T, 2, D // 2]), sb("half_b", [P, 2, T, 2, D // 2])
        half_c, half_d = sb("half_c", [P, 2, T, 2, D // 2]), sb("half_d", [P, 2, T, 2, D // 2])
        turned = sb("turned", [P, TILES, 2, D])
        kT, qT = sb("kT", [P, TILES, P]), sb("qT", [P, TILES, P])
        size = sb("size", [P, 2, S])
        tail = sb("tail", [P, 2, S])
        soft = sb("soft", [P, 2, S])
        over = sb("over", [P, 2, S])
        weiT = sb("weiT", [P, T, S])
        outT = sb("outT", [P, 2, S])

        ps_kqv = ps("ps_kqv", [P, 2, 512])
        psT = ps("psT", [P, 2, 4, P])
        ps_wei = ps("ps_wei", [P, 2, S])
        ps_out = ps("ps_out", [P, S])
        ps_y = ps("ps_y", [P, T, D])

        weights_in, chain = sem("weights_in"), sem("chain")
        var_ready, std_ready = sem("var_ready"), sem("std_ready")
        xn_ready, xT_psum, xT_ready = sem("xn_ready"), sem("xT_psum"), sem("xT_ready")
        kqv_psum, kqv_ready = sem("kqv_psum"), sem("kqv_ready")
        parts_ready, turned_ready = sem("parts_ready"), sem("turned_ready")
        kq_psum, kq_ready = sem("kq_psum"), sem("kq_ready")
        wei_psum, size_ready, tail_ready, soft_ready = sem("wei_psum"), sem("size_ready"), sem("tail_ready"), sem("soft_ready")
        over_ready, wei_ready, wei_masked = sem("over_ready"), sem("wei_ready"), sem("wei_masked")
        out_psum, out_ready, y_psum, y_added = sem("out_psum"), sem("out_ready"), sem("y_psum"), sem("y_added")

        with nc.Block() as block:

            @block.sync
            def _(sp):
                loads = [(w_kqv[:, n, :], w[k]) for n, k in enumerate(("Wk", "Wq", "Wv"))]
                loads += [(b_kqv[:, n, :], w[k].unsqueeze(0).partition_broadcast(P)) for n, k in enumerate(("bk", "bq", "bv"))]
                loads += [(w_p[:, :], w["Wp"]), (b_p[:, :], w["bp"].unsqueeze(0).partition_broadcast(P)),
                          (cos[:, :, :], w["cos"].rearrange("(t p) f -> p t f", p=P)),
                          (sin[:, :, :], w["sin"].rearrange("(t p) f -> p t f", p=P))]
                assert len(loads) == CAUSAL_LOADS
                for dst, src in loads:
                    sp.dma_start(dst, src).then_inc(weights_in, 16)

            @block.scalar
            def _(act):
                act.wait_ge(var_ready, 1)
                nc.scalar.activation(newton[:, 0, :], mv[:, :, 1], ACT.Sqrt, bias=c["eps5"][:, 0:1]).then_inc(std_ready, 1)
                for g in range(4):
                    act.wait_ge(xT_psum, g + 1)
                    nc.scalar.copy(xnT[:, 4 * g:4 * g + 4, :], psT[:, g % 2, :, :]).then_inc(xT_ready, 1)
                for b in range(B):
                    for n, dst in enumerate((kT, qT)):
                        act.wait_ge(kq_psum, 2 * b + n + 1)
                        nc.scalar.copy(dst[:, T * b:T * b + T, :], psT[:, n, :, :]).then_inc(kq_ready, 1)
                nc.scalar.preload_act_table_set("natural_log_exp_and_others")
                for b in range(B):
                    for j in range(T):
                        k, u = T * b + j, j % 2
                        cols = slice(P * j, S)
                        act.wait_ge(wei_psum, k + 1)
                        if k >= 2:
                            act.wait_ge(wei_ready, k - 1)
                        nc.scalar.activation(size[:, u, cols], ps_wei[:, u, cols], ACT.Abs, scale=scale).then_inc(size_ready, 1)
                        act.wait_ge(size_ready, k + 1)
                        nc.scalar.activation(tail[:, u, cols], size[:, u, cols], ACT.Exp, scale=-1.0).then_inc(tail_ready, 1)
                        act.wait_ge(tail_ready, k + 1)
                        nc.scalar.activation(soft[:, u, cols], tail[:, u, cols], ACT.Ln, bias=1.0).then_inc(soft_ready, 1)
                    act.wait_ge(out_psum, b + 1)
                    if b >= 2:
                        act.wait_ge(y_psum, b - 1)
                    nc.scalar.copy(outT[:, b % 2, :], ps_out[:, :]).then_inc(out_ready, 1)

            @block.gpsimd
            def _(pool):
                for b in range(B):
                    pool.wait_ge(kqv_ready, T * b + T)
                    if b >= 2:
                        pool.wait_ge(turned_ready, b - 1)
                    pair = kqv[:, T * b:T * b + T, 0:2, :].rearrange("p t n (f two) -> p t n f two", two=2)
                    wide = (P, T, 2, D // 2)
                    cs, sn = cos[:, :, :].unsqueeze(2).broadcast_to(wide), sin[:, :, :].unsqueeze(2).broadcast_to(wide)
                    pool.tensor_tensor(half_c[:, b % 2, :, :, :], pair[:, :, :, :, 0], sn, ALU.mult)
                    pool.tensor_tensor(half_d[:, b % 2, :, :, :], pair[:, :, :, :, 1], cs, ALU.mult).then_inc(parts_ready, 1)
                for b in range(B):
                    for j in range(T):
                        pool.wait_ge(wei_ready, T * b + j + 1)
                        block_ = weiT[:, j, P * j:P * j + P]
                        pool.affine_select(block_, block_, compare_op=ALU.is_ge, fill=0.0, base=0,
                                           pattern=[[1, P]], channel_multiplier=-1).then_inc(wei_masked, 1)

            @block.vector
            def _(dve):
                done = chain_on(dve, chain)

                def add_y(b):
                    dve.wait_ge(y_psum, b + 1)
                    xb = x[:, T * b:T * b + T, :]
                    dve.tensor_tensor(xb, ps_y[:, :, :], xb, ALU.add).then_inc(y_added, 1)
                    dve.wait_ge(y_added, b + 1)
                    done(dve.tensor_tensor(xb, xb, b_p[:, :].unsqueeze(1).broadcast_to((P, T, D)), ALU.add))

                normalise_tokens(dve, done, x, (stats, mv, rstd, newton), 1e-5, std_ready, var_ready)
                for t in range(TILES):
                    dve.tensor_scalar(xn[:, t, :], x[:, t, :], mv[:, t, 0:1], newton[:, 4, t:t + 1],
                                      ALU.subtract, ALU.mult).then_inc(xn_ready, 1)
                dve.wait_ge(weights_in, 16 * CAUSAL_LOADS)
                for b in range(B):
                    for t in range(T * b, T * b + T):
                        dve.wait_ge(kqv_psum, t + 1)
                        dve.tensor_tensor(kqv[:, t, :, :], ps_kqv[:, t % 2, 0:3 * D].rearrange("p (n d) -> p n d", n=3),
                                          b_kqv[:, :, :], ALU.add).then_inc(kqv_ready, 1)
                    dve.wait_ge(kqv_ready, T * b + T)
                    pair = kqv[:, T * b:T * b + T, 0:2, :].rearrange("p t n (f two) -> p t n f two", two=2)
                    out = turned[:, T * b:T * b + T, :, :].rearrange("p t n (f two) -> p t n f two", two=2)
                    wide = (P, T, 2, D // 2)
                    cs, sn = cos[:, :, :].unsqueeze(2).broadcast_to(wide), sin[:, :, :].unsqueeze(2).broadcast_to(wide)
                    dve.tensor_tensor(half_a[:, b % 2, :, :, :], pair[:, :, :, :, 0], cs, ALU.mult)
                    done(dve.tensor_tensor(half_b[:, b % 2, :, :, :], pair[:, :, :, :, 1], sn, ALU.mult))
                    dve.tensor_tensor(out[:, :, :, :, 0], half_a[:, b % 2, :, :, :], half_b[:, b % 2, :, :, :], ALU.add)
                    dve.wait_ge(parts_ready, b + 1)
                    dve.tensor_tensor(out[:, :, :, :, 1], half_d[:, b % 2, :, :, :], half_c[:, b % 2, :, :, :], ALU.subtract)\
                        .then_inc(turned_ready, 1)
                for b in range(B):
                    for j in range(T):
                        k, u = T * b + j, j % 2
                        cols = slice(P * j, S)
                        dve.wait_ge(size_ready, k + 1)
                        dve.tensor_scalar(over[:, u, cols], ps_wei[:, u, cols], scale, 0.0, ALU.mult, ALU.max).then_inc(over_ready, 1)
                        dve.wait_ge(over_ready, k + 1)
                        dve.wait_ge(soft_ready, k + 1)
                        if b:
                            dve.wait_ge(out_psum, b)
                        dve.tensor_tensor(weiT[:, j, cols], over[:, u, cols], soft[:, u, cols], ALU.add).then_inc(wei_ready, 1)
                    if b:
                        add_y(b - 1)
                add_y(B - 1)

            @block.tensor
            def _(pe):
                for g in range(4):
                    for k in range(4):
                        t = 4 * g + k
                        pe.wait_ge(xn_ready, t + 1)
                        if g >= 2 and k == 0:
                            pe.wait_ge(xT_ready, g - 1)
                        last = pe.transpose(psT[:, g % 2, k, :], xn[:, t, :], c["ident"][:, :])
                    last.then_inc(xT_psum, 1)
                pe.wait_ge(weights_in, 16 * CAUSAL_LOADS)

                def turn(b):
                    pe.wait_ge(turned_ready, b + 1)
                    for n in range(2):
                        pe.wait_ge(*((xT_ready, 4) if b == 0 else (kq_ready, 2 * b - 1 + n)))
                        for k in range(T):
                            last = pe.transpose(psT[:, n, k, :], turned[:, T * b + k, n, :], c["ident"][:, :])
                        last.then_inc(kq_psum, 1)

                for t in range(TILES):
                    pe.wait_ge(xT_ready, t // 4 + 1)
                    if t >= 2:
                        pe.wait_ge(kqv_ready, t - 1)
                    pe.matmul(ps_kqv[:, t % 2, 0:3 * D], xnT[:, t, :], w_kqv[:, :, :].rearrange("p n d -> p (n d)"),
                              start=True, stop=True).then_inc(kqv_psum, 1)
                    if t % T == T - 1 and t // T:
                        turn(t // T - 1)
                turn(B - 1)

                def project(b):
                    pe.wait_ge(out_ready, b + 1)
                    if b:
                        pe.wait_ge(y_added, b)
                    for k in range(T):
                        last = pe.matmul(ps_y[:, k, :], outT[:, b % 2, k * P:(k + 1) * P], w_p[:, :], start=True, stop=True)
                    last.then_inc(y_psum, 1)

                for b in range(B):
                    for j in range(T):
                        k = T * b + j
                        pe.wait_ge(kq_ready, 2 * b + 2)
                        if k >= 2:
                            pe.wait_ge(over_ready, k - 1)
                        pe.matmul(ps_wei[:, j % 2, P * j:S], qT[:, k, :],
                                  kT[:, k:T * b + T, :].rearrange("p t q -> p (t q)"), start=True, stop=True).then_inc(wei_psum, 1)
                    if b:
                        project(b - 1)
                    for j in range(T):
                        pe.wait_ge(wei_masked, T * b + j + 1)
                        if b and j == 0:
                            pe.wait_ge(out_ready, b)
                        last = pe.matmul(ps_out[:, P * j:S], kqv[:, T * b + j, 2, :], weiT[:, j, P * j:S],
                                         start=(j == 0), stop=(j == T - 1), skip_group_check=True)
                    last.then_inc(out_psum, 1)
                project(B - 1)

        clear_semaphores(nc, own_sems)


def network(nc, inputs, out, tables):
    def weights(prefix, *more):
        names = {n[len(prefix):]: a for n, a in inputs.items() if n.startswith(prefix)}
        return {**names, **{n: tables[n] for n in more}}

    sorted_tokens = nc.dram_tensor("sorted_tokens", (SLOTS * P, D), F32).ap()
    sorted_results = nc.dram_tensor("sorted_results", (SLOTS * P, D), F32).ap()
    with ExitStack() as ctx:
        x = ctx.enter_context(nc.sbuf_tensor("x_tokens", [P, TILES, D], F32))
        c = constants_phase(nc, ctx, x, inputs["L0_attn_hidden_states"], sorted_tokens)
        ffn_phase(nc, ctx, "l0f0", x, c, weights("L0_ffn_"), (sorted_tokens, sorted_results))
        relative_phase(nc, ctx, "l0a", x, c, weights("L0_attn_", "own_head", "far_mask", "block_hot"), attention_dram(nc))
        ffn_phase(nc, ctx, "l0f1", x, c, weights("L0_ffn_"), (sorted_tokens, sorted_results))
        spline_phase(nc, "l1f0", x, c, weights("L1_ffn_"))
        causal_phase(nc, "l1a", x, c, weights("L1_attn_", "cos", "sin"))
        spline_phase(nc, "l1f1", x, c, weights("L1_ffn_"))
        x_out = ctx.enter_context(nc.semaphore("x_out"))
        with nc.Block() as block:

            @block.sync
            def _(sp):
                sp.dma_start(out.rearrange("b (t p) d -> p (b t) d", p=P), x[:, :, :]).then_inc(x_out, 16)
                sp.wait_ge(x_out, 16)


def kernel(**inputs):
    import concourse.bacc as _bacc
    from concourse.bass_utils import run_bass_kernel_spmd as _run

    nc = _bacc.Bacc("TRN2", target_bir_lowering=False, num_devices=1)
    arrays, handles = {}, {}
    for name, a in {**inputs, **host_tables()}.items():
        if name == "L0_attn_attention_mask":
            continue
        arrays[f"in_{name}"] = np.ascontiguousarray(a)
        handles[name] = nc.dram_tensor(f"in_{name}", a.shape, F32, kind="ExternalInput").ap()
    out = nc.dram_tensor("out", (B, S, D), F32, kind="ExternalOutput").ap()
    tables = {name: handles.pop(name) for name in host_tables()}
    network(nc, handles, out, tables)
    r = _run(nc, [arrays], core_ids=[0])
    return r.results[0]["out"]
```
